# Optimizing a Trainium2 kernel written in Bass

```python
import numpy as np
import jax
import jax.numpy as jnp

def _softmax(x, axis=-1):
    return jax.nn.softmax(x, axis=axis)

def _gelu(x):
    return jax.nn.gelu(x, approximate=True)

def _silu(x):
    return jax.nn.silu(x)

def _sigmoid(x):
    return jax.nn.sigmoid(x)

def _layernorm(x, axis=-1, eps=1e-05):
    m = jnp.mean(x, axis=axis, keepdims=True)
    v = jnp.var(x, axis=axis, keepdims=True)
    return (x - m) / jnp.sqrt(v + eps)

def _scatter_add(tgt, idx, src, axis=0):
    return tgt.at[idx].add(src)

def _segment_sum(src, seg, n):
    return jax.ops.segment_sum(src, seg, n)
kernel_name = 'mk_gnn_preln_d2_gnn_r8_046941'

def setup_inputs(seed: int=0):
    np.random.seed(seed)
    _w = jnp.asarray

    def _rec_inputs():
        import jax
        import jax.numpy as jnp
        _gk = jax.random.key(seed)
        x = -0.0002117 + 1 * jax.random.normal(jax.random.fold_in(_gk, 1), (6250, 256), jnp.float32)
        src = jax.random.randint(jax.random.fold_in(_gk, 2), (100000,), 0, 6250, jnp.int32)
        dst = jax.random.randint(jax.random.fold_in(_gk, 3), (100000,), 0, 6250, jnp.int32)
        _o = jnp.argsort(dst, stable=True)
        src = src[_o]
        dst = dst[_o]
        edge_attr_64 = 0.000279952 + 1.00013 * jax.random.normal(jax.random.fold_in(_gk, 11), (100000, 64), jnp.float32)
        return (x, src, dst, edge_attr_64)
    x, src, dst, edge_attr_64 = _rec_inputs()

    def _L0_gnn_setup():
        import jax, jax.numpy as jnp
        import numpy as np
        N = 12500
        E = 40000
        CIN = 256
        EDIM = 64
        EEMB = 256
        H = 1024
        LN_EPS = 1e-05

        def _ln(x, g, b):
            m = jnp.mean(x, axis=-1, keepdims=True)
            v = jnp.var(x, axis=-1, keepdims=True)
            return (x - m) * jax.lax.rsqrt(v + LN_EPS) * g + b
        key = jax.random.key(seed)
        ks = jax.random.split(key, 16)

        def w(k, i, o):
            return (jax.random.normal(k, (i, o), jnp.float32) / np.sqrt(i)).astype(jnp.float32)
        return {'x': jax.random.normal(ks[0], (N, CIN), jnp.float32), 'edge_index': jax.random.randint(ks[1], (2, E), 0, N, dtype=jnp.int64), 'edge_attr': jax.random.normal(ks[2], (E, EDIM), jnp.float32), 'eps': jnp.float32(0.0), 'ee_w1': w(ks[3], EDIM, EEMB), 'ee_b1': jnp.zeros((EEMB,), jnp.float32), 'ee_w2': w(ks[4], EEMB, CIN), 'ee_b2': jnp.zeros((CIN,), jnp.float32), 'w1': w(ks[5], CIN, H), 'b1': jnp.zeros((H,), jnp.float32), 'g1': jnp.ones((H,), jnp.float32), 'be1': jnp.zeros((H,), jnp.float32), 'w2': w(ks[6], H, H), 'b2': jnp.zeros((H,), jnp.float32), 'g2': jnp.ones((H,), jnp.float32), 'be2': jnp.zeros((H,), jnp.float32), 'w3': w(ks[7], H, CIN), 'b3': jnp.zeros((CIN,), jnp.float32), 'bn_g': jnp.ones((CIN,), jnp.float32), 'bn_b': jnp.zeros((CIN,), jnp.float32)}
    _L0_gnn_all = _L0_gnn_setup()
    _L0_gnn_in = {k: v for k, v in _L0_gnn_all.items() if k in ('eps', 'ee_w1', 'ee_b1', 'ee_w2', 'ee_b2', 'w1', 'b1', 'g1', 'be1', 'w2', 'b2', 'g2', 'be2', 'w3', 'b3', 'bn_g', 'bn_b')}
    del _L0_gnn_all

    def _L1_gnn_setup():
        import jax, jax.numpy as jnp
        import numpy as np
        N = 6250
        E = 100000
        F_IN = 256
        K = 8
        F_OUT = 32
        NEG_SLOPE = 0.2
        key = jax.random.key(seed)
        k1, k2, k3, k4, k5, k6 = jax.random.split(key, 6)
        x = jax.random.normal(k1, (N, F_IN), dtype=jnp.float32)
        edge_index = jax.random.randint(k2, (2, E), 0, N, dtype=jnp.int64)
        W = jax.random.normal(k3, (F_IN, K * F_OUT), dtype=jnp.float32) * (2.0 / (F_IN + K * F_OUT)) ** 0.5
        b = jax.random.uniform(k4, (K * F_OUT,), dtype=jnp.float32)
        a_src = jax.random.normal(k5, (1, K, F_OUT), dtype=jnp.float32) * (2.0 / (K * F_OUT + 1)) ** 0.5
        a_trg = jax.random.normal(k6, (1, K, F_OUT), dtype=jnp.float32) * (2.0 / (K * F_OUT + 1)) ** 0.5
        return {'x': x, 'edge_index': edge_index, 'W': W, 'b': b, 'a_src': a_src, 'a_trg': a_trg}
    _L1_gnn_all = _L1_gnn_setup()
    _L1_gnn_in = {k: v for k, v in _L1_gnn_all.items() if k in ('W', 'b', 'a_src', 'a_trg')}
    del _L1_gnn_all
    return {'x': x, 'src': src, 'dst': dst, 'edge_attr_64': edge_attr_64, 'L0_gnn_eps': _L0_gnn_in['eps'], 'L0_gnn_ee_w1': _L0_gnn_in['ee_w1'], 'L0_gnn_ee_b1': _L0_gnn_in['ee_b1'], 'L0_gnn_ee_w2': _L0_gnn_in['ee_w2'], 'L0_gnn_ee_b2': _L0_gnn_in['ee_b2'], 'L0_gnn_w1': _L0_gnn_in['w1'], 'L0_gnn_b1': _L0_gnn_in['b1'], 'L0_gnn_g1': _L0_gnn_in['g1'], 'L0_gnn_be1': _L0_gnn_in['be1'], 'L0_gnn_w2': _L0_gnn_in['w2'], 'L0_gnn_b2': _L0_gnn_in['b2'], 'L0_gnn_g2': _L0_gnn_in['g2'], 'L0_gnn_be2': _L0_gnn_in['be2'], 'L0_gnn_w3': _L0_gnn_in['w3'], 'L0_gnn_b3': _L0_gnn_in['b3'], 'L0_gnn_bn_g': _L0_gnn_in['bn_g'], 'L0_gnn_bn_b': _L0_gnn_in['bn_b'], 'L1_gnn_W': _L1_gnn_in['W'], 'L1_gnn_b': _L1_gnn_in['b'], 'L1_gnn_a_src': _L1_gnn_in['a_src'], 'L1_gnn_a_trg': _L1_gnn_in['a_trg']}

def reference(x, src, dst, edge_attr_64, L0_gnn_eps, L0_gnn_ee_w1, L0_gnn_ee_b1, L0_gnn_ee_w2, L0_gnn_ee_b2, L0_gnn_w1, L0_gnn_b1, L0_gnn_g1, L0_gnn_be1, L0_gnn_w2, L0_gnn_b2, L0_gnn_g2, L0_gnn_be2, L0_gnn_w3, L0_gnn_b3, L0_gnn_bn_g, L0_gnn_bn_b, L1_gnn_W, L1_gnn_b, L1_gnn_a_src, L1_gnn_a_trg):
    import jax
    import jax.numpy as jnp

    def _L0_gnn_ref(x, edge_index, edge_attr, eps, ee_w1, ee_b1, ee_w2, ee_b2, w1, b1, g1, be1, w2, b2, g2, be2, w3, b3, bn_g, bn_b):
        import jax, jax.numpy as jnp
        import numpy as np
        N = 12500
        E = 40000
        CIN = 256
        EDIM = 64
        EEMB = 256
        H = 1024
        LN_EPS = 1e-05

        def _ln(x, g, b):
            m = jnp.mean(x, axis=-1, keepdims=True)
            v = jnp.var(x, axis=-1, keepdims=True)
            return (x - m) * jax.lax.rsqrt(v + LN_EPS) * g + b
        n = x.shape[0]
        sl = jnp.arange(n, dtype=edge_index.dtype)
        ei = jnp.concatenate([edge_index, jnp.stack([sl, sl], axis=0)], axis=1)
        ea = jnp.concatenate([edge_attr, jnp.zeros((n, edge_attr.shape[1]), edge_attr.dtype)], axis=0)
        src, dst = (ei[0], ei[1])
        e = jax.nn.relu(ea @ ee_w1 + ee_b1) @ ee_w2 + ee_b2
        msg = x[src] + e
        agg = jax.ops.segment_sum(msg, dst, num_segments=n)
        h = (1.0 + eps) * x + agg
        h = jax.nn.relu(_ln(h @ w1 + b1, g1, be1))
        h = jax.nn.relu(_ln(h @ w2 + b2, g2, be2))
        y = h @ w3 + b3
        out = x + y
        out = _ln(out, bn_g, bn_b)
        return jax.nn.relu(out)

    def _L1_gnn_ref(x, edge_index, W, b, a_src, a_trg):
        import jax, jax.numpy as jnp
        import numpy as np
        N = 6250
        E = 100000
        F_IN = 256
        K = 8
        F_OUT = 32
        NEG_SLOPE = 0.2
        n = x.shape[0]
        loops = jnp.arange(n, dtype=edge_index.dtype)
        src = jnp.concatenate([edge_index[0], loops])
        trg = jnp.concatenate([edge_index[1], loops])
        h_prime = (x @ W + b).reshape(n, K, F_OUT)
        h_src = jnp.sum(h_prime * a_src, axis=2)
        h_trg = jnp.sum(h_prime * a_trg, axis=2)
        e = h_src[src] + h_trg[trg]
        e = jax.nn.leaky_relu(e, negative_slope=NEG_SLOPE)
        e = e - jnp.max(e)
        exp_e = jnp.exp(e)
        denom = jax.ops.segment_sum(exp_e, trg, num_segments=n)
        alpha = exp_e / (denom[trg] + 1e-10)
        msg = h_prime[src] * alpha[:, :, None]
        out = jax.ops.segment_sum(msg, trg, num_segments=n)
        return out.reshape(n, K * F_OUT)
    edge_index = jnp.stack([src, dst])
    h = jnp.maximum(_layernorm(x, axis=-1), 0.0)
    x = x + _L0_gnn_ref(h, edge_index, edge_attr_64, L0_gnn_eps, L0_gnn_ee_w1, L0_gnn_ee_b1, L0_gnn_ee_w2, L0_gnn_ee_b2, L0_gnn_w1, L0_gnn_b1, L0_gnn_g1, L0_gnn_be1, L0_gnn_w2, L0_gnn_b2, L0_gnn_g2, L0_gnn_be2, L0_gnn_w3, L0_gnn_b3, L0_gnn_bn_g, L0_gnn_bn_b)
    h = jnp.maximum(_layernorm(x, axis=-1), 0.0)
    x = x + _L1_gnn_ref(h, edge_index, L1_gnn_W, L1_gnn_b, L1_gnn_a_src, L1_gnn_a_trg)
    return x

_drawn_inputs = setup_inputs


def setup_inputs(seed=0):
    import zlib

    import numpy as np

    out = dict(_drawn_inputs(seed))
    spreads = {'L0_gnn_ee_b1': (0.0, 0.322),
     'L0_gnn_ee_b2': (0.0, 0.1),
     'L0_gnn_b1': (0.0, 2.0),
     'L0_gnn_g1': (1.0, 0.2),
     'L0_gnn_be1': (0.0, 0.285),
     'L0_gnn_b2': (0.0, 0.1),
     'L0_gnn_g2': (1.0, 0.2),
     'L0_gnn_be2': (0.0, 0.27),
     'L0_gnn_b3': (0.0, 0.1),
     'L0_gnn_bn_g': (1.0, 0.2),
     'L0_gnn_bn_b': (0.0, 0.1)}
    factors = {'L1_gnn_a_trg': 23.262, 'L1_gnn_a_src': 3.138}
    for name, (base, spread) in spreads.items():
        noise = np.random.default_rng([zlib.crc32(name.encode()), seed]).standard_normal(out[name].shape)
        drawn = base * np.exp(spread * noise) if base else spread * noise
        out[name] = jnp.asarray(drawn.astype(out[name].dtype))
    for name, factor in factors.items():
        out[name] = (out[name] * factor).astype(out[name].dtype)
    return out
```

```python
from contextlib import ExitStack

import concourse.bass as bass
from concourse import mybir

F32, F16, I32, I16 = mybir.dt.float32, mybir.dt.float16, mybir.dt.int32, mybir.dt.int16
BF16 = mybir.dt.bfloat16
ALU = mybir.AluOpType
ACT = mybir.ActivationFunctionType
AX = mybir.AxisListType.X
PE, DVE = mybir.EngineType.PE, mybir.EngineType.DVE

P = 128
N, D, E, ED, H = 6250, 256, 100000, 64, 1024
TN = 125
NT = N // TN
CB = 4
BE = CB * P
RING = 4
NB = -(-E // (BE * RING)) * RING
NBP = NB + RING
NCH = NBP * CB
KH, KD = H // P, D // P
HEADS, HD = 8, 32
TW = D + HEADS
AW = D + 2 * HEADS
LN_EPS = 1e-5
SLOPE = 0.2
GUARD = 1e-10
WS = 64.0
PG = 10
FAR = -1.0e30
CAP = 87.0


def build(nc, t, out):
    with ExitStack() as ctx:
        keep = Memory(nc, ctx)
        dram = {
            "h0": nc.dram_tensor("h0_scratch", (N, D), F32, kind="Internal").ap(),
            "tab0": nc.dram_tensor("tab0_scratch", (N, 2 * D), F16, kind="Internal").ap(),
            "tab1": nc.dram_tensor("tab1_scratch", (N, TW), F32, kind="Internal").ap(),
            "x1": nc.dram_tensor("x1_scratch", (N, D), F32, kind="Internal").ap(),
            "sched": nc.dram_tensor("sched_scratch", (2, NBP + 4), I32, kind="Internal").ap(),
        }
        sb = {}
        for name, shape, dt in [
            ("acc", [P, NT, 2 * D], F32),
            ("ident", [P, P], F32), ("iota16", [P, TN], F16),
            ("negbase", [P, NT], F32), ("nodeid", [P, NT], F32),
            ("st", [P, NT, 2 * HEADS], F32),
            ("epscol", [P, 1], F32), ("lneps", [P, 1], F32),
        ]:
            sb[name] = keep.sb(name, shape, dt)
        with ExitStack() as first:
            layer0 = Memory(nc, first)
            for name, shape, dt in [
                ("w1h", [P, KD, H], F16), ("w1l", [P, KD, H], F16),
                ("w2h", [P, KH, H], F16), ("w2l", [P, KH, H], F16),
                ("w3h", [P, KH, D], F16), ("w3l", [P, KH, D], F16),
            ]:
                sb[name] = layer0.sb(name, shape, dt)
            with ExitStack() as edge_mlp:
                for name, shape, dt in [("ewa", [P, D], F16), ("ewb", [ED + 2, D], F16)]:
                    sb[name] = Memory(nc, edge_mlp).sb(name, shape, dt)
                stale = prepare(nc, t, dram, sb)
                edges0(nc, t, dram, sb)
            nodes(nc, t, dram, sb, stale)
        smax, maxima = edges1(nc, t, dram, sb, keep)
        finish(nc, t, dram, sb, smax, maxima, out)


class Memory:

    def __init__(self, nc, ctx):
        self.nc, self.ctx, self.sems = nc, ctx, []

    def sb(self, name, shape, dt):
        return self.ctx.enter_context(self.nc.sbuf_tensor(name, shape, dt))

    def ps(self, name, shape, dt=F32):
        return self.ctx.enter_context(self.nc.psum_tensor(name, shape, dt))

    def sem(self, name):
        self.sems.append(self.ctx.enter_context(self.nc.semaphore(name)))
        return self.sems[-1]


def prepare(nc, t, dram, sb):
    with ExitStack() as ctx:
        m = Memory(nc, ctx)
        acc = sb["acc"]
        flat = acc[:].rearrange("p t c -> p (t c)")
        xall = flat[0:TN, 0:NT * D].rearrange("p (t c) -> p t c", c=D)
        o = NT * D
        w1r = flat[:, o:o + KD * H].rearrange("p (k n) -> p k n", n=H)
        w2r = flat[:, o + KD * H:o + (KD + KH) * H].rearrange("p (k n) -> p k n", n=H)
        o += (KD + KH) * H
        w3r = flat[:, o:o + KH * D].rearrange("p (k n) -> p k n", n=D)

        icol = m.sb("icol", [P, P], I32)
        idiag = m.sb("idiag", [P, P], I32)
        ineg = m.sb("ineg", [P, NT], I32)
        inode = m.sb("inode", [P, NT], I32)
        ithr = m.sb("ithr", [P, NT - 1], I32)
        thr = m.sb("thr", [P, NT - 1], F32)
        b2bc = m.sb("p_b2bc", [TN, D], F32)
        er = m.sb("er", [P, D], F32)
        ebr = m.sb("ebr", [ED + 2, D], F32)
        ebh = m.sb("ebh", [ED + 2, D], F16)
        stat = m.sb("stat", [TN, PG, 6], F32)
        mv = m.sb("mv", [TN, PG, 2], F32)
        sd = m.sb("sd", [TN, PG], F32)
        rstd = m.sb("rstd", [TN, PG], F32)
        nmr = m.sb("nmr", [TN, PG], F32)
        h0 = m.sb("h0", [TN, PG, D], F32)
        tb = m.sb("tb", [TN, PG, 2 * D], F16)
        wsum = m.sb("wsum", [P, KD + KH], F32)
        wneg = m.sb("wneg", [P, KD + KH], F32)
        half = NBP // 2
        drow = m.sb("drow", [half, 2, BE], I32)
        ext = m.sb("ext", [half, 4], F32)
        cmp_ = m.sb("cmp_", [half, 4, NT - 1], F32)
        tile = m.sb("tile", [half, 4], F32)
        sched_sb = m.sb("sched_sb", [half, 2, 2], I32)

        ld_x = [m.sem(f"ld_x{i}") for i in range(NT // PG)]
        ld_w = m.sem("ld_w")
        ld_small = m.sem("ld_small")
        ld_dst = m.sem("ld_dst")
        iotas = m.sem("iotas")
        eb_split = m.sem("eb_split")
        norm_in = m.sem("norm_in")
        var_ready = m.sem("var_ready")
        sd_ready = m.sem("sd_ready")
        coef_ready = m.sem("coef_ready")
        h0_ready = m.sem("h0_ready")
        t_ready = m.sem("t_ready")
        hi_ready = m.sem("hi_ready")
        tb_ready = m.sem("tb_ready")
        h0_stored = m.sem("h0_stored")
        tb_stored = m.sem("tb_stored")
        wsum_ready = m.sem("wsum_ready")
        wneg_ready = m.sem("wneg_ready")
        whi_ready = m.sem("whi_ready")
        act_chain = m.sem("p_act_chain")
        dve_chain = m.sem("p_dve_chain")
        sched_ready = m.sem("sched_ready")
        stored = m.sem("p_stored")
        ewb_done = m.sem("ewb_done")
        x_v = t["x"].rearrange("(p t) c -> p t c", t=NT)
        h0_v = dram["h0"].rearrange("(p t) c -> p t c", t=NT)
        tb_v = dram["tab0"].rearrange("(p t) c -> p t c", t=NT)
        splits = ([(w1r[:, k, :], sb["w1h"][:, k, :], sb["w1l"][:, k, :]) for k in range(KD)]
                  + [(w2r[:, k, :], sb["w2h"][:, k, :], sb["w2l"][:, k, :]) for k in range(KH)])
        w3s = (w3r[:, :, :], sb["w3h"][:, :, :], sb["w3l"][:, :, :])

        block = ctx.enter_context(nc.Block())

        @block.sync
        def _(sp):
            for i in range(NT // PG):
                sp.dma_start(xall[:, i * PG:(i + 1) * PG, :], x_v[:, i * PG:(i + 1) * PG, :]).then_inc(ld_x[i], 16)
            sp.dma_start(drow[:], t["dst_flat"].rearrange("(p j e) -> p j e", p=half, j=2)).then_inc(ld_dst, 16)
            sp.dma_start(w1r, t["L0_gnn_w1"].rearrange("(k p) n -> p k n", p=P)).then_inc(ld_w, 16)
            sp.dma_start(w2r, t["L0_gnn_w2"].rearrange("(k p) n -> p k n", p=P)).then_inc(ld_w, 16)
            sp.dma_start(w3r, t["L0_gnn_w3"].rearrange("(k p) n -> p k n", p=P)).then_inc(ld_w, 16)
            with sp.Fori(0, NT // PG) as i:
                sp.wait_ge(h0_ready, 1)
                sp.sem_inc(h0_ready, -1)
                sp.dma_start(h0_v[:, bass.ds(i * PG, PG), :], h0[:]).then_inc(h0_stored, 16)
                sp.wait_ge(tb_ready, 1)
                sp.sem_inc(tb_ready, -1)
                sp.dma_start(tb_v[:, bass.ds(i * PG, PG), :], tb[:]).then_inc(tb_stored, 16)
            sp.wait_ge(sched_ready, 1)
            sp.sem_inc(sched_ready, -1)
            for part in range(2):
                row = dram["sched"][part]
                sp.dma_start(row[1:NBP + 1].rearrange("(p j) -> p j", j=2), sched_sb[:, part, :]).then_inc(stored, 16)
                sp.dma_start(row[0:1].unsqueeze(0), sched_sb[0:1, part, 0:1]).then_inc(stored, 16)
            sp.wait_ge(stored, 64)
            sp.wait_ge(h0_stored, 16)
            sp.wait_ge(tb_stored, 16)

        @block.gpsimd
        def _(pool):
            pool.iota(icol[:], [[1, P]], base=0, channel_multiplier=0).then_inc(iotas, 1)
            pool.iota(idiag[:], [[1, P]], base=0, channel_multiplier=-1).then_inc(iotas, 1)
            pool.iota(ineg[:], [[-TN, NT]], base=0, channel_multiplier=0).then_inc(iotas, 1)
            pool.iota(inode[:], [[TN, NT]], base=0, channel_multiplier=1).then_inc(iotas, 1)
            pool.iota(ithr[:], [[TN, NT - 1]], base=TN, channel_multiplier=0).then_inc(iotas, 1)

        @block.scalar
        def _(act):
            act.dma_start(b2bc[:], t["L0_gnn_ee_b2"].partition_broadcast(TN)).then_inc(ld_small, 16)
            act.dma_start(er[0:ED, :], t["L0_gnn_ee_w1"]).then_inc(ld_small, 16)
            act.dma_start(er[ED:2 * ED, :], t["L0_gnn_ee_w1"]).then_inc(ld_small, 16)
            act.dma_start(ebr[0:ED, :], t["L0_gnn_ee_w1"]).then_inc(ld_small, 16)
            act.dma_start(ebr[ED:ED + 2, :], t["L0_gnn_ee_b1"].partition_broadcast(2)).then_inc(ld_small, 16)
            act.dma_start(sb["epscol"][:], t["L0_gnn_eps"].partition_broadcast(P)).then_inc(ld_small, 16)
            with act.Fori(0, NT // PG) as i:
                act.wait_ge(var_ready, 1)
                act.sem_inc(var_ready, -1)
                act.activation(sd[:], mv[:, :, 1], ACT.Sqrt, bias=sb["lneps"][0:TN, :]).then_inc(sd_ready, 1)
                act.wait_ge(coef_ready, 1)
                act.sem_inc(coef_ready, -1)
                for j in range(PG):
                    act.activation(h0[:, j, :], xall[:, bass.ds(i * PG + j, 1), :].rearrange("p a c -> p (a c)"),
                                   ACT.Relu, bias=nmr[:, j:j + 1], scale=rstd[:, j:j + 1]).then_inc(act_chain, 1)
                act.wait_ge(act_chain, PG)
                act.sem_inc(act_chain, -PG)
                act.sem_inc(h0_ready, 1)
                act.sem_inc(norm_in, 1)
                act.wait_ge(t_ready, 1)
                act.sem_inc(t_ready, -1)
                act.activation(tb[:, :, 0:D], xall[:, bass.ds(i * PG, PG), :], ACT.Copy).then_inc(hi_ready, 1)
            act.wait_ge(ld_w, 48)
            for k, (raw, hi, _) in enumerate(splits):
                act.activation(hi, raw, ACT.Copy, accum_out=wsum[:, k:k + 1]).then_inc(wsum_ready, 1)
            act.wait_ge(wneg_ready, 1)
            act.sem_inc(wneg_ready, -1)
            for k, (raw, _, _) in enumerate(splits):
                act.activation(raw, raw, ACT.Identity, bias=wneg[:, k:k + 1], scale=WS).then_inc(act_chain, 1)
            act.activation(w3s[0], w3s[0], ACT.Copy, scale=WS).then_inc(act_chain, 1)
            act.wait_ge(act_chain, KD + KH + 1)
            act.sem_inc(act_chain, -(KD + KH + 1))
            for raw, hi, _ in splits:
                act.activation(hi, raw, ACT.Copy).then_inc(whi_ready, 1)
            act.activation(w3s[1], w3s[0], ACT.Copy).then_inc(whi_ready, 1)
            act.wait_ge(eb_split, 1)
            act.sem_inc(eb_split, -1)
            act.dma_start(sb["ewb"][ED:ED + 1, :], ebh[ED:ED + 1, :]).then_inc(ewb_done, 16)
            act.wait_ge(ewb_done, 16)

        @block.vector
        def _(dve):
            dve.memset(sb["lneps"][:], LN_EPS).then_inc(dve_chain, 1)
            dve.wait_ge(dve_chain, 1)
            dve.sem_inc(dve_chain, -1)
            for i in range(NT // PG):
                dve.wait_ge(ld_x[i], 16)
            dve.wait_ge(ld_small, 96)
            dve.sem_inc(tb_stored, 16)
            dve.sem_inc(h0_stored, 16)
            with dve.Fori(0, NT // PG) as i:
                for j in range(PG):
                    dve.bn_stats(stat[:, j, :], xall[:, bass.ds(i * PG + j, 1), :].rearrange("p a c -> p (a c)")).then_inc(dve_chain, 1)
                dve.wait_ge(dve_chain, PG)
                dve.sem_inc(dve_chain, -PG)
                for j in range(PG):
                    dve.bn_aggr(mv[:, j, :], stat[:, j, :]).then_inc(dve_chain, 1)
                dve.wait_ge(dve_chain, PG)
                dve.sem_inc(dve_chain, -PG)
                dve.sem_inc(var_ready, 1)
                dve.wait_ge(sd_ready, 1)
                dve.sem_inc(sd_ready, -1)
                dve.reciprocal(rstd[:], sd[:]).then_inc(dve_chain, 1)
                dve.wait_ge(dve_chain, 1)
                dve.sem_inc(dve_chain, -1)
                dve.wait_ge(h0_stored, 16)
                dve.sem_inc(h0_stored, -16)
                dve.scalar_tensor_tensor(out=nmr[:], in0=mv[:, :, 0], scalar=-1.0, in1=rstd[:],
                                         op0=ALU.mult, op1=ALU.mult).then_inc(coef_ready, 1)
                dve.wait_ge(norm_in, 1)
                dve.sem_inc(norm_in, -1)
                xs = xall[:, bass.ds(i * PG, PG), :]
                dve.tensor_tensor(xs, h0[:], b2bc[:].unsqueeze(1).broadcast_to([TN, PG, D]), ALU.add).then_inc(dve_chain, 1)
                dve.wait_ge(dve_chain, 1)
                dve.sem_inc(dve_chain, -1)
                dve.wait_ge(tb_stored, 16)
                dve.sem_inc(tb_stored, -16)
                dve.sem_inc(t_ready, 1)
                dve.wait_ge(hi_ready, 1)
                dve.sem_inc(hi_ready, -1)
                dve.tensor_tensor(tb[:, :, D:2 * D], xs, tb[:, :, 0:D], ALU.subtract).then_inc(tb_ready, 1)
            dve.wait_ge(iotas, 5)
            dve.sem_inc(iotas, -5)
            dve.tensor_copy(sb["iota16"][:], icol[:, 0:TN]).then_inc(dve_chain, 1)
            dve.wait_ge(dve_chain, 1)
            dve.sem_inc(dve_chain, -1)
            dve.tensor_copy(sb["negbase"][:], ineg[:]).then_inc(dve_chain, 1)
            dve.wait_ge(dve_chain, 1)
            dve.sem_inc(dve_chain, -1)
            dve.tensor_copy(sb["nodeid"][:], inode[:]).then_inc(dve_chain, 1)
            dve.wait_ge(dve_chain, 1)
            dve.sem_inc(dve_chain, -1)
            dve.tensor_copy(thr[:], ithr[:]).then_inc(dve_chain, 1)
            dve.wait_ge(dve_chain, 1)
            dve.sem_inc(dve_chain, -1)
            dve.tensor_scalar(sb["ident"][:], idiag[:], 0.0, None, ALU.is_equal).then_inc(dve_chain, 1)
            dve.wait_ge(dve_chain, 1)
            dve.sem_inc(dve_chain, -1)
            dve.tensor_scalar(sb["epscol"][:], sb["epscol"][:], 2.0, None, ALU.add).then_inc(dve_chain, 1)
            dve.wait_ge(dve_chain, 1)
            dve.sem_inc(dve_chain, -1)
            dve.tensor_copy(sb["ewa"][:], er[:]).then_inc(dve_chain, 1)
            dve.wait_ge(dve_chain, 1)
            dve.sem_inc(dve_chain, -1)
            dve.tensor_copy(ebh[:], ebr[:]).then_inc(dve_chain, 1)
            dve.wait_ge(dve_chain, 1)
            dve.sem_inc(dve_chain, -1)
            dve.tensor_tensor(sb["ewb"][:], ebr[:], ebh[:], ALU.subtract).then_inc(dve_chain, 1)
            dve.wait_ge(dve_chain, 1)
            dve.sem_inc(dve_chain, -1)
            dve.sem_inc(eb_split, 1)
            dve.wait_ge(ld_dst, 16)
            dve.sem_inc(ld_dst, -16)
            for j in range(2):
                dve.tensor_reduce(ext[:, j:j + 1], drow[:, j, :], AX, ALU.min).then_inc(dve_chain, 1)
                dve.wait_ge(dve_chain, 1)
                dve.sem_inc(dve_chain, -1)
                dve.tensor_reduce(ext[:, 2 + j:3 + j], drow[:, j, :], AX, ALU.max).then_inc(dve_chain, 1)
                dve.wait_ge(dve_chain, 1)
                dve.sem_inc(dve_chain, -1)
            dve.tensor_tensor(cmp_[:], ext[:].unsqueeze(2).broadcast_to([half, 4, NT - 1]),
                              thr[0:half, :].unsqueeze(1).broadcast_to([half, 4, NT - 1]), ALU.is_ge).then_inc(dve_chain, 1)
            dve.wait_ge(dve_chain, 1)
            dve.sem_inc(dve_chain, -1)
            dve.tensor_reduce(tile[:], cmp_[:], AX, ALU.add).then_inc(dve_chain, 1)
            dve.wait_ge(dve_chain, 1)
            dve.sem_inc(dve_chain, -1)
            dve.tensor_copy(sched_sb[:, 0, :], tile[:, 0:2]).then_inc(dve_chain, 1)
            dve.wait_ge(dve_chain, 1)
            dve.sem_inc(dve_chain, -1)
            dve.tensor_scalar(sched_sb[:, 1, :], tile[:, 2:4], 1.0, None, ALU.add).then_inc(sched_ready, 1)
            dve.wait_ge(wsum_ready, KD + KH)
            dve.sem_inc(wsum_ready, -(KD + KH))
            dve.tensor_scalar(wneg[:], wsum[:], -WS / H, None, ALU.mult).then_inc(wneg_ready, 1)
            dve.wait_ge(whi_ready, KD + KH + 1)
            dve.sem_inc(whi_ready, -(KD + KH + 1))
            for raw, hi, lo in splits + [w3s]:
                dve.tensor_tensor(lo, raw, hi, ALU.subtract).then_inc(dve_chain, 1)
                dve.wait_ge(dve_chain, 1)
                dve.sem_inc(dve_chain, -1)
    return m.sems


def one_hot(dve, out, iota16, dsts, negbase, b, tile, passed=None):
    for k in range(CB):
        ins = dve.tensor_scalar(out[:, k, :], iota16[:], dsts[:, bass.ds(CB * (b + 1) + k, 1)],
                                negbase[:, bass.ds(tile, 1)], ALU.subtract, ALU.is_equal)
        if passed is not None and k == 0:
            ins.then_inc(passed, 1)
    return ins


def tiles_of(nc, engine, table, b, n):
    why = "the schedule counts the tile bounds that a dst has passed: 0 to NT - 1, and one more for ends"
    both = []
    for part, least in ((0, 0), (1, 1)):
        _, v = nc.values_load_multi_w_load_instructions(
            table[0:1, part, bass.ds(b + 1, n)], engines=[engine], min_val=least, max_val=NT - 1 + part,
            skip_runtime_bounds_check_because=why)
        both.append(v)
    return list(zip(*both))


def edges0(nc, t, dram, sb):
    with ExitStack() as ctx:
        m = Memory(nc, ctx)
        acc, iota16, negbase, ewa, ewb = sb["acc"], sb["iota16"], sb["negbase"], sb["ewa"], sb["ewb"]
        srcs = m.sb("srcs", [P, NCH], I32)
        dsts = m.sb("dsts", [P, NCH + CB], F32)
        idx = m.sb("idx", [P, RING, CB], I32)
        table = m.sb("table0", [1, 2, NBP + 4], I32)
        rows = m.sb("rows", [P, RING, CB, 2 * D], F16)
        ea = m.sb("ea", [P, 2, BE], F32)
        eab = m.sb("eab", [P, 2, BE], F16)
        eah = m.sb("eah", [ED + 2, 2, BE], F16)
        rh = m.sb("rh", [P, 2, CB, D], F16)
        rl = m.sb("rl", [P, 2, CB, D], F16)
        hot = m.sb("hot", [P, 3, CB, TN], F16)
        mlp_ps = m.ps("mlp_ps", [P, 2, CB, D])
        sum_ps = m.ps("sum_ps", [TN, 3, 2 * D])
        used_ps = m.ps("used_ps", [1, 1])

        ld_idx = m.sem("ld_idx")
        ld_dst = m.sem("e_ld_dst")
        ld_tab = m.sem("ld_tab")
        cleared = m.sem("cleared")
        idx_ready = [m.sem(f"idx_ready{s}") for s in range(RING)]
        rows_ready = [m.sem(f"rows_ready{s}") for s in range(RING)]
        ea_ready = [m.sem(f"ea_ready{s}") for s in range(2)]
        ea_free = m.sem("ea_free")
        ones_ready = m.sem("ones_ready")
        ea_high = m.sem("ea_high")
        ea_split = m.sem("ea_split")
        mlp_done = m.sem("mlp_done")
        r_high = m.sem("r_high")
        r_split = m.sem("r_split")
        r_free = m.sem("r_free")
        rows_free = m.sem("rows_free")
        x_chain = m.sem("x_chain")
        hot_ready = m.sem("hot_ready")
        sum_done = m.sem("sum_done")
        sum_free = m.sem("sum_free")
        xhot_ready = m.sem("xhot_ready")
        xsum_done = m.sem("xsum_done")
        chain_sem = m.sem("e_chain")

        block = ctx.enter_context(nc.Block())

        @block.sync
        def _(sp):
            sp.dma_start(srcs[:], t["src_cols"]).then_inc(ld_idx, 16)
            sp.dma_start(table[:, :, 0:NBP + 1], dram["sched"][:, 0:NBP + 1].unsqueeze(0)).then_inc(ld_tab, 16)

            def load(b, s):
                eb = t["edge_t"][bass.ds(b, 1)].rearrange("a d e -> (a d) e")
                sp.dma_start(ea[0:ED, s, :], eb).then_inc(ea_ready[s], 16)
                sp.dma_start(ea[ED:P, s, :], eb).then_inc(ea_ready[s], 16)

            load(0, 0)
            sp.sem_inc(ea_free, 1)
            with sp.Fori(0, NB // RING) as i:
                for u in range(RING):
                    sp.wait_ge(ea_free, 1)
                    sp.sem_inc(ea_free, -1)
                    load(RING * i + u + 1, (u + 1) % 2)

        @block.gpsimd
        def _(pool):
            pool.dma_start(dsts[:], t["dst_cols"]).then_inc(ld_dst, 16)
            pool.memset(eah[ED:ED + 2, :, :], 1.0).then_inc(ones_ready, 1)
            with pool.Fori(0, NB // RING):
                for s in range(RING):
                    pool.wait_ge(idx_ready[s], 1)
                    pool.sem_inc(idx_ready[s], -1)
                    for k in range(CB):
                        pool.indirect_dma_start(
                            rows[:, s, k, :], None, dram["tab0"],
                            bass.IndirectOffsetOnAxis(ap=idx[:, s, k:k + 1], axis=0),
                        ).then_inc(rows_ready[s], 16)

        @block.scalar
        def _(act):
            def high_parts(s):
                act.wait_ge(ea_ready[s], 32)
                act.sem_inc(ea_ready[s], -32)
                act.activation(eab[:, s, :], ea[:, s, :], ACT.Copy).then_inc(ea_high, 1)
                act.activation(eah[0:ED, s, :], ea[0:ED, s, :], ACT.Copy).then_inc(ea_high, 1)

            act.sem_inc(r_free, 2)
            high_parts(0)
            zero = acc[:, NT // 2:NT, :].rearrange("p t c -> p (t c)")
            act.activation(zero, iota16[:, 0:1].broadcast_to([P, NT // 2 * 2 * D]), ACT.Copy, scale=0.0).then_inc(cleared, 1)
            with act.Fori(0, NB // RING) as i:
                for u in range(RING):
                    b, s = RING * i + u, u % 2
                    high_parts(1 - s)
                    act.wait_ge(mlp_done, 1)
                    act.sem_inc(mlp_done, -1)
                    act.wait_ge(r_free, 1)
                    act.sem_inc(r_free, -1)
                    act.activation(rh[:, s].rearrange("p k d -> p (k d)"), mlp_ps[:, s].rearrange("p k d -> p (k d)"),
                                   ACT.Relu).then_inc(r_high, 1)

        @block.tensor
        def _(pe):
            def edge_mlp(s):
                pe.wait_ge(ea_split, 1)
                pe.sem_inc(ea_split, -1)
                pe.sem_inc(ea_free, 1)
                for k in range(CB):
                    e = slice(k * P, (k + 1) * P)
                    pe.matmul(mlp_ps[:, s, k, :], eab[:, s, e], ewa[:], start=True, stop=False)
                    ins = pe.matmul(mlp_ps[:, s, k, :], eah[:, s, e], ewb[:], start=False, stop=True)
                ins.then_inc(mlp_done, 1)

            def sums(out, h, ring, s):
                for k in range(CB):
                    lhs = hot[:, h, k, :]
                    pe.matmul(out[:, 0:D], lhs, rows[:, ring, k, 0:D], start=(k == 0), stop=False, skip_group_check=True)
                    pe.matmul(out[:, 0:D], lhs, rows[:, ring, k, D:2 * D], start=False, stop=False, skip_group_check=True)
                    pe.matmul(out[:, D:2 * D], lhs, rh[:, s, k, :], start=False, stop=False, skip_group_check=True)
                    ins = pe.matmul(out[:, D:2 * D], lhs, rl[:, s, k, :], start=False, stop=(k == CB - 1), skip_group_check=True)
                return ins

            pe.wait_ge(ld_tab, 16)
            pe.wait_ge(ones_ready, 1)
            pe.sem_inc(ones_ready, -1)
            pe.sem_inc(sum_free, 2)
            edge_mlp(0)
            with pe.Fori(0, NB // RING) as i:
                tiles = tiles_of(nc, PE, table, RING * i, RING)
                for u in range(RING):
                    b, s = RING * i + u, u % 2
                    edge_mlp(1 - s)
                    lo, end = tiles[u]
                    pe.wait_ge(hot_ready, 1)
                    pe.sem_inc(hot_ready, -1)
                    pe.wait_ge(sum_free, 1)
                    pe.sem_inc(sum_free, -1)
                    pe.wait_ge(r_split, 1)
                    pe.sem_inc(r_split, -1)
                    pe.wait_ge(rows_ready[u], 16 * CB * (i + 1))
                    sums(sum_ps[:, s, :], s, u, s).then_inc(sum_done, 1)
                    with pe.If(end > lo + 1):
                        with pe.Fori(lo + 1, end):
                            pe.wait_ge(xhot_ready, 1)
                            pe.sem_inc(xhot_ready, -1)
                            sums(sum_ps[:, 2, :], 2, u, s).then_inc(xsum_done, 1)
                    pe.matmul(used_ps[:], ewa[:, 0:1], ewa[:, 0:1], start=True, stop=True).then_inc(r_free, 1)
                    pe.matmul(used_ps[:], ewa[:, 0:1], ewa[:, 0:1], start=True, stop=True).then_inc(rows_free, 1)

        @block.vector
        def _(dve):
            def low_parts(s):
                dve.wait_ge(ea_high, 2)
                dve.sem_inc(ea_high, -2)
                dve.tensor_tensor(eab[ED:P, s, :], ea[ED:P, s, :], eab[ED:P, s, :], ALU.subtract).then_inc(ea_split, 1)

            def add(s, lo):
                dve.wait_ge(chain_sem, 1)
                dve.sem_inc(chain_sem, -1)
                dve.wait_ge(sum_done, 1)
                dve.sem_inc(sum_done, -1)
                a = acc[0:TN, bass.ds(lo, 1), :].rearrange("p a c -> p (a c)")
                dve.tensor_tensor(a, a, sum_ps[:, s, :], ALU.add).then_inc(sum_free, 1)

            def extras(b, lo, end):
                with dve.If(end > lo + 1):
                    with dve.Fori(lo + 1, end) as x:
                        one_hot(dve, hot[:, 2], iota16, dsts, negbase, b, x).then_inc(xhot_ready, 1)
                        dve.wait_ge(xsum_done, 1)
                        dve.sem_inc(xsum_done, -1)
                        ax = acc[0:TN, bass.ds(x, 1), :].rearrange("p a c -> p (a c)")
                        dve.tensor_tensor(ax, ax, sum_ps[:, 2, :], ALU.add).then_inc(x_chain, 1)
                        dve.wait_ge(x_chain, 1)
                        dve.sem_inc(x_chain, -1)

            def indices(b, s):
                dve.tensor_copy(idx[:, s, :], srcs[:, bass.ds(CB * b, CB)]).then_inc(idx_ready[s], 1)

            def finish_block(b, ring, tiles):
                extras(b, *tiles)
                dve.wait_ge(rows_free, 1)
                dve.sem_inc(rows_free, -1)
                indices(b + RING, ring)

            def main_hot(b, s, lo):
                one_hot(dve, hot[:, s], iota16, dsts, negbase, b, lo, chain_sem).then_inc(hot_ready, 1)

            dve.wait_ge(ld_dst, 16)
            dve.wait_ge(ld_tab, 16)
            dve.wait_ge(ld_idx, 16)
            for b in range(RING):
                indices(b, b)
            main_hot(0, 0, tiles_of(nc, DVE, table, 0, 1)[0][0])
            dve.wait_ge(chain_sem, 1)
            dve.sem_inc(chain_sem, -1)
            low_parts(0)
            dve.memset(acc[:, 0:NT // 2, :], 0.0).then_inc(chain_sem, 1)
            dve.wait_ge(chain_sem, 1)
            dve.sem_inc(chain_sem, -1)
            dve.wait_ge(cleared, 1)
            dve.sem_inc(cleared, -1)
            with dve.Fori(0, NB // RING) as i:
                tiles = tiles_of(nc, DVE, table, RING * i - 1, RING + 2)
                for u in range(RING):
                    b, s = RING * i + u, u % 2
                    low_parts(1 - s)
                    dve.wait_ge(r_high, 1)
                    dve.sem_inc(r_high, -1)
                    dve.scalar_tensor_tensor(out=rl[:, s].rearrange("p k d -> p (k d)"), in0=mlp_ps[:, s].rearrange("p k d -> p (k d)"),
                                             scalar=0.0, in1=rh[:, s].rearrange("p k d -> p (k d)"),
                                             op0=ALU.max, op1=ALU.subtract).then_inc(r_split, 1)
                    if u:
                        add(1 - s, tiles[u][0])
                    else:
                        with dve.If(i > 0):
                            add(1 - s, tiles[u][0])
                    main_hot(b + 1, 1 - s, tiles[u + 2][0])
                    if u:
                        finish_block(b - 1, u - 1, tiles[u])
                    else:
                        with dve.If(i > 0):
                            finish_block(b - 1, RING - 1, tiles[u])
            lo, end = tiles_of(nc, DVE, table, NB - 1, 1)[0]
            add((NB - 1) % 2, lo)
            extras(NB - 1, lo, end)


def nodes(nc, t, dram, sb, stale):
    with ExitStack() as ctx:
        m = Memory(nc, ctx)
        acc, ident, lneps, epscol = sb["acc"], sb["ident"], sb["lneps"], sb["epscol"]
        w2e = m.sb("w2e", [P, KD, D], F32)
        waug = m.sb("waug", [P, KD, AW], F32)
        bcol = m.sb("bcol", [P, KD], F32)
        ones = m.sb("ones", [P, P], F32)
        zero = m.sb("zero", [P, 1], F32)
        eb1 = m.sb("eb1", [P, KD], F32)
        cols = {n: m.sb("c_" + n, [P, KH], F32) for n in ("b1", "g1", "be1", "b2", "g2", "be2")}
        csum = m.sb("csum", [P, 2], F32)
        bc = {n: m.sb("bc_" + n, [TN, D], F32) for n in ("ee_b2", "b3", "bn_g", "bn_b")}
        baug = m.sb("baug", [TN, AW], F32)
        hf = m.sb("hf", [TN, 2, D], F32)
        u = m.sb("u", [TN, 2, D], F32)
        rr = m.sb("rr", [TN, 2, D], F32)
        rt = m.sb("rt", [P, KD, TN], F32)
        hh = m.sb("hh", [P, KD, TN], F16)
        hl = m.sb("hl", [P, KD, TN], F16)
        z = [m.sb(f"z{j}", [P, KH, TN], F32) for j in (1, 2)]
        a = m.sb("a", [P, KH, TN], F32)
        room = z[0][:].rearrange("p k n -> p (k n)")
        o1, o2 = KD * D, KD * (D + TN)
        wt = room[:, 0:o1].rearrange("p (k n) -> p k n", n=D)
        bcb = room[:, o1:o2].rearrange("p (k n) -> p k n", n=TN)
        att = room[:, o2:o2 + KD * 2 * HEADS].rearrange("p (k n) -> p k n", n=2 * HEADS)
        ah = [m.sb(f"ah{j}", [P, n, KH, TN], F16) for j, n in ((1, 2), (2, 1))]
        al = [m.sb(f"al{j}", [P, n, KH, TN], F16) for j, n in ((1, 2), (2, 1))]
        ssq = [m.sb(f"ssq{j}", [P, TN], F32) for j in (1, 2)]
        sd = [m.sb(f"sd{j}", [P, TN], F32) for j in (1, 2)]
        hx = m.sb("hx", [TN, 2, 2, D], F32)
        o = m.sb("o", [TN, D], F32)
        x1 = m.sb("x1", [TN, 2, D], F32)
        h2 = m.sb("h2", [TN, D], F32)
        h2t = m.sb("h2t", [P, KD, TN], F32)
        prow = m.sb("prow", [TN, 2, AW], F32)
        st3 = m.sb("st3", [TN, 2, 6], F32)
        mv3 = m.sb("mv3", [TN, 2, 2], F32)
        co3 = m.sb("co3", [TN, 2, 3], F32)

        z_ps = [m.ps(f"z{j}_ps", [P, 2, 512]) for j in (1, 2)]
        tv_ps = m.ps("tv_ps", [P, 4, TN])
        h_ps = m.ps("h_ps", [P, KD, TN])
        y_ps = m.ps("y_ps", [P, D])
        gp_ps = m.ps("gp_ps", [P, 512])
        t_ps, v_ps = tv_ps[:, 0:KD, :], [tv_ps[:, KD + j, :] for j in (0, 1)]
        g_ps = gp_ps[:, 0:KD * TN].rearrange("p (k n) -> p k n", n=TN)
        p_ps = gp_ps[0:TN, 0:AW]

        def sem(n):
            return m.sem("n_" + n)

        ld, ld_act, setup, setup_ps, setup_done, ready = (
            sem("ld"), sem("ld_act"), sem("setup"), sem("setup_ps"), sem("setup_done"), sem("ready"))
        hf_ready = [sem(f"hf_ready{p}") for p in (0, 1)]
        hx_ready = [sem(f"hx_ready{p}") for p in (0, 1)]
        hf_free, hx_free = sem("hf_free"), sem("hx_free")
        u_ready, acc_free = sem("u_ready"), sem("acc_free")
        rr_ready, rr_free, t_done, rt_ready = sem("rr_ready"), sem("rr_free"), sem("t_done"), sem("rt_ready")
        h_done, hh_ready, h_split = sem("h_done"), sem("hh_ready"), sem("h_split")
        z_done = [sem(f"z{j}_done") for j in (1, 2)]
        z_ready = [sem(f"z{j}_ready") for j in (1, 2)]
        ssq_ready = [sem(f"ssq{j}_ready") for j in (1, 2)]
        var_done = [sem(f"var{j}_done") for j in (1, 2)]
        sd_ready = [sem(f"sd{j}_ready") for j in (1, 2)]
        zn_ready = [sem(f"zn{j}_ready") for j in (1, 2)]
        a_ready = [sem(f"a{j}_ready") for j in (1, 2)]
        ah_ready = [sem(f"ah{j}_ready") for j in (1, 2)]
        a_split = [sem(f"a{j}_split") for j in (1, 2)]
        y_done, y_free, hb_ready = sem("y_done"), sem("y_free"), sem("hb_ready")
        row_var = [sem(f"row_var{j}") for j in (0, 1)]
        row_sd = [sem(f"row_sd{j}") for j in (0, 1)]
        row_coef = [sem(f"row_coef{j}") for j in (0, 1)]
        on_ready, x1_ready, h2_ready = sem("on_ready"), sem("x1_ready"), sem("h2_ready")
        x1_stored = [sem(f"x1_stored{p}") for p in (0, 1)]
        g_done, h2t_ready, p_done, p_free, prow_ready = (
            sem("g_done"), sem("h2t_ready"), sem("p_done"), sem("p_free"), sem("prow_ready"))
        prow_stored = [sem(f"prow_stored{p}") for p in (0, 1)]
        chain_sem = sem("chain")

        def tiles_v(ap):
            return ap.rearrange("(t p) c -> t p c", p=TN)

        h0_v, x_v, x1_v, tab_v = tiles_v(dram["h0"]), tiles_v(t["x"]), tiles_v(dram["x1"]), tiles_v(dram["tab1"])

        def one(ap, i):
            return ap[bass.ds(i, 1)].rearrange("a p c -> (a p) c")

        def bodies(eng, body):
            first, last = 4, NT - 2
            for i in range(first):
                body(i, i % 2)
            with eng.Fori(0, (last - first) // 2) as pair:
                for k in range(2):
                    body(2 * pair + (first + k), k)
            for i in range(last, NT + 4):
                body(i, i % 2)

        def has(i, back, ahead=0):
            return not isinstance(i, int) or 0 <= i + ahead - back < NT

        block = ctx.enter_context(nc.Block())

        @block.sync
        def _(sp):
            sp.dma_start(w2e[:], t["L0_gnn_ee_w2"].rearrange("(k p) n -> p k n", p=P)).then_inc(ld, 16)
            sp.dma_start(waug[:, :, 0:D], t["L1_gnn_W"].rearrange("(k p) n -> p k n", p=P)).then_inc(ld, 16)
            sp.dma_start(wt, t["L1_gnn_W_t"].rearrange("(k p) n -> p k n", p=P)).then_inc(ld, 16)
            sp.dma_start(bcol[:], t["L1_gnn_b_cols"]).then_inc(ld, 16)
            sp.dma_start(eb1[:], t["L0_gnn_ee_b1_cols"]).then_inc(ld, 16)
            for n, c in cols.items():
                sp.dma_start(c[:], t[f"L0_gnn_{n}_cols"]).then_inc(ld, 16)
            for n, c in bc.items():
                sp.dma_start(c[:], t[f"L0_gnn_{n}"].partition_broadcast(TN)).then_inc(ld, 16)
            sp.dma_start(baug[:, 0:D], t["L1_gnn_b"].partition_broadcast(TN)).then_inc(ld, 16)

            def load_front(i, p):
                sp.dma_start(hf[:, p, :], one(h0_v, i)).then_inc(hf_ready[p], 16)

            load_front(0, 0)
            load_front(1, 1)
            sp.sem_inc(hx_free, 2)

            def body(i, p):
                if has(i, 0, 2):
                    sp.wait_ge(hf_free, 1)
                    sp.sem_inc(hf_free, -1)
                    load_front(i + 2, p)
                if has(i, 2):
                    sp.wait_ge(hx_free, 1)
                    sp.sem_inc(hx_free, -1)
                    sp.dma_start(hx[:, p, 0, :], one(h0_v, i - 2)).then_inc(hx_ready[p], 16)
                    sp.dma_start(hx[:, p, 1, :], one(x_v, i - 2)).then_inc(hx_ready[p], 16)
                if has(i, 3):
                    sp.wait_ge(x1_ready, 1)
                    sp.sem_inc(x1_ready, -1)
                    sp.dma_start(one(x1_v, i - 3), x1[:, 1 - p, :]).then_inc(x1_stored[1 - p], 16)
                if has(i, 4):
                    sp.wait_ge(prow_ready, 1)
                    sp.sem_inc(prow_ready, -1)
                    sp.dma_start(one(tab_v, i - 4), prow[:, p, 0:TW]).then_inc(prow_stored[p], 16)

            bodies(sp, body)
            for p in (0, 1):
                sp.wait_ge(x1_stored[p], 16)
                sp.wait_ge(prow_stored[p], 16)

        @block.gpsimd
        def _(pool):
            for old in stale:
                pool.sem_clear(old)
            pool.memset(zero[:], 0.0).then_inc(setup, 1)
            pool.memset(att, 0.0).then_inc(setup, 1)
            pool.wait_ge(setup, 2)
            pool.sem_inc(setup, -2)
            for h in range(HEADS):
                q = slice(HD * (h % 4), HD * (h % 4) + HD)
                for c, n in ((h, "L1_gnn_a_src"), (HEADS + h, "L1_gnn_a_trg")):
                    pool.dma_start(att[q, h // 4, c:c + 1], t[n][0, h, :].unsqueeze(1)).then_inc(ld_act, 16)

            def turnable(i, p):
                pool.tensor_copy(rr[:, p, :], acc[0:TN, bass.ds(i, 1), D:2 * D].rearrange("p a c -> p (a c)")).then_inc(rr_ready, 1)

            pool.sem_inc(rr_free, 1)
            turnable(0, 0)

            def body(i, p):
                if has(i, 0, 1):
                    pool.wait_ge(rr_free, 1)
                    pool.sem_inc(rr_free, -1)
                    turnable(i + 1, 1 - p)
                if has(i, 3):
                    pool.wait_ge(hx_ready[1 - p], 32)
                    pool.sem_inc(hx_ready[1 - p], -32)
                    pool.tensor_tensor(hx[:, 1 - p, 0, :], hx[:, 1 - p, 0, :], bc["b3"][:], ALU.add).then_inc(hb_ready, 1)
                for j, back in ((0, 0), (1, 1)):
                    if has(i, back):
                        pool.wait_ge(a_ready[j], 1)
                        pool.sem_inc(a_ready[j], -1)
                        pool.tensor_copy(ah[j][:, p if j == 0 else 0], a[:]).then_inc(ah_ready[j], 1)
                if has(i, 0):
                    pool.wait_ge(acc_free, 1)
                    pool.sem_inc(acc_free, -1)
                    pool.tensor_copy(acc[0:TN, bass.ds(i, 1), 0:TW].rearrange("p a c -> p (a c)"), zero[0:TN, :].broadcast_to([TN, TW]))

            pool.wait_ge(ready, 1)
            bodies(pool, body)

        @block.tensor
        def _(pe):
            pe.wait_ge(ld, 16 * (6 + len(cols) + len(bc)))
            pe.wait_ge(ld_act, 16 * 2 * HEADS)
            pe.wait_ge(setup_done, 1)
            pe.sem_inc(setup_done, -1)
            for j in range(KD):
                for k in range(KD):
                    pe.matmul(t_ps[:, 0, 2 * HEADS * j:2 * HEADS * (j + 1)], wt[:, k, j * P:(j + 1) * P], att[:, k, :],
                              start=(k == 0), stop=(k == KD - 1))
            for k in range(KD):
                pe.matmul(p_ps[:, 0:2 * HEADS], bcb[:, k, :], att[:, k, :], start=(k == 0), stop=(k == KD - 1))
            pe.matmul(y_ps[:, 0:KH], ones[:], cols["b1"][:], start=True, stop=True)
            pe.matmul(y_ps[:, KH:2 * KH], ones[:], cols["b2"][:], start=True, stop=True).then_inc(setup_ps, 1)

            def turn(i, p):
                pe.wait_ge(rr_ready, 1)
                pe.sem_inc(rr_ready, -1)
                for k in range(KD):
                    ins = pe.transpose(t_ps[:, k, :], rr[:, p, k * P:(k + 1) * P], ident[0:TN, 0:TN])
                ins.then_inc(t_done, 1)

            def products(out, hi, lo, whi, wlo, n, start, stop, sem_, rows=False):
                ins = None
                for k in range(n):
                    for q, (x_, w_) in enumerate(((hi, whi), (lo, whi), (hi, wlo))):
                        lhs, rhs = (x_(k), w_(k)) if rows else (w_(k), x_(k))
                        ins = pe.matmul(out, lhs, rhs, start=(k == 0 and q == 0), stop=(k == n - 1 and q == 2))
                return ins

            def hidden(j, half, n, hi, lo, whi, wlo):
                for b in range(4):
                    f = slice((4 * half + b) * P, (4 * half + b + 1) * P)
                    out = z_ps[j][:, half, b * TN:(b + 1) * TN]
                    ins = products(out, hi, lo, lambda k: whi[:, k, f], lambda k: wlo[:, k, f], n, True, True, None)
                ins.then_inc(z_done[j], 1)

            def layer2(half, p):
                hidden(1, half, KH, lambda k: ah[0][:, p, k, :], lambda k: al[0][:, p, k, :], sb["w2h"], sb["w2l"])

            def variance(j):
                pe.wait_ge(ssq_ready[j], 1)
                pe.sem_inc(ssq_ready[j], -1)
                pe.matmul(v_ps[j], ones[:], ssq[j][:], start=True, stop=True).then_inc(var_done[j], 1)

            pe.wait_ge(ready, 1)
            turn(0, 0)
            pe.sem_inc(y_free, 1)
            pe.sem_inc(p_free, 1)

            def body(i, p):
                if has(i, 0):
                    pe.wait_ge(rt_ready, 1)
                    pe.sem_inc(rt_ready, -1)
                    pe.sem_inc(rr_free, 1)
                    pe.wait_ge(u_ready, 1)
                    pe.sem_inc(u_ready, -1)
                    for j in range(KD):
                        f = slice(j * P, (j + 1) * P)
                        for k in range(KD):
                            pe.matmul(h_ps[:, j, :], w2e[:, k, f], rt[:, k, :], start=(k == 0), stop=False)
                        ins = pe.matmul(h_ps[:, j, :], u[:, p, f], ident[0:TN, 0:TN], start=False, stop=True)
                    ins.then_inc(h_done, 1)
                if has(i, 4):
                    pe.wait_ge(h2_ready, 1)
                    pe.sem_inc(h2_ready, -1)
                    pe.wait_ge(p_free, 1)
                    pe.sem_inc(p_free, -1)
                    for k in range(KD):
                        ins = pe.transpose(g_ps[:, k, :], h2[:, k * P:(k + 1) * P], ident[0:TN, 0:TN])
                    ins.then_inc(g_done, 1)
                if has(i, 0):
                    pe.wait_ge(h_split, 1)
                    pe.sem_inc(h_split, -1)
                    if has(i, 0, 1):
                        turn(i + 1, 1 - p)
                    for half in range(2):
                        hidden(0, half, KD, lambda k: hh[:, k, :], lambda k: hl[:, k, :], sb["w1h"], sb["w1l"])
                if has(i, 1):
                    pe.wait_ge(a_split[0], 1)
                    pe.sem_inc(a_split[0], -1)
                    layer2(0, 1 - p)
                if has(i, 0):
                    variance(0)
                if has(i, 1):
                    layer2(1, 1 - p)
                if has(i, 4):
                    pe.wait_ge(h2t_ready, 1)
                    pe.sem_inc(h2t_ready, -1)
                    for k in range(KD):
                        ins = pe.matmul(p_ps, h2t[:, k, :], waug[:, k, :], start=(k == 0), stop=(k == KD - 1))
                    ins.then_inc(p_done, 1)
                if has(i, 2):
                    pe.wait_ge(a_split[1], 1)
                    pe.sem_inc(a_split[1], -1)
                    pe.wait_ge(y_free, 1)
                    pe.sem_inc(y_free, -1)
                    products(y_ps[0:TN, 0:D], lambda k: ah[1][:, 0, k, :], lambda k: al[1][:, 0, k, :],
                             lambda k: sb["w3h"][:, k, :], lambda k: sb["w3l"][:, k, :], KH, True, True, None,
                             rows=True).then_inc(y_done, 1)
                if has(i, 1):
                    variance(1)

            bodies(pe, body)

        @block.scalar
        def _(act):
            act.wait_ge(ready, 1)

            def turned(i):
                act.wait_ge(t_done, 1)
                act.sem_inc(t_done, -1)
                for k in range(KD):
                    ins = act.activation(rt[:, k, :], t_ps[:, k, :], ACT.Identity, bias=eb1[:, k:k + 1])
                ins.then_inc(rt_ready, 1)

            def biased(j, b):
                for half in range(2):
                    act.wait_ge(z_done[j], 1)
                    act.sem_inc(z_done[j], -1)
                    for k in range(4 * half, 4 * half + 4):
                        ins = act.activation(z[j][:, k, :], z_ps[j][:, half, (k % 4) * TN:(k % 4 + 1) * TN], ACT.Identity,
                                             bias=cols[b][:, k:k + 1], scale=(1.0, 1.0 / WS)[j])
                ins.then_inc(z_ready[j], 1)

            def deviation(j):
                act.wait_ge(var_done[j], 1)
                act.sem_inc(var_done[j], -1)
                act.activation(sd[j][:], v_ps[j], ACT.Sqrt, bias=lneps[:]).then_inc(sd_ready[j], 1)

            def activated(j, g, be):
                act.wait_ge(zn_ready[j], 1)
                act.sem_inc(zn_ready[j], -1)
                for k in range(KH):
                    ins = act.activation(a[:, k, :], z[j][:, k, :], ACT.Relu, bias=cols[be][:, k:k + 1], scale=cols[g][:, k:k + 1])
                ins.then_inc(a_ready[j], 1)

            def row_deviation(j):
                act.wait_ge(row_var[j], 1)
                act.sem_inc(row_var[j], -1)
                act.activation(co3[:, j, 0:1], mv3[:, j, 1:2], ACT.Sqrt, bias=lneps[0:TN, :]).then_inc(row_sd[j], 1)

            turned(0)

            def body(i, p):
                if has(i, 0):
                    act.wait_ge(h_done, 1)
                    act.sem_inc(h_done, -1)
                    act.activation(hh[:], h_ps[:], ACT.Copy, scale=1.0 / WS).then_inc(hh_ready, 1)
                if has(i, 0, 1):
                    turned(i + 1)
                if has(i, 3):
                    row_deviation(0)
                if has(i, 0):
                    biased(0, "b1")
                if has(i, 4):
                    act.wait_ge(g_done, 1)
                    act.sem_inc(g_done, -1)
                    act.activation(h2t[:], g_ps, ACT.Copy).then_inc(h2t_ready, 1)
                if has(i, 3):
                    act.wait_ge(row_coef[0], 1)
                    act.sem_inc(row_coef[0], -1)
                    act.activation(o[:], o[:], ACT.Identity, bias=co3[:, 0, 2:3], scale=co3[:, 0, 1:2]).then_inc(on_ready, 1)
                if has(i, 0):
                    deviation(0)
                if has(i, 3):
                    row_deviation(1)
                if has(i, 0):
                    activated(0, "g1", "be1")
                if has(i, 3):
                    act.wait_ge(row_coef[1], 1)
                    act.sem_inc(row_coef[1], -1)
                    act.activation(h2[:], x1[:, 1 - p, :], ACT.Relu, bias=co3[:, 1, 2:3], scale=co3[:, 1, 1:2]).then_inc(h2_ready, 1)
                if has(i, 1):
                    biased(1, "b2")
                    deviation(1)
                    activated(1, "g2", "be2")

            bodies(act, body)

        @block.vector
        def _(dve):
            dve.wait_ge(ld, 16 * (6 + len(cols) + len(bc)))
            dve.memset(ones[:], 1.0 / H).then_inc(chain_sem, 1)
            dve.wait_ge(chain_sem, 1)
            dve.sem_inc(chain_sem, -1)
            dve.tensor_scalar(eb1[:], eb1[:], 0.0, None, ALU.max).then_inc(chain_sem, 1)
            dve.wait_ge(chain_sem, 1)
            dve.sem_inc(chain_sem, -1)
            dve.tensor_copy(bcb, bcol[:].unsqueeze(2).broadcast_to([P, KD, TN])).then_inc(chain_sem, 1)
            dve.wait_ge(chain_sem, 1)
            dve.sem_inc(chain_sem, -1)
            dve.sem_inc(setup_done, 1)
            dve.wait_ge(setup_ps, 1)
            dve.sem_inc(setup_ps, -1)
            for j in range(KD):
                dve.tensor_copy(waug[:, j, D:AW], t_ps[:, 0, 2 * HEADS * j:2 * HEADS * (j + 1)]).then_inc(chain_sem, 1)
                dve.wait_ge(chain_sem, 1)
                dve.sem_inc(chain_sem, -1)
            dve.tensor_copy(baug[:, D:AW], p_ps[:, 0:2 * HEADS]).then_inc(chain_sem, 1)
            dve.wait_ge(chain_sem, 1)
            dve.sem_inc(chain_sem, -1)
            for j, n in ((0, "b1"), (1, "b2")):
                dve.tensor_reduce(csum[:, j:j + 1], y_ps[:, KH * j:KH * (j + 1)], AX, ALU.add).then_inc(chain_sem, 1)
                dve.wait_ge(chain_sem, 1)
                dve.sem_inc(chain_sem, -1)
                dve.tensor_scalar(cols[n][:], cols[n][:], csum[:, j:j + 1], None, ALU.subtract).then_inc(chain_sem, 1)
                dve.wait_ge(chain_sem, 1)
                dve.sem_inc(chain_sem, -1)
            dve.sem_inc(ready, 1)
            dve.sem_inc(x1_stored[0], 16)
            dve.sem_inc(x1_stored[1], 16)
            dve.sem_inc(prow_stored[0], 16)
            dve.sem_inc(prow_stored[1], 16)

            def front(i, p):
                dve.wait_ge(hf_ready[p], 16)
                dve.sem_inc(hf_ready[p], -16)
                dve.scalar_tensor_tensor(out=u[:, p, :], in0=hf[:, p, :], scalar=epscol[0:TN, :], in1=bc["ee_b2"][:],
                                         op0=ALU.mult, op1=ALU.add).then_inc(chain_sem, 1)
                dve.wait_ge(chain_sem, 1)
                dve.sem_inc(chain_sem, -1)
                dve.sem_inc(hf_free, 1)
                dve.tensor_tensor(u[:, p, :], u[:, p, :], acc[0:TN, bass.ds(i, 1), 0:D].rearrange("p a c -> p (a c)"), ALU.add).then_inc(chain_sem, 1)
                dve.wait_ge(chain_sem, 1)
                dve.sem_inc(chain_sem, -1)
                dve.sem_inc(u_ready, 1)
                dve.sem_inc(acc_free, 1)

            def squares(j):
                dve.wait_ge(z_ready[j], 1)
                dve.sem_inc(z_ready[j], -1)
                dve.tensor_tensor(a[:], z[j][:], z[j][:], ALU.mult).then_inc(chain_sem, 1)
                dve.wait_ge(chain_sem, 1)
                dve.sem_inc(chain_sem, -1)
                dve.tensor_reduce(ssq[j][:], a[:].rearrange("p k n -> p n k"), AX, ALU.add).then_inc(ssq_ready[j], 1)

            def scaled(j):
                dve.wait_ge(sd_ready[j], 1)
                dve.sem_inc(sd_ready[j], -1)
                dve.reciprocal(sd[j][:], sd[j][:]).then_inc(chain_sem, 1)
                dve.wait_ge(chain_sem, 1)
                dve.sem_inc(chain_sem, -1)
                dve.tensor_tensor(z[j][:], z[j][:], sd[j][:].unsqueeze(1).broadcast_to([P, KH, TN]), ALU.mult).then_inc(zn_ready[j], 1)

            def low(j, slot):
                dve.wait_ge(ah_ready[j], 1)
                dve.sem_inc(ah_ready[j], -1)
                dve.tensor_tensor(al[j][:, slot], a[:], ah[j][:, slot], ALU.subtract).then_inc(chain_sem, 1)
                dve.wait_ge(chain_sem, 1)
                dve.sem_inc(chain_sem, -1)
                dve.sem_inc(a_split[j], 1)

            def row_stats(j, src):
                dve.bn_stats(st3[:, j, :], src).then_inc(chain_sem, 1)
                dve.wait_ge(chain_sem, 1)
                dve.sem_inc(chain_sem, -1)
                dve.bn_aggr(mv3[:, j, :], st3[:, j, :]).then_inc(row_var[j], 1)

            def row_coefs(j):
                dve.wait_ge(row_sd[j], 1)
                dve.sem_inc(row_sd[j], -1)
                dve.reciprocal(co3[:, j, 1:2], co3[:, j, 0:1]).then_inc(chain_sem, 1)
                dve.wait_ge(chain_sem, 1)
                dve.sem_inc(chain_sem, -1)
                dve.scalar_tensor_tensor(out=co3[:, j, 2:3], in0=mv3[:, j, 0:1], scalar=-1.0, in1=co3[:, j, 1:2],
                                         op0=ALU.mult, op1=ALU.mult).then_inc(row_coef[j], 1)

            front(0, 0)

            def body(i, p):
                q = 1 - p
                if has(i, 0, 1):
                    front(i + 1, q)
                if has(i, 3):
                    dve.wait_ge(y_done, 1)
                    dve.sem_inc(y_done, -1)
                    dve.wait_ge(hb_ready, 1)
                    dve.sem_inc(hb_ready, -1)
                    dve.scalar_tensor_tensor(out=o[:], in0=y_ps[0:TN, 0:D], scalar=1.0 / WS, in1=hx[:, q, 0, :],
                                             op0=ALU.mult, op1=ALU.add).then_inc(chain_sem, 1)
                    dve.wait_ge(chain_sem, 1)
                    dve.sem_inc(chain_sem, -1)
                    dve.sem_inc(y_free, 1)
                    row_stats(0, o[:])
                if has(i, 0):
                    dve.wait_ge(hh_ready, 1)
                    dve.sem_inc(hh_ready, -1)
                    dve.scalar_tensor_tensor(out=hl[:], in0=h_ps[:], scalar=1.0 / WS, in1=hh[:],
                                             op0=ALU.mult, op1=ALU.subtract).then_inc(h_split, 1)
                if has(i, 3):
                    row_coefs(0)
                if has(i, 0):
                    squares(0)
                if has(i, 3):
                    dve.wait_ge(on_ready, 1)
                    dve.sem_inc(on_ready, -1)
                    dve.tensor_tensor(o[:], o[:], bc["bn_g"][:], ALU.mult).then_inc(chain_sem, 1)
                    dve.wait_ge(chain_sem, 1)
                    dve.sem_inc(chain_sem, -1)
                    dve.tensor_tensor(o[:], o[:], bc["bn_b"][:], ALU.add).then_inc(chain_sem, 1)
                    dve.wait_ge(chain_sem, 1)
                    dve.sem_inc(chain_sem, -1)
                    dve.wait_ge(x1_stored[q], 16)
                    dve.sem_inc(x1_stored[q], -16)
                    dve.scalar_tensor_tensor(out=x1[:, q, :], in0=o[:], scalar=0.0, in1=hx[:, q, 1, :],
                                             op0=ALU.max, op1=ALU.add).then_inc(chain_sem, 1)
                    dve.wait_ge(chain_sem, 1)
                    dve.sem_inc(chain_sem, -1)
                    dve.sem_inc(x1_ready, 1)
                    dve.sem_inc(hx_free, 1)
                    row_stats(1, x1[:, q, :])
                if has(i, 0):
                    scaled(0)
                if has(i, 3):
                    row_coefs(1)
                if has(i, 0):
                    low(0, p)
                if has(i, 1):
                    squares(1)
                if has(i, 4):
                    dve.wait_ge(p_done, 1)
                    dve.sem_inc(p_done, -1)
                    dve.wait_ge(prow_stored[p], 16)
                    dve.sem_inc(prow_stored[p], -16)
                    dve.tensor_tensor(prow[:, p, :], p_ps, baug[:], ALU.add).then_inc(chain_sem, 1)
                    dve.wait_ge(chain_sem, 1)
                    dve.sem_inc(chain_sem, -1)
                    dve.sem_inc(p_free, 1)
                    dve.sem_inc(prow_ready, 1)
                    dve.tensor_copy(sb["st"][0:TN, bass.ds(i - 4, 1), :].rearrange("p a c -> p (a c)"), prow[:, p, D:AW])
                if has(i, 1):
                    scaled(1)
                    low(1, 0)

            bodies(dve, body)


def split3(dve, chain_sem, x, parts, rest):
    dve.tensor_copy(parts[0], x).then_inc(chain_sem, 1)
    dve.wait_ge(chain_sem, 1)
    dve.sem_inc(chain_sem, -1)
    dve.tensor_tensor(rest, x, parts[0], ALU.subtract).then_inc(chain_sem, 1)
    dve.wait_ge(chain_sem, 1)
    dve.sem_inc(chain_sem, -1)
    dve.tensor_copy(parts[1], rest).then_inc(chain_sem, 1)
    dve.wait_ge(chain_sem, 1)
    dve.sem_inc(chain_sem, -1)
    dve.tensor_tensor(parts[2], rest, parts[1], ALU.subtract).then_inc(chain_sem, 1)
    dve.wait_ge(chain_sem, 1)
    dve.sem_inc(chain_sem, -1)


def leaky(dve, out, x):
    return dve.scalar_tensor_tensor(out=out, in0=x, scalar=SLOPE, in1=x, op0=ALU.mult, op1=ALU.max)


def edges1(nc, t, dram, sb, keep):
    smax = keep.sb("smax", [P, HEADS], F32)
    maxima = keep.sb("maxima", [P, CB, HEADS], F32)
    with ExitStack() as ctx:
        m = Memory(nc, ctx)
        acc, iota16, negbase, nodeid, ident, st = (
            sb["acc"], sb["iota16"], sb["negbase"], sb["nodeid"], sb["ident"], sb["st"])
        srcs = m.sb("a_srcs", [P, NCH], I32)
        dsts = m.sb("a_dsts", [P, NCH + CB], F32)
        far = m.sb("far", [P, NCH + CB], F32)
        idx = m.sb("a_idx", [P, RING, CB], I32)
        table = m.sb("table1", [1, 2, NBP + 4], I32)
        dstb = m.sb("dstb", [P, 2, BE], I32)
        trg = m.sb("trg", [TN, 3, NT, HEADS], BF16)
        rest = m.sb("rest", [TN, NT, HEADS], F32)
        rows = m.sb("a_rows", [P, RING, CB, TW], F32)
        hot_t = m.sb("hot_t", [TN, 3, BE], BF16)
        hot = m.sb("a_hot", [P, 3, CB, TN], F32)
        ht = m.sb("ht", [P, 2, CB, HEADS], F32)
        e = m.sb("e", [P, CB, HEADS], F32)
        c = m.sb("c", [P, CB, HEADS], F32)
        d = m.sb("d", [P, 2, CB, HEADS], F32)
        feat = m.sb("feat", [P, 2, CB, TW], F32)
        part = m.sb("part", [TN, HEADS], F32)
        smax_col = m.sb("smax_col", [HEADS, 1], F32)
        diag = m.sb("diag", [HEADS, HEADS], F32)
        ones = m.sb("a_ones", [HEADS, P], F32)
        ht_ps = [m.ps(f"ht{s}_ps", [P, CB, HEADS]) for s in range(3)]
        sum_ps = [m.ps(f"sum{s}_ps", [TN, TW]) for s in range(3)]

        ld_idx, ld_dst, ld_tab = m.sem("a_ld_idx"), m.sem("a_ld_dst"), m.sem("a_ld_tab")
        smax_in, smax_turned = m.sem("smax_in"), m.sem("smax_turned")
        diag_ready, smax_done = m.sem("diag_ready"), m.sem("smax_done")
        idx_ready = [m.sem(f"a_idx_ready{s}") for s in range(RING)]
        rows_ready = [m.sem(f"a_rows_ready{s}") for s in range(RING)]
        dstb_ready = [m.sem(f"dstb_ready{s}") for s in range(2)]
        dstb_free = m.sem("dstb_free")
        hot_t_ready = m.sem("hot_t_ready")
        ht_done = m.sem("ht_done")
        xhot_t_ready = m.sem("xhot_t_ready")
        xht_done = m.sem("xht_done")
        d_ready = m.sem("d_ready")
        p_ready = m.sem("p_ready")
        feat_ready = m.sem("feat_ready")
        sum_done = m.sem("a_sum_done")
        xhot_ready = m.sem("a_xhot_ready")
        xsum_done = m.sem("a_xsum_done")
        chain_sem = m.sem("a_chain")

        block = ctx.enter_context(nc.Block())

        @block.sync
        def _(sp):
            sp.dma_start(srcs[:], t["src_cols"]).then_inc(ld_idx, 16)
            sp.dma_start(table[:, :, 0:NBP + 1], dram["sched"][:, 0:NBP + 1].unsqueeze(0)).then_inc(ld_tab, 16)
            dst_rows = t["dst_flat"].rearrange("(b e) -> b e", e=BE)

            def load(b, s):
                sp.dma_start(dstb[:, s, :], dst_rows[bass.ds(b, 1)].broadcast_to([P, BE])).then_inc(dstb_ready[s], 16)

            load(0, 0)
            load(1, 1)
            with sp.Fori(0, NB // 2) as i:
                for u in range(2):
                    sp.wait_ge(dstb_free, 1)
                    sp.sem_inc(dstb_free, -1)
                    load(2 * i + u + 2, u)

        @block.gpsimd
        def _(pool):
            pool.dma_start(dsts[:], t["dst_cols"]).then_inc(ld_dst, 16)
            with pool.Fori(0, NB // RING):
                for s in range(RING):
                    pool.wait_ge(idx_ready[s], 1)
                    pool.sem_inc(idx_ready[s], -1)
                    for k in range(CB):
                        pool.indirect_dma_start(
                            rows[:, s, k, :], None, dram["tab1"],
                            bass.IndirectOffsetOnAxis(ap=idx[:, s, k:k + 1], axis=0),
                        ).then_inc(rows_ready[s], 16)

        @block.scalar
        def _(act):
            with act.Fori(0, NB // 2):
                for s in range(2):
                    act.wait_ge(d_ready, 1)
                    act.sem_inc(d_ready, -1)
                    act.activation(feat[:, s, :, D:TW], d[:, s], ACT.Exp).then_inc(p_ready, 1)

        @block.tensor
        def _(pe):
            def targets(out, h, tile):
                for k in range(CB):
                    lhs = hot_t[:, h, k * P:(k + 1) * P]
                    for q in range(3):
                        ins = pe.matmul(out[:, k, :], lhs, trg[:, q, bass.ds(tile, 1), :].rearrange("p a c -> p (a c)"),
                                        start=(q == 0), stop=(q == 2))
                return ins

            def block_targets(s, lo, end):
                pe.wait_ge(hot_t_ready, 1)
                pe.sem_inc(hot_t_ready, -1)
                targets(ht_ps[s], s, lo).then_inc(ht_done, 1)
                with pe.If(end > lo + 1):
                    with pe.Fori(lo + 1, end) as x:
                        pe.wait_ge(xhot_t_ready, 1)
                        pe.sem_inc(xhot_t_ready, -1)
                        targets(ht_ps[2], 2, x).then_inc(xht_done, 1)

            def sums(out, h, s):
                for k in range(CB):
                    ins = pe.matmul(out[:], hot[:, h, k, :], feat[:, s, k, :], start=(k == 0), stop=(k == CB - 1))
                return ins

            def other_sums(s, lo, end):
                with pe.If(end > lo + 1):
                    with pe.Fori(lo + 1, end):
                        pe.wait_ge(xhot_ready, 1)
                        pe.sem_inc(xhot_ready, -1)
                        sums(sum_ps[2], 2, s).then_inc(xsum_done, 1)

            pe.wait_ge(smax_in, 1)
            pe.sem_inc(smax_in, -1)
            pe.transpose(sum_ps[0][0:HEADS, 0:TN], part[:], ident[0:TN, 0:TN]).then_inc(smax_turned, 1)
            pe.wait_ge(diag_ready, 1)
            pe.sem_inc(diag_ready, -1)
            pe.matmul(ht_ps[0][:, 0, :], ones[:], diag[:], start=True, stop=True).then_inc(smax_done, 1)
            pe.wait_ge(ld_tab, 16)
            block_targets(0, *tiles_of(nc, PE, table, 0, 1)[0])
            with pe.Fori(0, NB // RING) as i:
                tiles = tiles_of(nc, PE, table, RING * i - 1, RING + 2)
                for u in range(RING):
                    s = u % 2
                    block_targets(1 - s, *tiles[u + 2])
                    if u:
                        other_sums(1 - s, *tiles[u])
                    else:
                        with pe.If(i > 0):
                            other_sums(1 - s, *tiles[u])
                    pe.wait_ge(feat_ready, 1)
                    pe.sem_inc(feat_ready, -1)
                    sums(sum_ps[s], s, s).then_inc(sum_done, 1)
            other_sums((NB - 1) % 2, *tiles_of(nc, PE, table, NB - 1, 1)[0])

        @block.vector
        def _(dve):
            def node_hot(slot, s, tile):
                return dve.tensor_scalar(hot_t[:, slot, :], dstb[0:TN, s, :], nodeid[0:TN, bass.ds(tile, 1)], None, ALU.is_equal)

            def targets(b, s, lo, end):
                dve.wait_ge(ht_done, 1)
                dve.sem_inc(ht_done, -1)
                fars = far[:, bass.ds(CB * (b + 1), CB)].unsqueeze(2).broadcast_to([P, CB, HEADS])
                dve.tensor_tensor(ht[:, s], ht_ps[s][:], fars, ALU.add).then_inc(chain_sem, 1)
                dve.wait_ge(chain_sem, 1)
                dve.sem_inc(chain_sem, -1)
                with dve.If(end > lo + 1):
                    with dve.Fori(lo + 1, end) as x:
                        node_hot(2, s, x).then_inc(xhot_t_ready, 1)
                        dve.wait_ge(xht_done, 1)
                        dve.sem_inc(xht_done, -1)
                        dve.tensor_tensor(ht[:, s], ht[:, s], ht_ps[2][:], ALU.add).then_inc(chain_sem, 1)
                        dve.wait_ge(chain_sem, 1)
                        dve.sem_inc(chain_sem, -1)
                dve.sem_inc(dstb_free, 1)

            def logits(i, u, s):
                dve.wait_ge(rows_ready[u], 16 * CB * (i + 1))
                dve.tensor_tensor(e[:], rows[:, u, :, D:TW], ht[:, s], ALU.add)
                dve.tensor_tensor(c[:], ht[:, s], smax[:].unsqueeze(1).broadcast_to([P, CB, HEADS]), ALU.add).then_inc(chain_sem, 1)
                dve.wait_ge(chain_sem, 1)
                dve.sem_inc(chain_sem, -1)
                leaky(dve, e[:], e[:])
                leaky(dve, c[:], c[:]).then_inc(chain_sem, 1)
                dve.wait_ge(chain_sem, 1)
                dve.sem_inc(chain_sem, -1)
                dve.tensor_tensor(d[:, s], e[:], c[:], ALU.subtract).then_inc(d_ready, 1)
                dve.tensor_tensor(maxima[:], maxima[:], e[:], ALU.max).then_inc(chain_sem, 1)

            def weighted(u, s):
                dve.wait_ge(p_ready, 1)
                dve.sem_inc(p_ready, -1)
                p = feat[:, s, :, D:TW].unsqueeze(3).broadcast_to([P, CB, HEADS, HD])
                dve.tensor_tensor(feat[:, s, :, 0:D].rearrange("p k (h f) -> p k h f", h=HEADS),
                                  rows[:, u, :, 0:D].rearrange("p k (h f) -> p k h f", h=HEADS), p, ALU.mult).then_inc(feat_ready, 1)

            def add(slot, tile):
                a = acc[0:TN, bass.ds(tile, 1), 0:TW].rearrange("p a c -> p (a c)")
                dve.tensor_tensor(a, a, sum_ps[slot][:], ALU.add).then_inc(chain_sem, 1)
                dve.wait_ge(chain_sem, 1)
                dve.sem_inc(chain_sem, -1)

            def finish_block(b, s, lo, end):
                dve.wait_ge(sum_done, 1)
                dve.sem_inc(sum_done, -1)
                add(s, lo)
                with dve.If(end > lo + 1):
                    with dve.Fori(lo + 1, end) as x:
                        one_hot(dve, hot[:, 2], iota16, dsts, negbase, b, x).then_inc(xhot_ready, 1)
                        dve.wait_ge(xsum_done, 1)
                        dve.sem_inc(xsum_done, -1)
                        add(2, x)

            def indices(b, s):
                dve.tensor_copy(idx[:, s, :], srcs[:, bass.ds(CB * b, CB)]).then_inc(idx_ready[s], 1)

            dve.wait_ge(ld_idx, 16)
            for b in range(RING):
                indices(b, b)
            dve.tensor_reduce(part[:], st[0:TN, :, 0:HEADS].rearrange("p t h -> p h t"), AX, ALU.max).then_inc(chain_sem, 1)
            dve.wait_ge(chain_sem, 1)
            dve.sem_inc(chain_sem, -1)
            dve.sem_inc(smax_in, 1)
            dve.memset(ones[:], 1.0).then_inc(chain_sem, 1)
            dve.wait_ge(chain_sem, 1)
            dve.sem_inc(chain_sem, -1)
            dve.memset(maxima[:], FAR).then_inc(chain_sem, 1)
            dve.wait_ge(chain_sem, 1)
            dve.sem_inc(chain_sem, -1)
            dve.wait_ge(smax_turned, 1)
            dve.sem_inc(smax_turned, -1)
            dve.tensor_reduce(smax_col[:], sum_ps[0][0:HEADS, 0:TN], AX, ALU.max).then_inc(chain_sem, 1)
            dve.wait_ge(chain_sem, 1)
            dve.sem_inc(chain_sem, -1)
            dve.tensor_scalar(diag[:], ident[0:HEADS, 0:HEADS], smax_col[:], None, ALU.mult).then_inc(chain_sem, 1)
            dve.wait_ge(chain_sem, 1)
            dve.sem_inc(chain_sem, -1)
            dve.sem_inc(diag_ready, 1)
            split3(dve, chain_sem, st[0:TN, :, HEADS:2 * HEADS], [trg[:, q] for q in range(3)], rest[:])
            dve.wait_ge(smax_done, 1)
            dve.sem_inc(smax_done, -1)
            dve.tensor_copy(smax[:], ht_ps[0][:, 0, :]).then_inc(chain_sem, 1)
            dve.wait_ge(chain_sem, 1)
            dve.sem_inc(chain_sem, -1)
            dve.wait_ge(ld_dst, 16)
            dve.wait_ge(ld_tab, 16)
            dve.tensor_scalar(far[:], dsts[:], float(N), FAR, ALU.is_ge, ALU.mult).then_inc(chain_sem, 1)
            dve.wait_ge(chain_sem, 1)
            dve.sem_inc(chain_sem, -1)
            lo, end = tiles_of(nc, DVE, table, 0, 1)[0]
            dve.wait_ge(dstb_ready[0], 16)
            dve.sem_inc(dstb_ready[0], -16)
            node_hot(0, 0, lo).then_inc(hot_t_ready, 1)
            targets(0, 0, lo, end)
            with dve.Fori(0, NB // RING) as i:
                tiles = tiles_of(nc, DVE, table, RING * i - 1, RING + 2)
                for u in range(RING):
                    b, s = RING * i + u, u % 2
                    dve.wait_ge(dstb_ready[1 - s], 16)
                    dve.sem_inc(dstb_ready[1 - s], -16)
                    node_hot(1 - s, 1 - s, tiles[u + 2][0]).then_inc(hot_t_ready, 1)
                    logits(i, u, s)
                    one_hot(dve, hot[:, s], iota16, dsts, negbase, b, tiles[u + 1][0])
                    dve.wait_ge(chain_sem, 1)
                    dve.sem_inc(chain_sem, -1)
                    targets(b + 1, 1 - s, *tiles[u + 2])
                    weighted(u, s)
                    if u:
                        finish_block(b - 1, 1 - s, *tiles[u])
                    else:
                        with dve.If(i > 0):
                            finish_block(b - 1, 1 - s, *tiles[u])
                    indices(b + RING, u)
            lo, end = tiles_of(nc, DVE, table, NB - 1, 1)[0]
            finish_block(NB - 1, (NB - 1) % 2, lo, end)
            dve.wait_ge(dstb_ready[(NB + 1) % 2], 16)
            dve.sem_inc(dstb_ready[(NB + 1) % 2], -16)
    return smax, maxima


def finish(nc, t, dram, sb, smax, maxima, out):
    with ExitStack() as ctx:
        m = Memory(nc, ctx)
        acc, ident, st = sb["acc"], sb["ident"], sb["st"]
        e = m.sb("f_e", [TN, NT, HEADS], F32)
        c = m.sb("f_c", [TN, NT, HEADS], F32)
        p = m.sb("f_p", [TN, NT, HEADS], F32)
        g = m.sb("f_g", [TN, NT, HEADS], F32)
        mx = m.sb("mx", [P, 2], F32)
        mrow = m.sb("mrow", [1, 1], F32)
        ones = m.sb("f_ones", [1, P], F32)
        top = m.sb("top", [P, 1], F32)
        FB = 5
        hp = m.sb("hp", [TN, 2, FB, D], F32)
        x1 = m.sb("f_x1", [TN, 2, FB, D], F32)
        turn_ps = m.ps("turn_ps", [1, P])
        top_ps = m.ps("top_ps", [P, 1])

        loaded = [m.sem(f"f_loaded{s}") for s in range(2)]
        out_ready = m.sem("out_ready")
        out_stored = [m.sem(f"out_stored{s}") for s in range(2)]
        mx_ready, turned, mrow_ready, top_done = m.sem("mx_ready"), m.sem("turned"), m.sem("mrow_ready"), m.sem("top_done")
        exp_in, exp_ready = m.sem("exp_in"), m.sem("exp_ready")
        coef_ready, self_ready = m.sem("f_coef_ready"), m.sem("self_ready")
        chain_sem = m.sem("f_chain")

        block = ctx.enter_context(nc.Block())

        @block.sync
        def _(sp):
            x1_v = dram["x1"].rearrange("(t p) c -> p t c", p=TN)
            hp_v = dram["tab1"].rearrange("(t p) c -> p t c", p=TN)
            out_v = out.rearrange("(t p) c -> p t c", p=TN)

            def load(i, s):
                sp.dma_start(hp[:, s], hp_v[:, bass.ds(i * FB, FB), 0:D]).then_inc(loaded[s], 16)
                sp.dma_start(x1[:, s], x1_v[:, bass.ds(i * FB, FB), :]).then_inc(loaded[s], 16)

            def store(i, s):
                sp.wait_ge(out_ready, 1)
                sp.sem_inc(out_ready, -1)
                sp.dma_start(out_v[:, bass.ds(i * FB, FB), :], acc[0:TN, bass.ds(i * FB, FB), 0:D]).then_inc(out_stored[s], 16)

            load(0, 0)
            load(1, 1)
            last = NT // FB // 2 - 1
            with sp.Fori(0, last) as i:
                for s in range(2):
                    store(2 * i + s, s)
                    load(2 * i + s + 2, s)
            for s in range(2):
                store(2 * last + s, s)
                sp.wait_ge(out_stored[s], 16 * (last + 1))

        @block.scalar
        def _(act):
            act.wait_ge(exp_in, 1)
            act.sem_inc(exp_in, -1)
            act.activation(p[:], e[:], ACT.Exp).then_inc(exp_ready, 1)
            act.wait_ge(exp_in, 1)
            act.sem_inc(exp_in, -1)
            act.activation(g[:], c[:], ACT.Exp).then_inc(exp_ready, 1)

        @block.tensor
        def _(pe):
            pe.wait_ge(mx_ready, 1)
            pe.sem_inc(mx_ready, -1)
            pe.transpose(turn_ps[:], mx[:, 0:1], ident[:]).then_inc(turned, 1)
            pe.wait_ge(mrow_ready, 1)
            pe.sem_inc(mrow_ready, -1)
            pe.matmul(top_ps[:], ones[:], mrow[:], start=True, stop=True).then_inc(top_done, 1)

        @block.gpsimd
        def _(pool):
            pool.wait_ge(coef_ready, 1)
            with pool.Fori(0, NT // FB // 2) as i:
                for s in range(2):
                    pool.wait_ge(loaded[s], 32)
                    pool.sem_inc(loaded[s], -32)
                    h = hp[:, s].rearrange("p t (h f) -> p t h f", h=HEADS)
                    pool.tensor_tensor(h, h, p[:, bass.ds((2 * i + s) * FB, FB), :].unsqueeze(3).broadcast_to([TN, FB, HEADS, HD]),
                                       ALU.mult).then_inc(self_ready, 1)

        @block.vector
        def _(dve):
            dve.memset(ones[:], 1.0).then_inc(chain_sem, 1)
            dve.wait_ge(chain_sem, 1)
            dve.sem_inc(chain_sem, -1)
            dve.tensor_tensor(e[:], st[0:TN, :, 0:HEADS], st[0:TN, :, HEADS:2 * HEADS], ALU.add).then_inc(chain_sem, 1)
            dve.wait_ge(chain_sem, 1)
            dve.sem_inc(chain_sem, -1)
            leaky(dve, e[:], e[:]).then_inc(chain_sem, 1)
            dve.wait_ge(chain_sem, 1)
            dve.sem_inc(chain_sem, -1)
            dve.tensor_tensor(c[:], st[0:TN, :, HEADS:2 * HEADS], smax[0:TN, :].unsqueeze(1).broadcast_to([TN, NT, HEADS]), ALU.add).then_inc(chain_sem, 1)
            dve.wait_ge(chain_sem, 1)
            dve.sem_inc(chain_sem, -1)
            leaky(dve, c[:], c[:]).then_inc(chain_sem, 1)
            dve.wait_ge(chain_sem, 1)
            dve.sem_inc(chain_sem, -1)
            dve.tensor_reduce(mx[:, 0:1], maxima[:].rearrange("p k h -> p (k h)"), AX, ALU.max).then_inc(chain_sem, 1)
            dve.wait_ge(chain_sem, 1)
            dve.sem_inc(chain_sem, -1)
            dve.tensor_reduce(mx[0:TN, 1:2], e[:].rearrange("p t h -> p (t h)"), AX, ALU.max).then_inc(chain_sem, 1)
            dve.wait_ge(chain_sem, 1)
            dve.sem_inc(chain_sem, -1)
            dve.tensor_tensor(mx[0:TN, 0:1], mx[0:TN, 0:1], mx[0:TN, 1:2], ALU.max).then_inc(chain_sem, 1)
            dve.wait_ge(chain_sem, 1)
            dve.sem_inc(chain_sem, -1)
            dve.sem_inc(mx_ready, 1)
            dve.tensor_tensor(e[:], e[:], c[:], ALU.subtract).then_inc(chain_sem, 1)
            dve.wait_ge(chain_sem, 1)
            dve.sem_inc(chain_sem, -1)
            dve.sem_inc(exp_in, 1)
            dve.wait_ge(turned, 1)
            dve.sem_inc(turned, -1)
            dve.tensor_reduce(mrow[:], turn_ps[:], AX, ALU.max).then_inc(mrow_ready, 1)
            dve.wait_ge(top_done, 1)
            dve.sem_inc(top_done, -1)
            dve.tensor_copy(top[:], top_ps[:]).then_inc(chain_sem, 1)
            dve.wait_ge(chain_sem, 1)
            dve.sem_inc(chain_sem, -1)
            dve.tensor_scalar(c[:], c[:], top[0:TN, :], -1.0, ALU.subtract, ALU.mult).then_inc(chain_sem, 1)
            dve.wait_ge(chain_sem, 1)
            dve.sem_inc(chain_sem, -1)
            dve.tensor_scalar(c[:], c[:], CAP, None, ALU.min).then_inc(chain_sem, 1)
            dve.wait_ge(chain_sem, 1)
            dve.sem_inc(chain_sem, -1)
            dve.sem_inc(exp_in, 1)
            dve.wait_ge(exp_ready, 2)
            dve.sem_inc(exp_ready, -2)
            dve.scalar_tensor_tensor(out=g[:], in0=g[:], scalar=GUARD, in1=p[:], op0=ALU.mult, op1=ALU.add).then_inc(chain_sem, 1)
            dve.wait_ge(chain_sem, 1)
            dve.sem_inc(chain_sem, -1)
            dve.tensor_tensor(g[:], g[:], acc[0:TN, :, D:TW], ALU.add).then_inc(chain_sem, 1)
            dve.wait_ge(chain_sem, 1)
            dve.sem_inc(chain_sem, -1)
            dve.reciprocal(g[:], g[:]).then_inc(chain_sem, 1)
            dve.wait_ge(chain_sem, 1)
            dve.sem_inc(chain_sem, -1)
            dve.tensor_tensor(p[:], p[:], g[:], ALU.mult).then_inc(chain_sem, 1)
            dve.wait_ge(chain_sem, 1)
            dve.sem_inc(chain_sem, -1)
            dve.sem_inc(coef_ready, 1)
            with dve.Fori(0, NT // FB // 2) as i:
                for s in range(2):
                    tiles = bass.ds((2 * i + s) * FB, FB)
                    a = acc[0:TN, tiles, 0:D]
                    a4 = a.rearrange("p t (h f) -> p t h f", h=HEADS)
                    dve.tensor_tensor(a4, a4, g[:, tiles, :].unsqueeze(3).broadcast_to([TN, FB, HEADS, HD]), ALU.mult).then_inc(chain_sem, 1)
                    dve.wait_ge(chain_sem, 1)
                    dve.sem_inc(chain_sem, -1)
                    dve.wait_ge(self_ready, 1)
                    dve.sem_inc(self_ready, -1)
                    dve.tensor_tensor(a, a, x1[:, s], ALU.add).then_inc(chain_sem, 1)
                    dve.wait_ge(chain_sem, 1)
                    dve.sem_inc(chain_sem, -1)
                    dve.tensor_tensor(a, a, hp[:, s], ALU.add).then_inc(out_ready, 1)


_PLAIN = ["x", "L0_gnn_eps", "L0_gnn_ee_w1", "L0_gnn_ee_b1", "L0_gnn_ee_w2", "L0_gnn_ee_b2", "L0_gnn_w1",
          "L0_gnn_w2", "L0_gnn_w3", "L0_gnn_b3", "L0_gnn_bn_g", "L0_gnn_bn_b", "L1_gnn_W", "L1_gnn_b",
          "L1_gnn_a_src", "L1_gnn_a_trg"]
_COLS = ["L0_gnn_b1", "L0_gnn_g1", "L0_gnn_be1", "L0_gnn_b2", "L0_gnn_g2", "L0_gnn_be2"]


def kernel(**inputs):
    import concourse.bacc as bacc
    import numpy as np
    from concourse.bass_utils import run_bass_kernel_spmd

    a = {n: np.ascontiguousarray(inputs[n]) for n in _PLAIN}
    a["L0_gnn_eps"] = a["L0_gnn_eps"].reshape(1)
    for n in _COLS:
        a[n + "_cols"] = np.ascontiguousarray(np.asarray(inputs[n]).reshape(KH, P).T)
    a["L0_gnn_ee_b1_cols"] = np.ascontiguousarray(np.asarray(inputs["L0_gnn_ee_b1"]).reshape(KD, P).T)
    a["L1_gnn_b_cols"] = np.ascontiguousarray(np.asarray(inputs["L1_gnn_b"]).reshape(KD, P).T)
    a["L1_gnn_W_t"] = np.ascontiguousarray(np.asarray(inputs["L1_gnn_W"]).T)
    pad = NBP * BE - E
    src = np.concatenate([np.asarray(inputs["src"]), np.zeros(pad, np.int32)])
    dst = np.concatenate([np.asarray(inputs["dst"]), np.full(pad, N, np.int32)])
    a["src_cols"] = np.ascontiguousarray(src.reshape(NCH, P).T)
    a["dst_cols"] = np.ascontiguousarray(np.concatenate([np.full(BE, N, np.int32), dst]).reshape(NCH + CB, P).T)
    a["dst_flat"] = dst
    ea = np.concatenate([np.asarray(inputs["edge_attr_64"]), np.zeros((pad, ED), np.float32)])
    a["edge_t"] = np.ascontiguousarray(ea.reshape(NBP, BE, ED).transpose(0, 2, 1))

    nc = bacc.Bacc("TRN2", target_bir_lowering=False, num_devices=1)
    t = {n: nc.dram_tensor(n, v.shape, mybir.dt.from_np(v.dtype), kind="ExternalInput").ap() for n, v in a.items()}
    out = nc.dram_tensor("out", (N, D), F32, kind="ExternalOutput").ap()
    build(nc, t, out)
    r = run_bass_kernel_spmd(nc, [a], core_ids=[0])
    return r.results[0]["out"]
```

```python
from contextlib import ExitStack

import concourse.bass as bass
from concourse import mybir

F32, F16, I32, I16 = mybir.dt.float32, mybir.dt.float16, mybir.dt.int32, mybir.dt.int16
BF16 = mybir.dt.bfloat16
ALU = mybir.AluOpType
ACT = mybir.ActivationFunctionType
AX = mybir.AxisListType.X
PE, DVE = mybir.EngineType.PE, mybir.EngineType.DVE

P = 128
N, D, E, ED, H = 6250, 256, 100000, 64, 1024
TN = 125
NT = N // TN
CB = 4
BE = CB * P
RING = 4
NB = -(-E // (BE * RING)) * RING
NBP = NB + RING
NCH = NBP * CB
KH, KD = H // P, D // P
HEADS, HD = 8, 32
TW = D + HEADS
AW = D + 2 * HEADS
LN_EPS = 1e-5
SLOPE = 0.2
GUARD = 1e-10
WS = 64.0
PG = 10
FAR = -1.0e30
CAP = 87.0


def build(nc, t, out):
    with ExitStack() as ctx:
        keep = Memory(nc, ctx)
        dram = {
            "h0": nc.dram_tensor("h0_scratch", (N, D), F32, kind="Internal").ap(),
            "tab0": nc.dram_tensor("tab0_scratch", (N, 2 * D), F16, kind="Internal").ap(),
            "tab1": nc.dram_tensor("tab1_scratch", (N, TW), F32, kind="Internal").ap(),
            "x1": nc.dram_tensor("x1_scratch", (N, D), F32, kind="Internal").ap(),
            "sched": nc.dram_tensor("sched_scratch", (2, NBP + 4), I32, kind="Internal").ap(),
        }
        sb = {}
        for name, shape, dt in [
            ("acc", [P, NT, 2 * D], F32),
            ("ident", [P, P], F32), ("iota16", [P, TN], F16),
            ("negbase", [P, NT], F32), ("nodeid", [P, NT], F32),
            ("st", [P, NT, 2 * HEADS], F32),
            ("epscol", [P, 1], F32), ("lneps", [P, 1], F32),
        ]:
            sb[name] = keep.sb(name, shape, dt)
        with ExitStack() as first:
            layer0 = Memory(nc, first)
            for name, shape, dt in [
                ("w1h", [P, KD, H], F16), ("w1l", [P, KD, H], F16),
                ("w2h", [P, KH, H], F16), ("w2l", [P, KH, H], F16),
                ("w3h", [P, KH, D], F16), ("w3l", [P, KH, D], F16),
            ]:
                sb[name] = layer0.sb(name, shape, dt)
            with ExitStack() as edge_mlp:
                for name, shape, dt in [("ewa", [P, D], F16), ("ewb", [ED + 2, D], F16)]:
                    sb[name] = Memory(nc, edge_mlp).sb(name, shape, dt)
                stale = prepare(nc, t, dram, sb)
                edges0(nc, t, dram, sb)
            nodes(nc, t, dram, sb, stale)
        smax, maxima = edges1(nc, t, dram, sb, keep)
        finish(nc, t, dram, sb, smax, maxima, out)


class Memory:

    def __init__(self, nc, ctx):
        self.nc, self.ctx, self.sems = nc, ctx, []

    def sb(self, name, shape, dt):
        return self.ctx.enter_context(self.nc.sbuf_tensor(name, shape, dt))

    def ps(self, name, shape, dt=F32):
        return self.ctx.enter_context(self.nc.psum_tensor(name, shape, dt))

    def sem(self, name):
        self.sems.append(self.ctx.enter_context(self.nc.semaphore(name)))
        return self.sems[-1]


def prepare(nc, t, dram, sb):
    with ExitStack() as ctx:
        m = Memory(nc, ctx)
        acc = sb["acc"]
        flat = acc[:].rearrange("p t c -> p (t c)")
        xall = flat[0:TN, 0:NT * D].rearrange("p (t c) -> p t c", c=D)
        o = NT * D
        w1r = flat[:, o:o + KD * H].rearrange("p (k n) -> p k n", n=H)
        w2r = flat[:, o + KD * H:o + (KD + KH) * H].rearrange("p (k n) -> p k n", n=H)
        o += (KD + KH) * H
        w3r = flat[:, o:o + KH * D].rearrange("p (k n) -> p k n", n=D)

        icol = m.sb("icol", [P, P], I32)
        idiag = m.sb("idiag", [P, P], I32)
        ineg = m.sb("ineg", [P, NT], I32)
        inode = m.sb("inode", [P, NT], I32)
        ithr = m.sb("ithr", [P, NT - 1], I32)
        thr = m.sb("thr", [P, NT - 1], F32)
        b2bc = m.sb("p_b2bc", [TN, D], F32)
        er = m.sb("er", [P, D], F32)
        ebr = m.sb("ebr", [ED + 2, D], F32)
        ebh = m.sb("ebh", [ED + 2, D], F16)
        stat = m.sb("stat", [TN, PG, 6], F32)
        mv = m.sb("mv", [TN, PG, 2], F32)
        sd = m.sb("sd", [TN, PG], F32)
        rstd = m.sb("rstd", [TN, PG], F32)
        nmr = m.sb("nmr", [TN, PG], F32)
        h0 = m.sb("h0", [TN, PG, D], F32)
        tb = m.sb("tb", [TN, PG, 2 * D], F16)
        wsum = m.sb("wsum", [P, KD + KH], F32)
        wneg = m.sb("wneg", [P, KD + KH], F32)
        half = NBP // 2
        drow = m.sb("drow", [half, 2, BE], I32)
        ext = m.sb("ext", [half, 4], F32)
        cmp_ = m.sb("cmp_", [half, 4, NT - 1], F32)
        tile = m.sb("tile", [half, 4], F32)
        sched_sb = m.sb("sched_sb", [half, 2, 2], I32)

        ld_x = [m.sem(f"ld_x{i}") for i in range(NT // PG)]
        ld_w = m.sem("ld_w")
        ld_small = m.sem("ld_small")
        ld_dst = m.sem("ld_dst")
        iotas = m.sem("iotas")
        eb_split = m.sem("eb_split")
        norm_in = m.sem("norm_in")
        var_ready = m.sem("var_ready")
        sd_ready = m.sem("sd_ready")
        coef_ready = m.sem("coef_ready")
        h0_ready = m.sem("h0_ready")
        t_ready = m.sem("t_ready")
        hi_ready = m.sem("hi_ready")
        tb_ready = m.sem("tb_ready")
        h0_stored = m.sem("h0_stored")
        tb_stored = m.sem("tb_stored")
        wsum_ready = m.sem("wsum_ready")
        wneg_ready = m.sem("wneg_ready")
        whi_ready = m.sem("whi_ready")
        act_chain = m.sem("p_act_chain")
        dve_chain = m.sem("p_dve_chain")
        sched_ready = m.sem("sched_ready")
        stored = m.sem("p_stored")
        ewb_done = m.sem("ewb_done")
        x_v = t["x"].rearrange("(p t) c -> p t c", t=NT)
        h0_v = dram["h0"].rearrange("(p t) c -> p t c", t=NT)
        tb_v = dram["tab0"].rearrange("(p t) c -> p t c", t=NT)
        splits = ([(w1r[:, k, :], sb["w1h"][:, k, :], sb["w1l"][:, k, :]) for k in range(KD)]
                  + [(w2r[:, k, :], sb["w2h"][:, k, :], sb["w2l"][:, k, :]) for k in range(KH)])
        w3s = (w3r[:, :, :], sb["w3h"][:, :, :], sb["w3l"][:, :, :])

        block = ctx.enter_context(nc.Block())

        @block.sync
        def _(sp):
            for i in range(NT // PG):
                sp.dma_start(xall[:, i * PG:(i + 1) * PG, :], x_v[:, i * PG:(i + 1) * PG, :]).then_inc(ld_x[i], 16)
            sp.dma_start(drow[:], t["dst_flat"].rearrange("(p j e) -> p j e", p=half, j=2)).then_inc(ld_dst, 16)
            sp.dma_start(w1r, t["L0_gnn_w1"].rearrange("(k p) n -> p k n", p=P)).then_inc(ld_w, 16)
            sp.dma_start(w2r, t["L0_gnn_w2"].rearrange("(k p) n -> p k n", p=P)).then_inc(ld_w, 16)
            sp.dma_start(w3r, t["L0_gnn_w3"].rearrange("(k p) n -> p k n", p=P)).then_inc(ld_w, 16)
            with sp.Fori(0, NT // PG) as i:
                sp.wait_ge(h0_ready, 1)
                sp.sem_inc(h0_ready, -1)
                sp.dma_start(h0_v[:, bass.ds(i * PG, PG), :], h0[:]).then_inc(h0_stored, 16)
                sp.wait_ge(tb_ready, 1)
                sp.sem_inc(tb_ready, -1)
                sp.dma_start(tb_v[:, bass.ds(i * PG, PG), :], tb[:]).then_inc(tb_stored, 16)
            sp.wait_ge(sched_ready, 1)
            sp.sem_inc(sched_ready, -1)
            for part in range(2):
                row = dram["sched"][part]
                sp.dma_start(row[1:NBP + 1].rearrange("(p j) -> p j", j=2), sched_sb[:, part, :]).then_inc(stored, 16)
                sp.dma_start(row[0:1].unsqueeze(0), sched_sb[0:1, part, 0:1]).then_inc(stored, 16)
            sp.wait_ge(stored, 64)
            sp.wait_ge(h0_stored, 16)
            sp.wait_ge(tb_stored, 16)

        @block.gpsimd
        def _(pool):
            pool.iota(icol[:], [[1, P]], base=0, channel_multiplier=0).then_inc(iotas, 1)
            pool.iota(idiag[:], [[1, P]], base=0, channel_multiplier=-1).then_inc(iotas, 1)
            pool.iota(ineg[:], [[-TN, NT]], base=0, channel_multiplier=0).then_inc(iotas, 1)
            pool.iota(inode[:], [[TN, NT]], base=0, channel_multiplier=1).then_inc(iotas, 1)
            pool.iota(ithr[:], [[TN, NT - 1]], base=TN, channel_multiplier=0).then_inc(iotas, 1)

        @block.scalar
        def _(act):
            act.dma_start(b2bc[:], t["L0_gnn_ee_b2"].partition_broadcast(TN)).then_inc(ld_small, 16)
            act.dma_start(er[0:ED, :], t["L0_gnn_ee_w1"]).then_inc(ld_small, 16)
            act.dma_start(er[ED:2 * ED, :], t["L0_gnn_ee_w1"]).then_inc(ld_small, 16)
            act.dma_start(ebr[0:ED, :], t["L0_gnn_ee_w1"]).then_inc(ld_small, 16)
            act.dma_start(ebr[ED:ED + 2, :], t["L0_gnn_ee_b1"].partition_broadcast(2)).then_inc(ld_small, 16)
            act.dma_start(sb["epscol"][:], t["L0_gnn_eps"].partition_broadcast(P)).then_inc(ld_small, 16)
            with act.Fori(0, NT // PG) as i:
                act.wait_ge(var_ready, 1)
                act.sem_inc(var_ready, -1)
                act.activation(sd[:], mv[:, :, 1], ACT.Sqrt, bias=sb["lneps"][0:TN, :]).then_inc(sd_ready, 1)
                act.wait_ge(coef_ready, 1)
                act.sem_inc(coef_ready, -1)
                for j in range(PG):
                    act.activation(h0[:, j, :], xall[:, bass.ds(i * PG + j, 1), :].rearrange("p a c -> p (a c)"),
                                   ACT.Relu, bias=nmr[:, j:j + 1], scale=rstd[:, j:j + 1]).then_inc(act_chain, 1)
                act.wait_ge(act_chain, PG)
                act.sem_inc(act_chain, -PG)
                act.sem_inc(h0_ready, 1)
                act.sem_inc(norm_in, 1)
                act.wait_ge(t_ready, 1)
                act.sem_inc(t_ready, -1)
                act.activation(tb[:, :, 0:D], xall[:, bass.ds(i * PG, PG), :], ACT.Copy).then_inc(hi_ready, 1)
            act.wait_ge(ld_w, 48)
            for k, (raw, hi, _) in enumerate(splits):
                act.activation(hi, raw, ACT.Copy, accum_out=wsum[:, k:k + 1]).then_inc(wsum_ready, 1)
            act.wait_ge(wneg_ready, 1)
            act.sem_inc(wneg_ready, -1)
            for k, (raw, _, _) in enumerate(splits):
                act.activation(raw, raw, ACT.Identity, bias=wneg[:, k:k + 1], scale=WS).then_inc(act_chain, 1)
            act.activation(w3s[0], w3s[0], ACT.Copy, scale=WS).then_inc(act_chain, 1)
            act.wait_ge(act_chain, KD + KH + 1)
            act.sem_inc(act_chain, -(KD + KH + 1))
            for raw, hi, _ in splits:
                act.activation(hi, raw, ACT.Copy).then_inc(whi_ready, 1)
            act.activation(w3s[1], w3s[0], ACT.Copy).then_inc(whi_ready, 1)
            act.wait_ge(eb_split, 1)
            act.sem_inc(eb_split, -1)
            act.dma_start(sb["ewb"][ED:ED + 1, :], ebh[ED:ED + 1, :]).then_inc(ewb_done, 16)
            act.wait_ge(ewb_done, 16)

        @block.vector
        def _(dve):
            dve.memset(sb["lneps"][:], LN_EPS).then_inc(dve_chain, 1)
            dve.wait_ge(dve_chain, 1)
            dve.sem_inc(dve_chain, -1)
            for i in range(NT // PG):
                dve.wait_ge(ld_x[i], 16)
            dve.wait_ge(ld_small, 96)
            dve.sem_inc(tb_stored, 16)
            dve.sem_inc(h0_stored, 16)
            with dve.Fori(0, NT // PG) as i:
                for j in range(PG):
                    dve.bn_stats(stat[:, j, :], xall[:, bass.ds(i * PG + j, 1), :].rearrange("p a c -> p (a c)")).then_inc(dve_chain, 1)
                dve.wait_ge(dve_chain, PG)
                dve.sem_inc(dve_chain, -PG)
                for j in range(PG):
                    dve.bn_aggr(mv[:, j, :], stat[:, j, :]).then_inc(dve_chain, 1)
                dve.wait_ge(dve_chain, PG)
                dve.sem_inc(dve_chain, -PG)
                dve.sem_inc(var_ready, 1)
                dve.wait_ge(sd_ready, 1)
                dve.sem_inc(sd_ready, -1)
                dve.reciprocal(rstd[:], sd[:]).then_inc(dve_chain, 1)
                dve.wait_ge(dve_chain, 1)
                dve.sem_inc(dve_chain, -1)
                dve.wait_ge(h0_stored, 16)
                dve.sem_inc(h0_stored, -16)
                dve.scalar_tensor_tensor(out=nmr[:], in0=mv[:, :, 0], scalar=-1.0, in1=rstd[:],
                                         op0=ALU.mult, op1=ALU.mult).then_inc(coef_ready, 1)
                dve.wait_ge(norm_in, 1)
                dve.sem_inc(norm_in, -1)
                xs = xall[:, bass.ds(i * PG, PG), :]
                dve.tensor_tensor(xs, h0[:], b2bc[:].unsqueeze(1).broadcast_to([TN, PG, D]), ALU.add).then_inc(dve_chain, 1)
                dve.wait_ge(dve_chain, 1)
                dve.sem_inc(dve_chain, -1)
                dve.wait_ge(tb_stored, 16)
                dve.sem_inc(tb_stored, -16)
                dve.sem_inc(t_ready, 1)
                dve.wait_ge(hi_ready, 1)
                dve.sem_inc(hi_ready, -1)
                dve.tensor_tensor(tb[:, :, D:2 * D], xs, tb[:, :, 0:D], ALU.subtract).then_inc(tb_ready, 1)
            dve.wait_ge(iotas, 5)
            dve.sem_inc(iotas, -5)
            dve.tensor_copy(sb["iota16"][:], icol[:, 0:TN]).then_inc(dve_chain, 1)
            dve.wait_ge(dve_chain, 1)
            dve.sem_inc(dve_chain, -1)
            dve.tensor_copy(sb["negbase"][:], ineg[:]).then_inc(dve_chain, 1)
            dve.wait_ge(dve_chain, 1)
            dve.sem_inc(dve_chain, -1)
            dve.tensor_copy(sb["nodeid"][:], inode[:]).then_inc(dve_chain, 1)
            dve.wait_ge(dve_chain, 1)
            dve.sem_inc(dve_chain, -1)
            dve.tensor_copy(thr[:], ithr[:]).then_inc(dve_chain, 1)
            dve.wait_ge(dve_chain, 1)
            dve.sem_inc(dve_chain, -1)
            dve.tensor_scalar(sb["ident"][:], idiag[:], 0.0, None, ALU.is_equal).then_inc(dve_chain, 1)
            dve.wait_ge(dve_chain, 1)
            dve.sem_inc(dve_chain, -1)
            dve.tensor_scalar(sb["epscol"][:], sb["epscol"][:], 2.0, None, ALU.add).then_inc(dve_chain, 1)
            dve.wait_ge(dve_chain, 1)
            dve.sem_inc(dve_chain, -1)
            dve.tensor_copy(sb["ewa"][:], er[:]).then_inc(dve_chain, 1)
            dve.wait_ge(dve_chain, 1)
            dve.sem_inc(dve_chain, -1)
            dve.tensor_copy(ebh[:], ebr[:]).then_inc(dve_chain, 1)
            dve.wait_ge(dve_chain, 1)
            dve.sem_inc(dve_chain, -1)
            dve.tensor_tensor(sb["ewb"][:], ebr[:], ebh[:], ALU.subtract).then_inc(dve_chain, 1)
            dve.wait_ge(dve_chain, 1)
            dve.sem_inc(dve_chain, -1)
            dve.sem_inc(eb_split, 1)
            dve.wait_ge(ld_dst, 16)
            dve.sem_inc(ld_dst, -16)
            for j in range(2):
                dve.tensor_reduce(ext[:, j:j + 1], drow[:, j, :], AX, ALU.min).then_inc(dve_chain, 1)
                dve.wait_ge(dve_chain, 1)
                dve.sem_inc(dve_chain, -1)
                dve.tensor_reduce(ext[:, 2 + j:3 + j], drow[:, j, :], AX, ALU.max).then_inc(dve_chain, 1)
                dve.wait_ge(dve_chain, 1)
                dve.sem_inc(dve_chain, -1)
            dve.tensor_tensor(cmp_[:], ext[:].unsqueeze(2).broadcast_to([half, 4, NT - 1]),
                              thr[0:half, :].unsqueeze(1).broadcast_to([half, 4, NT - 1]), ALU.is_ge).then_inc(dve_chain, 1)
            dve.wait_ge(dve_chain, 1)
            dve.sem_inc(dve_chain, -1)
            dve.tensor_reduce(tile[:], cmp_[:], AX, ALU.add).then_inc(dve_chain, 1)
            dve.wait_ge(dve_chain, 1)
            dve.sem_inc(dve_chain, -1)
            dve.tensor_copy(sched_sb[:, 0, :], tile[:, 0:2]).then_inc(dve_chain, 1)
            dve.wait_ge(dve_chain, 1)
            dve.sem_inc(dve_chain, -1)
            dve.tensor_scalar(sched_sb[:, 1, :], tile[:, 2:4], 1.0, None, ALU.add).then_inc(sched_ready, 1)
            dve.wait_ge(wsum_ready, KD + KH)
            dve.sem_inc(wsum_ready, -(KD + KH))
            dve.tensor_scalar(wneg[:], wsum[:], -WS / H, None, ALU.mult).then_inc(wneg_ready, 1)
            dve.wait_ge(whi_ready, KD + KH + 1)
            dve.sem_inc(whi_ready, -(KD + KH + 1))
            for raw, hi, lo in splits + [w3s]:
                dve.tensor_tensor(lo, raw, hi, ALU.subtract).then_inc(dve_chain, 1)
                dve.wait_ge(dve_chain, 1)
                dve.sem_inc(dve_chain, -1)
    return m.sems


def one_hot(dve, out, iota16, dsts, negbase, b, tile, passed=None):
    for k in range(CB):
        ins = dve.tensor_scalar(out[:, k, :], iota16[:], dsts[:, bass.ds(CB * (b + 1) + k, 1)],
                                negbase[:, bass.ds(tile, 1)], ALU.subtract, ALU.is_equal)
        if passed is not None and k == 0:
            ins.then_inc(passed, 1)
    return ins


def tiles_of(nc, engine, table, b, n):
    why = "the schedule counts the tile bounds that a dst has passed: 0 to NT - 1, and one more for ends"
    both = []
    for part, least in ((0, 0), (1, 1)):
        _, v = nc.values_load_multi_w_load_instructions(
            table[0:1, part, bass.ds(b + 1, n)], engines=[engine], min_val=least, max_val=NT - 1 + part,
            skip_runtime_bounds_check_because=why)
        both.append(v)
    return list(zip(*both))


def edges0(nc, t, dram, sb):
    with ExitStack() as ctx:
        m = Memory(nc, ctx)
        acc, iota16, negbase, ewa, ewb = sb["acc"], sb["iota16"], sb["negbase"], sb["ewa"], sb["ewb"]
        srcs = m.sb("srcs", [P, NCH], I32)
        dsts = m.sb("dsts", [P, NCH + CB], F32)
        idx = m.sb("idx", [P, RING, CB], I32)
        table = m.sb("table0", [1, 2, NBP + 4], I32)
        rows = m.sb("rows", [P, RING, CB, 2 * D], F16)
        ea = m.sb("ea", [P, 2, BE], F32)
        eab = m.sb("eab", [P, 2, BE], F16)
        eah = m.sb("eah", [ED + 2, 2, BE], F16)
        rh = m.sb("rh", [P, 2, CB, D], F16)
        rl = m.sb("rl", [P, 2, CB, D], F16)
        hot = m.sb("hot", [P, 3, CB, TN], F16)
        mlp_ps = m.ps("mlp_ps", [P, 2, CB, D])
        sum_ps = m.ps("sum_ps", [TN, 3, 2 * D])
        used_ps = m.ps("used_ps", [1, 1])

        ld_idx = m.sem("ld_idx")
        ld_dst = m.sem("e_ld_dst")
        ld_tab = m.sem("ld_tab")
        cleared = m.sem("cleared")
        idx_ready = [m.sem(f"idx_ready{s}") for s in range(RING)]
        rows_ready = [m.sem(f"rows_ready{s}") for s in range(RING)]
        ea_ready = [m.sem(f"ea_ready{s}") for s in range(2)]
        ea_free = m.sem("ea_free")
        ones_ready = m.sem("ones_ready")
        ea_high = m.sem("ea_high")
        ea_split = m.sem("ea_split")
        mlp_done = m.sem("mlp_done")
        r_high = m.sem("r_high")
        r_split = m.sem("r_split")
        r_free = m.sem("r_free")
        rows_free = m.sem("rows_free")
        x_chain = m.sem("x_chain")
        hot_ready = m.sem("hot_ready")
        sum_done = m.sem("sum_done")
        sum_free = m.sem("sum_free")
        xhot_ready = m.sem("xhot_ready")
        xsum_done = m.sem("xsum_done")
        chain_sem = m.sem("e_chain")

        block = ctx.enter_context(nc.Block())

        @block.sync
        def _(sp):
            sp.dma_start(srcs[:], t["src_cols"]).then_inc(ld_idx, 16)
            sp.dma_start(table[:, :, 0:NBP + 1], dram["sched"][:, 0:NBP + 1].unsqueeze(0)).then_inc(ld_tab, 16)

            def load(b, s):
                eb = t["edge_t"][bass.ds(b, 1)].rearrange("a d e -> (a d) e")
                sp.dma_start(ea[0:ED, s, :], eb).then_inc(ea_ready[s], 16)
                sp.dma_start(ea[ED:P, s, :], eb).then_inc(ea_ready[s], 16)

            load(0, 0)
            sp.sem_inc(ea_free, 1)
            with sp.Fori(0, NB // RING) as i:
                for u in range(RING):
                    sp.wait_ge(ea_free, 1)
                    sp.sem_inc(ea_free, -1)
                    load(RING * i + u + 1, (u + 1) % 2)

        @block.gpsimd
        def _(pool):
            pool.dma_start(dsts[:], t["dst_cols"]).then_inc(ld_dst, 16)
            pool.memset(eah[ED:ED + 2, :, :], 1.0).then_inc(ones_ready, 1)
            with pool.Fori(0, NB // RING):
                for s in range(RING):
                    pool.wait_ge(idx_ready[s], 1)
                    pool.sem_inc(idx_ready[s], -1)
                    for k in range(CB):
                        pool.indirect_dma_start(
                            rows[:, s, k, :], None, dram["tab0"],
                            bass.IndirectOffsetOnAxis(ap=idx[:, s, k:k + 1], axis=0),
                        ).then_inc(rows_ready[s], 16)

        @block.scalar
        def _(act):
            def high_parts(s):
                act.wait_ge(ea_ready[s], 32)
                act.sem_inc(ea_ready[s], -32)
                act.activation(eab[:, s, :], ea[:, s, :], ACT.Copy).then_inc(ea_high, 1)
                act.activation(eah[0:ED, s, :], ea[0:ED, s, :], ACT.Copy).then_inc(ea_high, 1)

            act.sem_inc(r_free, 2)
            high_parts(0)
            zero = acc[:, NT // 2:NT, :].rearrange("p t c -> p (t c)")
            act.activation(zero, iota16[:, 0:1].broadcast_to([P, NT // 2 * 2 * D]), ACT.Copy, scale=0.0).then_inc(cleared, 1)
            with act.Fori(0, NB // RING) as i:
                for u in range(RING):
                    b, s = RING * i + u, u % 2
                    high_parts(1 - s)
                    act.wait_ge(mlp_done, 1)
                    act.sem_inc(mlp_done, -1)
                    act.wait_ge(r_free, 1)
                    act.sem_inc(r_free, -1)
                    act.activation(rh[:, s].rearrange("p k d -> p (k d)"), mlp_ps[:, s].rearrange("p k d -> p (k d)"),
                                   ACT.Relu).then_inc(r_high, 1)

        @block.tensor
        def _(pe):
            def edge_mlp(s):
                pe.wait_ge(ea_split, 1)
                pe.sem_inc(ea_split, -1)
                pe.sem_inc(ea_free, 1)
                for k in range(CB):
                    e = slice(k * P, (k + 1) * P)
                    pe.matmul(mlp_ps[:, s, k, :], eab[:, s, e], ewa[:], start=True, stop=False)
                    ins = pe.matmul(mlp_ps[:, s, k, :], eah[:, s, e], ewb[:], start=False, stop=True)
                ins.then_inc(mlp_done, 1)

            def sums(out, h, ring, s):
                for k in range(CB):
                    lhs = hot[:, h, k, :]
                    pe.matmul(out[:, 0:D], lhs, rows[:, ring, k, 0:D], start=(k == 0), stop=False, skip_group_check=True)
                    pe.matmul(out[:, 0:D], lhs, rows[:, ring, k, D:2 * D], start=False, stop=False, skip_group_check=True)
                    pe.matmul(out[:, D:2 * D], lhs, rh[:, s, k, :], start=False, stop=False, skip_group_check=True)
                    ins = pe.matmul(out[:, D:2 * D], lhs, rl[:, s, k, :], start=False, stop=(k == CB - 1), skip_group_check=True)
                return ins

            pe.wait_ge(ld_tab, 16)
            pe.wait_ge(ones_ready, 1)
            pe.sem_inc(ones_ready, -1)
            pe.sem_inc(sum_free, 2)
            edge_mlp(0)
            with pe.Fori(0, NB // RING) as i:
                tiles = tiles_of(nc, PE, table, RING * i, RING)
                for u in range(RING):
                    b, s = RING * i + u, u % 2
                    edge_mlp(1 - s)
                    lo, end = tiles[u]
                    pe.wait_ge(hot_ready, 1)
                    pe.sem_inc(hot_ready, -1)
                    pe.wait_ge(sum_free, 1)
                    pe.sem_inc(sum_free, -1)
                    pe.wait_ge(r_split, 1)
                    pe.sem_inc(r_split, -1)
                    pe.wait_ge(rows_ready[u], 16 * CB * (i + 1))
                    sums(sum_ps[:, s, :], s, u, s).then_inc(sum_done, 1)
                    with pe.If(end > lo + 1):
                        with pe.Fori(lo + 1, end):
                            pe.wait_ge(xhot_ready, 1)
                            pe.sem_inc(xhot_ready, -1)
                            sums(sum_ps[:, 2, :], 2, u, s).then_inc(xsum_done, 1)
                    pe.matmul(used_ps[:], ewa[:, 0:1], ewa[:, 0:1], start=True, stop=True).then_inc(r_free, 1)
                    pe.matmul(used_ps[:], ewa[:, 0:1], ewa[:, 0:1], start=True, stop=True).then_inc(rows_free, 1)

        @block.vector
        def _(dve):
            def low_parts(s):
                dve.wait_ge(ea_high, 2)
                dve.sem_inc(ea_high, -2)
                dve.tensor_tensor(eab[ED:P, s, :], ea[ED:P, s, :], eab[ED:P, s, :], ALU.subtract).then_inc(ea_split, 1)

            def add(s, lo):
                dve.wait_ge(chain_sem, 1)
                dve.sem_inc(chain_sem, -1)
                dve.wait_ge(sum_done, 1)
                dve.sem_inc(sum_done, -1)
                a = acc[0:TN, bass.ds(lo, 1), :].rearrange("p a c -> p (a c)")
                dve.tensor_tensor(a, a, sum_ps[:, s, :], ALU.add).then_inc(sum_free, 1)

            def extras(b, lo, end):
                with dve.If(end > lo + 1):
                    with dve.Fori(lo + 1, end) as x:
                        one_hot(dve, hot[:, 2], iota16, dsts, negbase, b, x).then_inc(xhot_ready, 1)
                        dve.wait_ge(xsum_done, 1)
                        dve.sem_inc(xsum_done, -1)
                        ax = acc[0:TN, bass.ds(x, 1), :].rearrange("p a c -> p (a c)")
                        dve.tensor_tensor(ax, ax, sum_ps[:, 2, :], ALU.add).then_inc(x_chain, 1)
                        dve.wait_ge(x_chain, 1)
                        dve.sem_inc(x_chain, -1)

            def indices(b, s):
                dve.tensor_copy(idx[:, s, :], srcs[:, bass.ds(CB * b, CB)]).then_inc(idx_ready[s], 1)

            def finish_block(b, ring, tiles):
                extras(b, *tiles)
                dve.wait_ge(rows_free, 1)
                dve.sem_inc(rows_free, -1)
                indices(b + RING, ring)

            def main_hot(b, s, lo):
                one_hot(dve, hot[:, s], iota16, dsts, negbase, b, lo, chain_sem).then_inc(hot_ready, 1)

            dve.wait_ge(ld_dst, 16)
            dve.wait_ge(ld_tab, 16)
            dve.wait_ge(ld_idx, 16)
            for b in range(RING):
                indices(b, b)
            main_hot(0, 0, tiles_of(nc, DVE, table, 0, 1)[0][0])
            dve.wait_ge(chain_sem, 1)
            dve.sem_inc(chain_sem, -1)
            low_parts(0)
            dve.memset(acc[:, 0:NT // 2, :], 0.0).then_inc(chain_sem, 1)
            dve.wait_ge(chain_sem, 1)
            dve.sem_inc(chain_sem, -1)
            dve.wait_ge(cleared, 1)
            dve.sem_inc(cleared, -1)
            with dve.Fori(0, NB // RING) as i:
                tiles = tiles_of(nc, DVE, table, RING * i - 1, RING + 2)
                for u in range(RING):
                    b, s = RING * i + u, u % 2
                    low_parts(1 - s)
                    dve.wait_ge(r_high, 1)
                    dve.sem_inc(r_high, -1)
                    dve.scalar_tensor_tensor(out=rl[:, s].rearrange("p k d -> p (k d)"), in0=mlp_ps[:, s].rearrange("p k d -> p (k d)"),
                                             scalar=0.0, in1=rh[:, s].rearrange("p k d -> p (k d)"),
                                             op0=ALU.max, op1=ALU.subtract).then_inc(r_split, 1)
                    if u:
                        add(1 - s, tiles[u][0])
                    else:
                        with dve.If(i > 0):
                            add(1 - s, tiles[u][0])
                    main_hot(b + 1, 1 - s, tiles[u + 2][0])
                    if u:
                        finish_block(b - 1, u - 1, tiles[u])
                    else:
                        with dve.If(i > 0):
                            finish_block(b - 1, RING - 1, tiles[u])
            lo, end = tiles_of(nc, DVE, table, NB - 1, 1)[0]
            add((NB - 1) % 2, lo)
            extras(NB - 1, lo, end)


def nodes(nc, t, dram, sb, stale):
    with ExitStack() as ctx:
        m = Memory(nc, ctx)
        acc, ident, lneps, epscol = sb["acc"], sb["ident"], sb["lneps"], sb["epscol"]
        w2e = m.sb("w2e", [P, KD, D], F32)
        waug = m.sb("waug", [P, KD, AW], F32)
        bcol = m.sb("bcol", [P, KD], F32)
        ones = m.sb("ones", [P, P], F32)
        zero = m.sb("zero", [P, 1], F32)
        eb1 = m.sb("eb1", [P, KD], F32)
        cols = {n: m.sb("c_" + n, [P, KH], F32) for n in ("b1", "g1", "be1", "b2", "g2", "be2")}
        csum = m.sb("csum", [P, 2], F32)
        bc = {n: m.sb("bc_" + n, [TN, D], F32) for n in ("ee_b2", "b3", "bn_g", "bn_b")}
        baug = m.sb("baug", [TN, AW], F32)
        hf = m.sb("hf", [TN, D], F32)
        u = m.sb("u", [TN, 2, D], F32)
        rr = m.sb("rr", [TN, 2, D], F32)
        rt = m.sb("rt", [P, KD, TN], F32)
        hh = m.sb("hh", [P, KD, TN], F16)
        hl = m.sb("hl", [P, KD, TN], F16)
        z = [m.sb(f"z{j}", [P, KH, TN], F32) for j in (1, 2)]
        a = [m.sb(f"a{j}", [P, KH, TN], F32) for j in (1, 2)]
        room = z[0][:].rearrange("p k n -> p (k n)")
        o1, o2 = KD * D, KD * (D + TN)
        wt = room[:, 0:o1].rearrange("p (k n) -> p k n", n=D)
        bcb = room[:, o1:o2].rearrange("p (k n) -> p k n", n=TN)
        att = room[:, o2:o2 + KD * 2 * HEADS].rearrange("p (k n) -> p k n", n=2 * HEADS)
        ah = [m.sb(f"ah{j}", [P, n, KH, TN], F16) for j, n in ((1, 2), (2, 1))]
        al = [m.sb(f"al{j}", [P, n, KH, TN], F16) for j, n in ((1, 2), (2, 1))]
        ssq = [m.sb(f"ssq{j}", [P, TN], F32) for j in (1, 2)]
        rstd = [m.sb(f"rstd{j}", [P, TN], F32) for j in (1, 2)]
        hx = m.sb("hx", [TN, 2, D], F32)
        o = m.sb("o", [TN, D], F32)
        x1 = m.sb("x1", [TN, D], F32)
        h2 = m.sb("h2", [TN, D], F32)
        h2t = m.sb("h2t", [P, KD, TN], F32)
        prow = m.sb("prow", [TN, AW], F32)
        st3 = m.sb("st3", [TN, 2, 6], F32)
        mv3 = m.sb("mv3", [TN, 2, 2], F32)
        rrow = m.sb("rrow", [TN, 2], F32)

        z_ps = [m.ps(f"z{j}_ps", [P, 2, 512]) for j in (1, 2)]
        tv_ps = m.ps("tv_ps", [P, 3, TN])
        hv_ps = m.ps("hv_ps", [P, 3, TN])
        y_ps = m.ps("y_ps", [P, D])
        gp_ps = m.ps("gp_ps", [P, 512])
        t_ps, h_ps, v_ps = tv_ps[:, 0:KD, :], hv_ps[:, 0:KD, :], [hv_ps[:, KD, :], tv_ps[:, KD, :]]
        g_ps = gp_ps[:, 0:KD * TN].rearrange("p (k n) -> p k n", n=TN)
        p_ps = gp_ps[0:TN, 0:AW]

        def sem(n):
            return m.sem("n_" + n)

        ld, ld_act, setup, setup_ps, setup_done, ready = (
            sem("ld"), sem("ld_act"), sem("setup"), sem("setup_ps"), sem("setup_done"), sem("ready"))
        hf_ready, hf_free = sem("hf_ready"), sem("hf_free")
        hx_ready, hx_free = sem("hx_ready"), sem("hx_free")
        u_ready, acc_free = sem("u_ready"), sem("acc_free")
        rr_ready, rr_free = sem("rr_ready"), sem("rr_free")
        t_done, rt_ready = sem("t_done"), sem("rt_ready")
        h_done, hh_ready, h_split = sem("h_done"), sem("hh_ready"), sem("h_split")
        z_done = [sem(f"z{j}_done") for j in (1, 2)]
        z_ready = [sem(f"z{j}_ready") for j in (1, 2)]
        ssq_ready = [sem(f"ssq{j}_ready") for j in (1, 2)]
        var_done = [sem(f"var{j}_done") for j in (1, 2)]
        sd_ready = [sem(f"sd{j}_ready") for j in (1, 2)]
        zn_ready = [sem(f"zn{j}_ready") for j in (1, 2)]
        ah_ready = [sem(f"ah{j}_ready") for j in (1, 2)]
        a_split = [sem(f"a{j}_split") for j in (1, 2)]
        y_done, y_free, hb_ready = sem("y_done"), sem("y_free"), sem("hb_ready")
        x1_ready, x1_stored = sem("x1_ready"), sem("x1_stored")
        h2_ready, g_done, h2t_ready = sem("h2_ready"), sem("g_done"), sem("h2t_ready")
        p_done, p_free = sem("p_done"), sem("p_free")
        prow_ready, prow_stored = sem("prow_ready"), sem("prow_stored")
        row_var = [sem(f"row_var{j}") for j in (0, 1)]
        row_coef = [sem(f"row_coef{j}") for j in (0, 1)]
        act_chain, st_kept = sem("act_chain"), sem("st_kept")
        chain_sem = sem("chain")

        def tiles_v(ap):
            return ap.rearrange("(t p) c -> t p c", p=TN)

        h0_v, x_v, x1_v, tab_v = tiles_v(dram["h0"]), tiles_v(t["x"]), tiles_v(dram["x1"]), tiles_v(dram["tab1"])

        def one(ap, i):
            return ap[bass.ds(i, 1)].rearrange("a p c -> (a p) c")

        def bodies(eng, body):
            first, last = 4, NT - 2
            for i in range(first):
                body(i, i % 2)
            with eng.Fori(0, (last - first) // 2) as pair:
                for k in range(2):
                    body(2 * pair + (first + k), k)
            for i in range(last, NT + 4):
                body(i, i % 2)

        def has(i, back, ahead=0):
            return not isinstance(i, int) or 0 <= i + ahead - back < NT

        block = ctx.enter_context(nc.Block())

        @block.sync
        def _(sp):
            sp.dma_start(w2e[:], t["L0_gnn_ee_w2"].rearrange("(k p) n -> p k n", p=P)).then_inc(ld, 16)
            sp.dma_start(waug[:, :, 0:D], t["L1_gnn_W"].rearrange("(k p) n -> p k n", p=P)).then_inc(ld, 16)
            sp.dma_start(wt, t["L1_gnn_W_t"].rearrange("(k p) n -> p k n", p=P)).then_inc(ld, 16)
            sp.dma_start(bcol[:], t["L1_gnn_b_cols"]).then_inc(ld, 16)
            sp.dma_start(eb1[:], t["L0_gnn_ee_b1_cols"]).then_inc(ld, 16)
            for n, c in cols.items():
                sp.dma_start(c[:], t[f"L0_gnn_{n}_cols"]).then_inc(ld, 16)
            for n, c in bc.items():
                sp.dma_start(c[:], t[f"L0_gnn_{n}"].partition_broadcast(TN)).then_inc(ld, 16)
            sp.dma_start(baug[:, 0:D], t["L1_gnn_b"].partition_broadcast(TN)).then_inc(ld, 16)

            def load_front(i):
                sp.dma_start(hf[:], one(h0_v, i)).then_inc(hf_ready, 16)

            load_front(0)
            sp.sem_inc(hx_free, 1)

            def body(i, p):
                if has(i, 0, 1):
                    sp.wait_ge(hf_free, 1)
                    sp.sem_inc(hf_free, -1)
                    load_front(i + 1)
                if has(i, 2):
                    sp.wait_ge(hx_free, 1)
                    sp.sem_inc(hx_free, -1)
                    sp.dma_start(hx[:, 0, :], one(h0_v, i - 2)).then_inc(hx_ready, 16)
                    sp.dma_start(hx[:, 1, :], one(x_v, i - 2)).then_inc(hx_ready, 16)
                if has(i, 3):
                    sp.wait_ge(x1_ready, 1)
                    sp.sem_inc(x1_ready, -1)
                    sp.dma_start(one(x1_v, i - 3), x1[:]).then_inc(x1_stored, 16)
                if has(i, 4):
                    sp.wait_ge(prow_ready, 1)
                    sp.sem_inc(prow_ready, -1)
                    sp.dma_start(one(tab_v, i - 4), prow[:, 0:TW]).then_inc(prow_stored, 16)

            bodies(sp, body)
            sp.wait_ge(x1_stored, 16)
            sp.wait_ge(prow_stored, 16)

        @block.gpsimd
        def _(pool):
            for old in stale:
                pool.sem_clear(old)
            pool.memset(zero[:], 0.0).then_inc(setup, 1)
            pool.memset(att, 0.0).then_inc(setup, 1)
            pool.wait_ge(setup, 2)
            pool.sem_inc(setup, -2)
            for h in range(HEADS):
                q = slice(HD * (h % 4), HD * (h % 4) + HD)
                for c, n in ((h, "L1_gnn_a_src"), (HEADS + h, "L1_gnn_a_trg")):
                    pool.dma_start(att[q, h // 4, c:c + 1], t[n][0, h, :].unsqueeze(1)).then_inc(ld_act, 16)

            def turnable(i, p):
                pool.tensor_copy(rr[:, p, :], acc[0:TN, bass.ds(i, 1), D:2 * D].rearrange("p a c -> p (a c)")).then_inc(rr_ready, 1)

            turnable(0, 0)
            turnable(1, 1)

            def body(i, p):
                if has(i, 0):
                    pool.wait_ge(rr_free, 1)
                    pool.sem_inc(rr_free, -1)
                if has(i, 0, 2):
                    turnable(i + 2, p)
                if has(i, 2):
                    pool.wait_ge(hx_ready, 32)
                    pool.sem_inc(hx_ready, -32)
                    pool.tensor_tensor(hx[:, 0, :], hx[:, 0, :], bc["b3"][:], ALU.add).then_inc(hb_ready, 1)
                if has(i, 1):
                    pool.wait_ge(acc_free, 1)
                    pool.sem_inc(acc_free, -1)
                    pool.tensor_copy(acc[0:TN, bass.ds(i - 1, 1), 0:TW].rearrange("p a c -> p (a c)"), zero[0:TN, :].broadcast_to([TN, TW]))

            pool.wait_ge(ready, 1)
            bodies(pool, body)

        @block.tensor
        def _(pe):
            pe.wait_ge(ld, 16 * (6 + len(cols) + len(bc)))
            pe.wait_ge(ld_act, 16 * 2 * HEADS)
            pe.wait_ge(setup_done, 1)
            pe.sem_inc(setup_done, -1)
            for j in range(KD):
                for k in range(KD):
                    pe.matmul(t_ps[:, 0, 2 * HEADS * j:2 * HEADS * (j + 1)], wt[:, k, j * P:(j + 1) * P], att[:, k, :],
                              start=(k == 0), stop=(k == KD - 1))
            for k in range(KD):
                pe.matmul(p_ps[:, 0:2 * HEADS], bcb[:, k, :], att[:, k, :], start=(k == 0), stop=(k == KD - 1))
            pe.matmul(y_ps[:, 0:KH], ones[:], cols["b1"][:], start=True, stop=True)
            pe.matmul(y_ps[:, KH:2 * KH], ones[:], cols["b2"][:], start=True, stop=True).then_inc(setup_ps, 1)

            def turn(i, p):
                pe.wait_ge(rr_ready, 1)
                pe.sem_inc(rr_ready, -1)
                for k in range(KD):
                    ins = pe.transpose(t_ps[:, k, :], rr[:, p, k * P:(k + 1) * P], ident[0:TN, 0:TN])
                ins.then_inc(t_done, 1)

            def products(out, hi, lo, whi, wlo, n, ks=None, rows=False):
                for k in ks or range(n):
                    for q, (x_, w_) in enumerate(((hi, whi), (lo, whi), (hi, wlo))):
                        lhs, rhs = (x_(k), w_(k)) if rows else (w_(k), x_(k))
                        ins = pe.matmul(out, lhs, rhs, start=(k == 0 and q == 0), stop=(k == n - 1 and q == 2))
                return ins

            def hidden(j, half, outputs, n, hi, lo, whi, wlo):
                for b in outputs:
                    f = slice((4 * half + b) * P, (4 * half + b + 1) * P)
                    out = z_ps[j][:, half, b * TN:(b + 1) * TN]
                    ins = products(out, hi, lo, lambda k: whi[:, k, f], lambda k: wlo[:, k, f], n)
                if b == 3:
                    ins.then_inc(z_done[j], 1)

            def layer2(half, outputs, p):
                hidden(1, half, outputs, KH, lambda k: ah[0][:, p, k, :], lambda k: al[0][:, p, k, :], sb["w2h"], sb["w2l"])

            def output(ks):
                return products(y_ps[0:TN, 0:D], lambda k: ah[1][:, 0, k, :], lambda k: al[1][:, 0, k, :],
                                lambda k: sb["w3h"][:, k, :], lambda k: sb["w3l"][:, k, :], KH, ks, rows=True)

            def variance(j):
                pe.wait_ge(ssq_ready[j], 1)
                pe.sem_inc(ssq_ready[j], -1)
                pe.matmul(v_ps[j], ones[:], ssq[j][:], start=True, stop=True).then_inc(var_done[j], 1)

            pe.wait_ge(ready, 1)
            pe.sem_inc(y_free, 1)
            pe.sem_inc(p_free, 1)

            def make_h(i, p):
                pe.wait_ge(u_ready, 1)
                pe.sem_inc(u_ready, -1)
                for j in range(KD):
                    f = slice(j * P, (j + 1) * P)
                    for k in range(KD):
                        pe.matmul(h_ps[:, j, :], w2e[:, k, f], rt[:, k, :], start=(k == 0), stop=False)
                    ins = pe.matmul(h_ps[:, j, :], u[:, p, f], ident[0:TN, 0:TN], start=False, stop=True)
                ins.then_inc(h_done, 1)

            turn(0, 0)
            pe.wait_ge(rt_ready, 1)
            pe.sem_inc(rt_ready, -1)
            pe.sem_inc(rr_free, 1)
            make_h(0, 0)
            turn(1, 1)

            def body(i, p):
                if has(i, 0):
                    pe.wait_ge(h_split, 1)
                    pe.sem_inc(h_split, -1)
                    for half in range(2):
                        hidden(0, half, range(4), KD, lambda k: hh[:, k, :], lambda k: hl[:, k, :], sb["w1h"], sb["w1l"])
                if has(i, 0, 1):
                    pe.wait_ge(rt_ready, 1)
                    pe.sem_inc(rt_ready, -1)
                    pe.sem_inc(rr_free, 1)
                if has(i, 2):
                    variance(1)
                if has(i, 4):
                    pe.wait_ge(h2_ready, 1)
                    pe.sem_inc(h2_ready, -1)
                    pe.wait_ge(p_free, 1)
                    pe.sem_inc(p_free, -1)
                    for k in range(KD):
                        ins = pe.transpose(g_ps[:, k, :], h2[:, k * P:(k + 1) * P], ident[0:TN, 0:TN])
                    ins.then_inc(g_done, 1)
                if has(i, 1):
                    pe.wait_ge(a_split[0], 1)
                    pe.sem_inc(a_split[0], -1)
                    layer2(0, range(4), 1 - p)
                if has(i, 0):
                    variance(0)
                if has(i, 1):
                    layer2(1, range(4), 1 - p)
                if has(i, 4):
                    pe.wait_ge(h2t_ready, 1)
                    pe.sem_inc(h2t_ready, -1)
                    for k in range(KD):
                        ins = pe.matmul(p_ps, h2t[:, k, :], waug[:, k, :], start=(k == 0), stop=(k == KD - 1))
                    ins.then_inc(p_done, 1)
                if has(i, 2):
                    pe.wait_ge(a_split[1], 1)
                    pe.sem_inc(a_split[1], -1)
                    pe.wait_ge(y_free, 1)
                    pe.sem_inc(y_free, -1)
                    output(range(KH // 2))
                if has(i, 0, 1):
                    make_h(i + 1, 1 - p)
                if has(i, 0, 2):
                    turn(i + 2, p)
                if has(i, 2):
                    output(range(KH // 2, KH)).then_inc(y_done, 1)

            bodies(pe, body)

        @block.scalar
        def _(act):
            act.wait_ge(ready, 1)

            def turned(i):
                act.wait_ge(t_done, 1)
                act.sem_inc(t_done, -1)
                for k in range(KD):
                    ins = act.activation(rt[:, k, :], t_ps[:, k, :], ACT.Identity, bias=eb1[:, k:k + 1])
                ins.then_inc(rt_ready, 1)

            def biased(j, b, half):
                act.wait_ge(z_done[j], 1)
                act.sem_inc(z_done[j], -1)
                for k in range(4 * half, 4 * half + 4):
                    ins = act.activation(z[j][:, k, :], z_ps[j][:, half, (k % 4) * TN:(k % 4 + 1) * TN], ACT.Identity,
                                         bias=cols[b][:, k:k + 1], scale=(1.0, 1.0 / WS)[j])
                if half:
                    ins.then_inc(z_ready[j], 1)

            def deviation(j):
                act.wait_ge(var_done[j], 1)
                act.sem_inc(var_done[j], -1)
                act.activation(rstd[j][:], v_ps[j], ACT.Sqrt, bias=lneps[:]).then_inc(sd_ready[j], 1)

            def row_deviation(j):
                act.wait_ge(row_var[j], 1)
                act.sem_inc(row_var[j], -1)
                act.activation(rrow[:, j:j + 1], mv3[:, j, 1:2], ACT.Sqrt, bias=lneps[0:TN, :]).then_inc(row_coef[j], 1)

            def activated(j, slot, g, be):
                act.wait_ge(zn_ready[j], 1)
                act.sem_inc(zn_ready[j], -1)
                for k in range(KH):
                    ins = act.activation(a[j][:, k, :], z[j][:, k, :], ACT.Relu, bias=cols[be][:, k:k + 1], scale=cols[g][:, k:k + 1])
                ins.then_inc(act_chain, 1)
                act.wait_ge(act_chain, 1)
                act.sem_inc(act_chain, -1)
                act.activation(ah[j][:, slot], a[j][:], ACT.Copy).then_inc(ah_ready[j], 1)

            turned(0)

            def body(i, p):
                if has(i, 0):
                    act.wait_ge(h_done, 1)
                    act.sem_inc(h_done, -1)
                    act.activation(hh[:], h_ps, ACT.Copy, scale=1.0 / WS).then_inc(hh_ready, 1)
                if has(i, 0, 1):
                    turned(i + 1)
                if has(i, 0):
                    biased(0, "b1", 0)
                    biased(0, "b1", 1)
                if has(i, 2):
                    deviation(1)
                    activated(1, 0, "g2", "be2")
                if has(i, 4):
                    act.wait_ge(g_done, 1)
                    act.sem_inc(g_done, -1)
                    act.activation(h2t[:], g_ps, ACT.Relu).then_inc(h2t_ready, 1)
                if has(i, 0):
                    deviation(0)
                if has(i, 1):
                    biased(1, "b2", 0)
                if has(i, 3):
                    row_deviation(0)
                if has(i, 0):
                    activated(0, p, "g1", "be1")
                if has(i, 1):
                    biased(1, "b2", 1)
                if has(i, 3):
                    row_deviation(1)

            bodies(act, body)

        @block.vector
        def _(dve):
            dve.wait_ge(ld, 16 * (6 + len(cols) + len(bc)))
            dve.memset(ones[:], 1.0 / H).then_inc(chain_sem, 1)
            dve.wait_ge(chain_sem, 1)
            dve.sem_inc(chain_sem, -1)
            dve.tensor_scalar(eb1[:], eb1[:], 0.0, None, ALU.max).then_inc(chain_sem, 1)
            dve.wait_ge(chain_sem, 1)
            dve.sem_inc(chain_sem, -1)
            dve.tensor_copy(bcb, bcol[:].unsqueeze(2).broadcast_to([P, KD, TN])).then_inc(chain_sem, 1)
            dve.wait_ge(chain_sem, 1)
            dve.sem_inc(chain_sem, -1)
            dve.sem_inc(setup_done, 1)
            dve.wait_ge(setup_ps, 1)
            dve.sem_inc(setup_ps, -1)
            for j in range(KD):
                dve.tensor_copy(waug[:, j, D:AW], t_ps[:, 0, 2 * HEADS * j:2 * HEADS * (j + 1)]).then_inc(chain_sem, 1)
                dve.wait_ge(chain_sem, 1)
                dve.sem_inc(chain_sem, -1)
            dve.tensor_copy(baug[:, D:AW], p_ps[:, 0:2 * HEADS]).then_inc(chain_sem, 1)
            dve.wait_ge(chain_sem, 1)
            dve.sem_inc(chain_sem, -1)
            for j, n in ((0, "b1"), (1, "b2")):
                dve.tensor_reduce(csum[:, j:j + 1], y_ps[:, KH * j:KH * (j + 1)], AX, ALU.add).then_inc(chain_sem, 1)
                dve.wait_ge(chain_sem, 1)
                dve.sem_inc(chain_sem, -1)
                dve.tensor_scalar(cols[n][:], cols[n][:], csum[:, j:j + 1], None, ALU.subtract).then_inc(chain_sem, 1)
                dve.wait_ge(chain_sem, 1)
                dve.sem_inc(chain_sem, -1)
            dve.sem_inc(ready, 1)
            dve.sem_inc(x1_stored, 16)
            dve.sem_inc(prow_stored, 16)
            dve.sem_inc(st_kept, 1)

            def front(i, p):
                dve.wait_ge(hf_ready, 16)
                dve.sem_inc(hf_ready, -16)
                dve.scalar_tensor_tensor(out=u[:, p, :], in0=hf[:], scalar=epscol[0:TN, :], in1=bc["ee_b2"][:],
                                         op0=ALU.mult, op1=ALU.add).then_inc(chain_sem, 1)
                dve.wait_ge(chain_sem, 1)
                dve.sem_inc(chain_sem, -1)
                dve.sem_inc(hf_free, 1)
                dve.tensor_tensor(u[:, p, :], u[:, p, :], acc[0:TN, bass.ds(i, 1), 0:D].rearrange("p a c -> p (a c)"), ALU.add).then_inc(chain_sem, 1)
                dve.wait_ge(chain_sem, 1)
                dve.sem_inc(chain_sem, -1)
                dve.sem_inc(acc_free, 1)

            def squares(j):
                dve.wait_ge(z_ready[j], 1)
                dve.sem_inc(z_ready[j], -1)
                dve.tensor_tensor(a[j][:], z[j][:], z[j][:], ALU.mult).then_inc(chain_sem, 1)
                dve.wait_ge(chain_sem, 1)
                dve.sem_inc(chain_sem, -1)
                dve.tensor_reduce(ssq[j][:], a[j][:].rearrange("p k n -> p n k"), AX, ALU.add).then_inc(chain_sem, 1)
                dve.wait_ge(chain_sem, 1)
                dve.sem_inc(chain_sem, -1)
                dve.sem_inc(ssq_ready[j], 1)

            def scaled(j, read=None):
                dve.wait_ge(sd_ready[j], 1)
                dve.sem_inc(sd_ready[j], -1)
                if read is not None:
                    dve.sem_inc(read, 1)
                dve.reciprocal(rstd[j][:], rstd[j][:]).then_inc(chain_sem, 1)
                dve.wait_ge(chain_sem, 1)
                dve.sem_inc(chain_sem, -1)
                dve.tensor_tensor(z[j][:], z[j][:], rstd[j][:].unsqueeze(1).broadcast_to([P, KH, TN]), ALU.mult).then_inc(zn_ready[j], 1)

            def low(j, slot):
                dve.wait_ge(ah_ready[j], 1)
                dve.sem_inc(ah_ready[j], -1)
                dve.tensor_tensor(al[j][:, slot], a[j][:], ah[j][:, slot], ALU.subtract).then_inc(chain_sem, 1)
                dve.wait_ge(chain_sem, 1)
                dve.sem_inc(chain_sem, -1)
                dve.sem_inc(a_split[j], 1)

            def row_stats(j, src):
                dve.bn_stats(st3[:, j, :], src).then_inc(chain_sem, 1)
                dve.wait_ge(chain_sem, 1)
                dve.sem_inc(chain_sem, -1)
                dve.bn_aggr(mv3[:, j, :], st3[:, j, :]).then_inc(chain_sem, 1)
                dve.wait_ge(chain_sem, 1)
                dve.sem_inc(chain_sem, -1)
                dve.sem_inc(row_var[j], 1)

            def row_norm(j, dst, src):
                dve.wait_ge(row_coef[j], 1)
                dve.sem_inc(row_coef[j], -1)
                dve.reciprocal(rrow[:, j:j + 1], rrow[:, j:j + 1]).then_inc(chain_sem, 1)
                dve.wait_ge(chain_sem, 1)
                dve.sem_inc(chain_sem, -1)
                return dve.tensor_scalar(dst, src, mv3[:, j, 0:1], rrow[:, j:j + 1], ALU.subtract, ALU.mult)

            front(0, 0)
            dve.sem_inc(u_ready, 1)

            def body(i, p):
                if has(i, 0):
                    dve.wait_ge(hh_ready, 1)
                    dve.sem_inc(hh_ready, -1)
                    dve.scalar_tensor_tensor(out=hl[:], in0=h_ps, scalar=1.0 / WS, in1=hh[:],
                                             op0=ALU.mult, op1=ALU.subtract).then_inc(h_split, 1)
                if has(i, 1):
                    low(0, 1 - p)
                if has(i, 2):
                    squares(1)
                if has(i, 4):
                    row_norm(1, h2[:], x1[:]).then_inc(chain_sem, 1)
                    dve.wait_ge(chain_sem, 1)
                    dve.sem_inc(chain_sem, -1)
                    dve.sem_inc(h2_ready, 1)
                if has(i, 2):
                    scaled(1)
                if has(i, 0):
                    squares(0)
                if has(i, 0, 1):
                    front(i + 1, 1 - p)
                if has(i, 3):
                    dve.wait_ge(y_done, 1)
                    dve.sem_inc(y_done, -1)
                    dve.wait_ge(hb_ready, 1)
                    dve.sem_inc(hb_ready, -1)
                    dve.scalar_tensor_tensor(out=o[:], in0=y_ps[0:TN, 0:D], scalar=1.0 / WS, in1=hx[:, 0, :],
                                             op0=ALU.mult, op1=ALU.add).then_inc(chain_sem, 1)
                    dve.wait_ge(chain_sem, 1)
                    dve.sem_inc(chain_sem, -1)
                    dve.sem_inc(y_free, 1)
                    row_stats(0, o[:])
                if has(i, 0):
                    scaled(0, u_ready if has(i, 0, 1) else None)
                if has(i, 2):
                    low(1, 0)
                if has(i, 3):
                    row_norm(0, o[:], o[:]).then_inc(chain_sem, 1)
                    dve.wait_ge(chain_sem, 1)
                    dve.sem_inc(chain_sem, -1)
                    dve.tensor_tensor(o[:], o[:], bc["bn_g"][:], ALU.mult).then_inc(chain_sem, 1)
                    dve.wait_ge(chain_sem, 1)
                    dve.sem_inc(chain_sem, -1)
                if has(i, 4):
                    dve.wait_ge(p_done, 1)
                    dve.sem_inc(p_done, -1)
                    dve.wait_ge(prow_stored, 16)
                    dve.sem_inc(prow_stored, -16)
                    dve.wait_ge(st_kept, 1)
                    dve.sem_inc(st_kept, -1)
                    dve.tensor_tensor(prow[:], p_ps, baug[:], ALU.add).then_inc(chain_sem, 1)
                    dve.wait_ge(chain_sem, 1)
                    dve.sem_inc(chain_sem, -1)
                    dve.sem_inc(p_free, 1)
                    dve.sem_inc(prow_ready, 1)
                    dve.tensor_copy(sb["st"][0:TN, bass.ds(i - 4, 1), :].rearrange("p a c -> p (a c)"), prow[:, D:AW]).then_inc(st_kept, 1)
                if has(i, 3):
                    dve.tensor_tensor(o[:], o[:], bc["bn_b"][:], ALU.add).then_inc(chain_sem, 1)
                    dve.wait_ge(chain_sem, 1)
                    dve.sem_inc(chain_sem, -1)
                    dve.wait_ge(x1_stored, 16)
                    dve.sem_inc(x1_stored, -16)
                    dve.scalar_tensor_tensor(out=x1[:], in0=o[:], scalar=0.0, in1=hx[:, 1, :],
                                             op0=ALU.max, op1=ALU.add).then_inc(chain_sem, 1)
                    dve.wait_ge(chain_sem, 1)
                    dve.sem_inc(chain_sem, -1)
                    dve.sem_inc(x1_ready, 1)
                    dve.sem_inc(hx_free, 1)
                    row_stats(1, x1[:])

            bodies(dve, body)


def split3(dve, chain_sem, x, parts, rest):
    dve.tensor_copy(parts[0], x).then_inc(chain_sem, 1)
    dve.wait_ge(chain_sem, 1)
    dve.sem_inc(chain_sem, -1)
    dve.tensor_tensor(rest, x, parts[0], ALU.subtract).then_inc(chain_sem, 1)
    dve.wait_ge(chain_sem, 1)
    dve.sem_inc(chain_sem, -1)
    dve.tensor_copy(parts[1], rest).then_inc(chain_sem, 1)
    dve.wait_ge(chain_sem, 1)
    dve.sem_inc(chain_sem, -1)
    dve.tensor_tensor(parts[2], rest, parts[1], ALU.subtract).then_inc(chain_sem, 1)
    dve.wait_ge(chain_sem, 1)
    dve.sem_inc(chain_sem, -1)


def leaky(dve, out, x):
    return dve.scalar_tensor_tensor(out=out, in0=x, scalar=SLOPE, in1=x, op0=ALU.mult, op1=ALU.max)


def edges1(nc, t, dram, sb, keep):
    smax = keep.sb("smax", [P, HEADS], F32)
    maxima = keep.sb("maxima", [P, CB, HEADS], F32)
    with ExitStack() as ctx:
        m = Memory(nc, ctx)
        acc, iota16, negbase, nodeid, ident, st = (
            sb["acc"], sb["iota16"], sb["negbase"], sb["nodeid"], sb["ident"], sb["st"])
        srcs = m.sb("a_srcs", [P, NCH], I32)
        dsts = m.sb("a_dsts", [P, NCH + CB], F32)
        far = m.sb("far", [P, NCH + CB], F32)
        idx = m.sb("a_idx", [P, RING, CB], I32)
        table = m.sb("table1", [1, 2, NBP + 4], I32)
        dstb = m.sb("dstb", [P, RING, BE], I32)
        trg = m.sb("trg", [TN, 3, NT, HEADS], BF16)
        rest = m.sb("rest", [TN, NT, HEADS], F32)
        rows = m.sb("a_rows", [P, RING, CB, TW], F32)
        hot_t = m.sb("hot_t", [TN, 3, BE], BF16)
        hot = m.sb("a_hot", [P, 3, CB, TN], F32)
        ht = m.sb("ht", [P, 2, CB, HEADS], F32)
        e = m.sb("e", [P, CB, HEADS], F32)
        c = m.sb("c", [P, CB, HEADS], F32)
        d = m.sb("d", [P, 2, CB, HEADS], F32)
        feat = m.sb("feat", [P, 2, CB, TW], F32)
        part = m.sb("part", [TN, HEADS], F32)
        smax_col = m.sb("smax_col", [HEADS, 1], F32)
        diag = m.sb("diag", [HEADS, HEADS], F32)
        ones = m.sb("a_ones", [HEADS, P], F32)
        ht_ps = [m.ps(f"ht{s}_ps", [P, CB, HEADS]) for s in range(3)]
        sum_ps = [m.ps(f"sum{s}_ps", [TN, TW]) for s in range(3)]

        ld_idx, ld_dst, ld_tab = m.sem("a_ld_idx"), m.sem("a_ld_dst"), m.sem("a_ld_tab")
        smax_in, smax_turned = m.sem("smax_in"), m.sem("smax_turned")
        diag_ready, smax_done = m.sem("diag_ready"), m.sem("smax_done")
        idx_ready = [m.sem(f"a_idx_ready{s}") for s in range(RING)]
        rows_ready = [m.sem(f"a_rows_ready{s}") for s in range(RING)]
        dstb_ready = [m.sem(f"dstb_ready{s}") for s in range(RING)]
        dstb_free = m.sem("dstb_free")
        hot_t_ready = m.sem("hot_t_ready")
        ht_done = m.sem("ht_done")
        xhot_t_ready = m.sem("xhot_t_ready")
        xht_done = m.sem("xht_done")
        hot_cleared = m.sem("hot_cleared")
        d_ready = m.sem("d_ready")
        p_ready = m.sem("p_ready")
        feat_ready = m.sem("feat_ready")
        sum_done = m.sem("a_sum_done")
        xhot_ready = m.sem("a_xhot_ready")
        xsum_done = m.sem("a_xsum_done")
        chain_sem = m.sem("a_chain")

        block = ctx.enter_context(nc.Block())

        @block.sync
        def _(sp):
            sp.dma_start(srcs[:], t["src_cols"]).then_inc(ld_idx, 16)
            sp.dma_start(table[:, :, 0:NBP + 1], dram["sched"][:, 0:NBP + 1].unsqueeze(0)).then_inc(ld_tab, 16)
            dst_rows = t["dst_flat"].rearrange("(b e) -> b e", e=BE)

            def load(b, s):
                sp.dma_start(dstb[:, s, :], dst_rows[bass.ds(b, 1)].broadcast_to([P, BE])).then_inc(dstb_ready[s], 16)

            for s in range(RING):
                load(s, s)
            with sp.Fori(0, NB // RING) as i:
                for u in range(RING):
                    sp.wait_ge(dstb_free, 1)
                    sp.sem_inc(dstb_free, -1)
                    load(RING * (i + 1) + u, u)

        @block.gpsimd
        def _(pool):
            pool.dma_start(dsts[:], t["dst_cols"]).then_inc(ld_dst, 16)
            with pool.Fori(0, NB // RING):
                for s in range(RING):
                    pool.wait_ge(idx_ready[s], 1)
                    pool.sem_inc(idx_ready[s], -1)
                    for k in range(CB):
                        pool.indirect_dma_start(
                            rows[:, s, k, :], None, dram["tab1"],
                            bass.IndirectOffsetOnAxis(ap=idx[:, s, k:k + 1], axis=0),
                        ).then_inc(rows_ready[s], 16)

        @block.scalar
        def _(act):
            with act.Fori(0, NB // RING):
                for u in range(RING):
                    s = u % 2
                    act.wait_ge(d_ready, 1)
                    act.sem_inc(d_ready, -1)
                    act.activation(feat[:, s, :, D:TW], d[:, s], ACT.Exp).then_inc(p_ready, 1)

        @block.tensor
        def _(pe):
            def targets(out, h, tile):
                for k in range(CB):
                    lhs = hot_t[:, h, k * P:(k + 1) * P]
                    for q in range(3):
                        ins = pe.matmul(out[:, k, :], lhs, trg[:, q, bass.ds(tile, 1), :].rearrange("p a c -> p (a c)"),
                                        start=(q == 0), stop=(q == 2))
                return ins

            def other_targets(lo, end):
                with pe.If(end > lo + 1):
                    pe.wait_ge(xhot_t_ready, 1)
                    pe.sem_inc(xhot_t_ready, -1)
                    targets(ht_ps[2], 2, end - 1).then_inc(xht_done, 1)
                    with pe.If(end > lo + 2):
                        with pe.Fori(lo + 1, end - 1) as x:
                            pe.wait_ge(xhot_t_ready, 1)
                            pe.sem_inc(xhot_t_ready, -1)
                            targets(ht_ps[2], 2, x).then_inc(xht_done, 1)

            def sums(out, h, s):
                for k in range(CB):
                    ins = pe.matmul(out[:], hot[:, h, k, :], feat[:, s, k, :], start=(k == 0), stop=(k == CB - 1))
                return ins

            def other_sums(s, lo, end):
                with pe.If(end > lo + 1):
                    with pe.Fori(lo + 1, end):
                        pe.wait_ge(xhot_ready, 1)
                        pe.sem_inc(xhot_ready, -1)
                        sums(sum_ps[2], 2, s).then_inc(xsum_done, 1)

            pe.wait_ge(smax_in, 1)
            pe.sem_inc(smax_in, -1)
            pe.transpose(sum_ps[0][0:HEADS, 0:TN], part[:], ident[0:TN, 0:TN]).then_inc(smax_turned, 1)
            pe.wait_ge(diag_ready, 1)
            pe.sem_inc(diag_ready, -1)
            pe.matmul(ht_ps[0][:, 0, :], ones[:], diag[:], start=True, stop=True).then_inc(smax_done, 1)
            pe.wait_ge(ld_tab, 16)
            lo, end = tiles_of(nc, PE, table, 0, 1)[0]
            pe.wait_ge(hot_t_ready, 1)
            pe.sem_inc(hot_t_ready, -1)
            targets(ht_ps[0], 0, lo).then_inc(ht_done, 1)
            other_targets(lo, end)
            pe.wait_ge(hot_t_ready, 1)
            pe.sem_inc(hot_t_ready, -1)
            targets(ht_ps[1], 1, tiles_of(nc, PE, table, 1, 1)[0][0]).then_inc(ht_done, 1)
            pe.wait_ge(hot_cleared, 1)
            pe.sem_inc(hot_cleared, -1)
            sums(sum_ps[1], 1, 1).then_inc(sum_done, 1)
            with pe.Fori(0, NB // RING) as i:
                tiles = tiles_of(nc, PE, table, RING * i - 1, RING + 3)
                for u in range(RING):
                    s = u % 2
                    pe.wait_ge(hot_t_ready, 1)
                    pe.sem_inc(hot_t_ready, -1)
                    targets(ht_ps[s], s, tiles[u + 3][0]).then_inc(ht_done, 1)
                    other_sums(1 - s, *tiles[u])
                    other_targets(*tiles[u + 2])
                    pe.wait_ge(feat_ready, 1)
                    pe.sem_inc(feat_ready, -1)
                    sums(sum_ps[s], s, s).then_inc(sum_done, 1)
            other_sums((NB - 1) % 2, *tiles_of(nc, PE, table, NB - 1, 1)[0])

        @block.vector
        def _(dve):
            def node_hot(slot, row, tile):
                return dve.tensor_scalar(hot_t[:, slot, :], dstb[0:TN, row, :], nodeid[0:TN, bass.ds(tile, 1)], None, ALU.is_equal)

            def first_targets(b, s):
                dve.wait_ge(ht_done, 1)
                dve.sem_inc(ht_done, -1)
                fars = far[:, bass.ds(CB * (b + 1), CB)].unsqueeze(2).broadcast_to([P, CB, HEADS])
                dve.tensor_tensor(ht[:, s], ht_ps[s][:], fars, ALU.add).then_inc(chain_sem, 1)
                dve.wait_ge(chain_sem, 1)
                dve.sem_inc(chain_sem, -1)

            def target_hot(row, x):
                node_hot(2, row, x).then_inc(xhot_t_ready, 1)

            def more_targets(s):
                dve.wait_ge(xht_done, 1)
                dve.sem_inc(xht_done, -1)
                dve.tensor_tensor(ht[:, s], ht[:, s], ht_ps[2][:], ALU.add).then_inc(chain_sem, 1)
                dve.wait_ge(chain_sem, 1)
                dve.sem_inc(chain_sem, -1)

            def logits(i, u, s):
                dve.wait_ge(rows_ready[u], 16 * CB * (i + 1))
                dve.tensor_tensor(e[:], rows[:, u, :, D:TW], ht[:, s], ALU.add)
                dve.tensor_tensor(c[:], ht[:, s], smax[:].unsqueeze(1).broadcast_to([P, CB, HEADS]), ALU.add).then_inc(chain_sem, 1)
                dve.wait_ge(chain_sem, 1)
                dve.sem_inc(chain_sem, -1)
                leaky(dve, e[:], e[:])
                leaky(dve, c[:], c[:]).then_inc(chain_sem, 1)
                dve.wait_ge(chain_sem, 1)
                dve.sem_inc(chain_sem, -1)
                dve.tensor_tensor(d[:, s], e[:], c[:], ALU.subtract).then_inc(d_ready, 1)
                dve.tensor_tensor(maxima[:], maxima[:], e[:], ALU.max).then_inc(chain_sem, 1)

            def weighted(u, s):
                dve.wait_ge(p_ready, 1)
                dve.sem_inc(p_ready, -1)
                p = feat[:, s, :, D:TW].unsqueeze(3).broadcast_to([P, CB, HEADS, HD])
                dve.tensor_tensor(feat[:, s, :, 0:D].rearrange("p k (h f) -> p k h f", h=HEADS),
                                  rows[:, u, :, 0:D].rearrange("p k (h f) -> p k h f", h=HEADS), p, ALU.mult).then_inc(feat_ready, 1)

            def add(slot, tile):
                a = acc[0:TN, bass.ds(tile, 1), 0:TW].rearrange("p a c -> p (a c)")
                dve.tensor_tensor(a, a, sum_ps[slot][:], ALU.add).then_inc(chain_sem, 1)
                dve.wait_ge(chain_sem, 1)
                dve.sem_inc(chain_sem, -1)

            def extra_hot(b, x):
                one_hot(dve, hot[:, 2], iota16, dsts, negbase, b, x).then_inc(xhot_ready, 1)

            def add_extra(x):
                dve.wait_ge(xsum_done, 1)
                dve.sem_inc(xsum_done, -1)
                add(2, x)

            def middle(b, u, s, lo, end):
                with dve.If(end > lo + 1):
                    extra_hot(b - 1, end - 1)
                    first_targets(b + 1, 1 - s)
                    weighted(u, s)
                    add_extra(end - 1)
                    with dve.If(end > lo + 2):
                        with dve.Fori(lo + 1, end - 1) as x:
                            extra_hot(b - 1, x)
                            add_extra(x)
                with dve.Else():
                    first_targets(b + 1, 1 - s)
                    weighted(u, s)

            def last_part(b, s, row, before, lo, end):
                with dve.If(end > lo + 1):
                    target_hot(row, end - 1)
                    dve.wait_ge(sum_done, 1)
                    dve.sem_inc(sum_done, -1)
                    add(1 - s, before)
                    more_targets(1 - s)
                    with dve.If(end > lo + 2):
                        with dve.Fori(lo + 1, end - 1) as x:
                            target_hot(row, x)
                            more_targets(1 - s)
                with dve.Else():
                    dve.wait_ge(sum_done, 1)
                    dve.sem_inc(sum_done, -1)
                    add(1 - s, before)
                dve.sem_inc(dstb_free, 1)

            def indices(b, s):
                dve.tensor_copy(idx[:, s, :], srcs[:, bass.ds(CB * b, CB)]).then_inc(idx_ready[s], 1)

            dve.wait_ge(ld_idx, 16)
            for b in range(RING):
                indices(b, b)
            dve.tensor_reduce(part[:], st[0:TN, :, 0:HEADS].rearrange("p t h -> p h t"), AX, ALU.max).then_inc(chain_sem, 1)
            dve.wait_ge(chain_sem, 1)
            dve.sem_inc(chain_sem, -1)
            dve.sem_inc(smax_in, 1)
            dve.memset(ones[:], 1.0).then_inc(chain_sem, 1)
            dve.wait_ge(chain_sem, 1)
            dve.sem_inc(chain_sem, -1)
            dve.memset(maxima[:], FAR).then_inc(chain_sem, 1)
            dve.wait_ge(chain_sem, 1)
            dve.sem_inc(chain_sem, -1)
            dve.memset(hot[:, 1:2], 0.0)
            dve.memset(feat[:, 1], 0.0).then_inc(chain_sem, 1)
            dve.wait_ge(chain_sem, 1)
            dve.sem_inc(chain_sem, -1)
            dve.sem_inc(hot_cleared, 1)
            dve.wait_ge(smax_turned, 1)
            dve.sem_inc(smax_turned, -1)
            dve.tensor_reduce(smax_col[:], sum_ps[0][0:HEADS, 0:TN], AX, ALU.max).then_inc(chain_sem, 1)
            dve.wait_ge(chain_sem, 1)
            dve.sem_inc(chain_sem, -1)
            dve.tensor_scalar(diag[:], ident[0:HEADS, 0:HEADS], smax_col[:], None, ALU.mult).then_inc(chain_sem, 1)
            dve.wait_ge(chain_sem, 1)
            dve.sem_inc(chain_sem, -1)
            dve.sem_inc(diag_ready, 1)
            split3(dve, chain_sem, st[0:TN, :, HEADS:2 * HEADS], [trg[:, q] for q in range(3)], rest[:])
            dve.wait_ge(smax_done, 1)
            dve.sem_inc(smax_done, -1)
            dve.tensor_copy(smax[:], ht_ps[0][:, 0, :]).then_inc(chain_sem, 1)
            dve.wait_ge(chain_sem, 1)
            dve.sem_inc(chain_sem, -1)
            dve.wait_ge(ld_dst, 16)
            dve.wait_ge(ld_tab, 16)
            dve.tensor_scalar(far[:], dsts[:], float(N), FAR, ALU.is_ge, ALU.mult).then_inc(chain_sem, 1)
            dve.wait_ge(chain_sem, 1)
            dve.sem_inc(chain_sem, -1)
            lo, end = tiles_of(nc, DVE, table, 0, 1)[0]
            dve.wait_ge(dstb_ready[0], 16)
            dve.sem_inc(dstb_ready[0], -16)
            node_hot(0, 0, lo).then_inc(hot_t_ready, 1)
            dve.wait_ge(dstb_ready[1], 16)
            dve.sem_inc(dstb_ready[1], -16)
            node_hot(1, 1, tiles_of(nc, DVE, table, 1, 1)[0][0]).then_inc(hot_t_ready, 1)
            first_targets(0, 0)
            with dve.If(end > lo + 1):
                target_hot(0, end - 1)
                more_targets(0)
                with dve.If(end > lo + 2):
                    with dve.Fori(lo + 1, end - 1) as x:
                        target_hot(0, x)
                        more_targets(0)
            dve.sem_inc(dstb_free, 1)
            with dve.Fori(0, NB // RING) as i:
                tiles = tiles_of(nc, DVE, table, RING * i - 1, RING + 3)
                for u in range(RING):
                    b, s = RING * i + u, u % 2
                    logits(i, u, s)
                    dve.wait_ge(dstb_ready[(u + 2) % RING], 16)
                    dve.sem_inc(dstb_ready[(u + 2) % RING], -16)
                    node_hot(s, (u + 2) % RING, tiles[u + 3][0]).then_inc(hot_t_ready, 1)
                    one_hot(dve, hot[:, s], iota16, dsts, negbase, b, tiles[u + 1][0])
                    dve.wait_ge(chain_sem, 1)
                    dve.sem_inc(chain_sem, -1)
                    middle(b, u, s, *tiles[u])
                    indices(b + RING, u)
                    last_part(b, s, (u + 1) % RING, tiles[u][0], *tiles[u + 2])
            b, s = NB - 1, (NB - 1) % 2
            lo, end = tiles_of(nc, DVE, table, b, 1)[0]
            dve.wait_ge(sum_done, 1)
            dve.sem_inc(sum_done, -1)
            add(s, lo)
            with dve.If(end > lo + 1):
                with dve.Fori(lo + 1, end) as x:
                    extra_hot(b, x)
                    add_extra(x)
            dve.wait_ge(dstb_ready[(NB + 2) % RING], 16)
            dve.sem_inc(dstb_ready[(NB + 2) % RING], -16)
            dve.wait_ge(dstb_ready[(NB + 3) % RING], 16)
            dve.sem_inc(dstb_ready[(NB + 3) % RING], -16)
    return smax, maxima


def finish(nc, t, dram, sb, smax, maxima, out):
    with ExitStack() as ctx:
        m = Memory(nc, ctx)
        acc, ident, st = sb["acc"], sb["ident"], sb["st"]
        e = m.sb("f_e", [TN, NT, HEADS], F32)
        c = m.sb("f_c", [TN, NT, HEADS], F32)
        p = m.sb("f_p", [TN, NT, HEADS], F32)
        g = m.sb("f_g", [TN, NT, HEADS], F32)
        mx = m.sb("mx", [P, 2], F32)
        mrow = m.sb("mrow", [1, 1], F32)
        ones = m.sb("f_ones", [1, P], F32)
        top = m.sb("top", [P, 1], F32)
        FB = 5
        hp = m.sb("hp", [TN, 2, FB, D], F32)
        x1 = m.sb("f_x1", [TN, 2, FB, D], F32)
        turn_ps = m.ps("turn_ps", [1, P])
        top_ps = m.ps("top_ps", [P, 1])

        loaded = [m.sem(f"f_loaded{s}") for s in range(2)]
        out_ready = m.sem("out_ready")
        out_stored = [m.sem(f"out_stored{s}") for s in range(2)]
        mx_ready, turned, mrow_ready, top_done = m.sem("mx_ready"), m.sem("turned"), m.sem("mrow_ready"), m.sem("top_done")
        exp_in, exp_ready = m.sem("exp_in"), m.sem("exp_ready")
        coef_ready, self_ready = m.sem("f_coef_ready"), m.sem("self_ready")
        chain_sem = m.sem("f_chain")

        block = ctx.enter_context(nc.Block())

        @block.sync
        def _(sp):
            x1_v = dram["x1"].rearrange("(t p) c -> p t c", p=TN)
            hp_v = dram["tab1"].rearrange("(t p) c -> p t c", p=TN)
            out_v = out.rearrange("(t p) c -> p t c", p=TN)

            def load(i, s):
                sp.dma_start(hp[:, s], hp_v[:, bass.ds(i * FB, FB), 0:D]).then_inc(loaded[s], 16)
                sp.dma_start(x1[:, s], x1_v[:, bass.ds(i * FB, FB), :]).then_inc(loaded[s], 16)

            def store(i, s):
                sp.wait_ge(out_ready, 1)
                sp.sem_inc(out_ready, -1)
                sp.dma_start(out_v[:, bass.ds(i * FB, FB), :], acc[0:TN, bass.ds(i * FB, FB), 0:D]).then_inc(out_stored[s], 16)

            load(0, 0)
            load(1, 1)
            last = NT // FB // 2 - 1
            with sp.Fori(0, last) as i:
                for s in range(2):
                    store(2 * i + s, s)
                    load(2 * i + s + 2, s)
            for s in range(2):
                store(2 * last + s, s)
                sp.wait_ge(out_stored[s], 16 * (last + 1))

        @block.scalar
        def _(act):
            act.wait_ge(exp_in, 1)
            act.sem_inc(exp_in, -1)
            act.activation(p[:], e[:], ACT.Exp).then_inc(exp_ready, 1)
            act.wait_ge(exp_in, 1)
            act.sem_inc(exp_in, -1)
            act.activation(g[:], c[:], ACT.Exp).then_inc(exp_ready, 1)

        @block.tensor
        def _(pe):
            pe.wait_ge(mx_ready, 1)
            pe.sem_inc(mx_ready, -1)
            pe.transpose(turn_ps[:], mx[:, 0:1], ident[:]).then_inc(turned, 1)
            pe.wait_ge(mrow_ready, 1)
            pe.sem_inc(mrow_ready, -1)
            pe.matmul(top_ps[:], ones[:], mrow[:], start=True, stop=True).then_inc(top_done, 1)

        @block.gpsimd
        def _(pool):
            pool.wait_ge(coef_ready, 1)
            with pool.Fori(0, NT // FB // 2) as i:
                for s in range(2):
                    pool.wait_ge(loaded[s], 32)
                    pool.sem_inc(loaded[s], -32)
                    h = hp[:, s].rearrange("p t (h f) -> p t h f", h=HEADS)
                    pool.tensor_tensor(h, h, p[:, bass.ds((2 * i + s) * FB, FB), :].unsqueeze(3).broadcast_to([TN, FB, HEADS, HD]),
                                       ALU.mult).then_inc(self_ready, 1)

        @block.vector
        def _(dve):
            dve.memset(ones[:], 1.0).then_inc(chain_sem, 1)
            dve.wait_ge(chain_sem, 1)
            dve.sem_inc(chain_sem, -1)
            dve.tensor_tensor(e[:], st[0:TN, :, 0:HEADS], st[0:TN, :, HEADS:2 * HEADS], ALU.add).then_inc(chain_sem, 1)
            dve.wait_ge(chain_sem, 1)
            dve.sem_inc(chain_sem, -1)
            leaky(dve, e[:], e[:]).then_inc(chain_sem, 1)
            dve.wait_ge(chain_sem, 1)
            dve.sem_inc(chain_sem, -1)
            dve.tensor_tensor(c[:], st[0:TN, :, HEADS:2 * HEADS], smax[0:TN, :].unsqueeze(1).broadcast_to([TN, NT, HEADS]), ALU.add).then_inc(chain_sem, 1)
            dve.wait_ge(chain_sem, 1)
            dve.sem_inc(chain_sem, -1)
            leaky(dve, c[:], c[:]).then_inc(chain_sem, 1)
            dve.wait_ge(chain_sem, 1)
            dve.sem_inc(chain_sem, -1)
            dve.tensor_reduce(mx[:, 0:1], maxima[:].rearrange("p k h -> p (k h)"), AX, ALU.max).then_inc(chain_sem, 1)
            dve.wait_ge(chain_sem, 1)
            dve.sem_inc(chain_sem, -1)
            dve.tensor_reduce(mx[0:TN, 1:2], e[:].rearrange("p t h -> p (t h)"), AX, ALU.max).then_inc(chain_sem, 1)
            dve.wait_ge(chain_sem, 1)
            dve.sem_inc(chain_sem, -1)
            dve.tensor_tensor(mx[0:TN, 0:1], mx[0:TN, 0:1], mx[0:TN, 1:2], ALU.max).then_inc(chain_sem, 1)
            dve.wait_ge(chain_sem, 1)
            dve.sem_inc(chain_sem, -1)
            dve.sem_inc(mx_ready, 1)
            dve.tensor_tensor(e[:], e[:], c[:], ALU.subtract).then_inc(chain_sem, 1)
            dve.wait_ge(chain_sem, 1)
            dve.sem_inc(chain_sem, -1)
            dve.sem_inc(exp_in, 1)
            dve.wait_ge(turned, 1)
            dve.sem_inc(turned, -1)
            dve.tensor_reduce(mrow[:], turn_ps[:], AX, ALU.max).then_inc(mrow_ready, 1)
            dve.wait_ge(top_done, 1)
            dve.sem_inc(top_done, -1)
            dve.tensor_copy(top[:], top_ps[:]).then_inc(chain_sem, 1)
            dve.wait_ge(chain_sem, 1)
            dve.sem_inc(chain_sem, -1)
            dve.tensor_scalar(c[:], c[:], top[0:TN, :], -1.0, ALU.subtract, ALU.mult).then_inc(chain_sem, 1)
            dve.wait_ge(chain_sem, 1)
            dve.sem_inc(chain_sem, -1)
            dve.tensor_scalar(c[:], c[:], CAP, None, ALU.min).then_inc(chain_sem, 1)
            dve.wait_ge(chain_sem, 1)
            dve.sem_inc(chain_sem, -1)
            dve.sem_inc(exp_in, 1)
            dve.wait_ge(exp_ready, 2)
            dve.sem_inc(exp_ready, -2)
            dve.scalar_tensor_tensor(out=g[:], in0=g[:], scalar=GUARD, in1=p[:], op0=ALU.mult, op1=ALU.add).then_inc(chain_sem, 1)
            dve.wait_ge(chain_sem, 1)
            dve.sem_inc(chain_sem, -1)
            dve.tensor_tensor(g[:], g[:], acc[0:TN, :, D:TW], ALU.add).then_inc(chain_sem, 1)
            dve.wait_ge(chain_sem, 1)
            dve.sem_inc(chain_sem, -1)
            dve.reciprocal(g[:], g[:]).then_inc(chain_sem, 1)
            dve.wait_ge(chain_sem, 1)
            dve.sem_inc(chain_sem, -1)
            dve.tensor_tensor(p[:], p[:], g[:], ALU.mult).then_inc(chain_sem, 1)
            dve.wait_ge(chain_sem, 1)
            dve.sem_inc(chain_sem, -1)
            dve.sem_inc(coef_ready, 1)
            with dve.Fori(0, NT // FB // 2) as i:
                for s in range(2):
                    tiles = bass.ds((2 * i + s) * FB, FB)
                    a = acc[0:TN, tiles, 0:D]
                    a4 = a.rearrange("p t (h f) -> p t h f", h=HEADS)
                    dve.tensor_tensor(a4, a4, g[:, tiles, :].unsqueeze(3).broadcast_to([TN, FB, HEADS, HD]), ALU.mult).then_inc(chain_sem, 1)
                    dve.wait_ge(chain_sem, 1)
                    dve.sem_inc(chain_sem, -1)
                    dve.wait_ge(self_ready, 1)
                    dve.sem_inc(self_ready, -1)
                    dve.tensor_tensor(a, a, x1[:, s], ALU.add).then_inc(chain_sem, 1)
                    dve.wait_ge(chain_sem, 1)
                    dve.sem_inc(chain_sem, -1)
                    dve.tensor_tensor(a, a, hp[:, s], ALU.add).then_inc(out_ready, 1)


_PLAIN = ["x", "L0_gnn_eps", "L0_gnn_ee_w1", "L0_gnn_ee_b1", "L0_gnn_ee_w2", "L0_gnn_ee_b2", "L0_gnn_w1",
          "L0_gnn_w2", "L0_gnn_w3", "L0_gnn_b3", "L0_gnn_bn_g", "L0_gnn_bn_b", "L1_gnn_W", "L1_gnn_b",
          "L1_gnn_a_src", "L1_gnn_a_trg"]
_COLS = ["L0_gnn_b1", "L0_gnn_g1", "L0_gnn_be1", "L0_gnn_b2", "L0_gnn_g2", "L0_gnn_be2"]


def kernel(**inputs):
    import concourse.bacc as bacc
    import numpy as np
    from concourse.bass_utils import run_bass_kernel_spmd

    a = {n: np.ascontiguousarray(inputs[n]) for n in _PLAIN}
    a["L0_gnn_eps"] = a["L0_gnn_eps"].reshape(1)
    for n in _COLS:
        a[n + "_cols"] = np.ascontiguousarray(np.asarray(inputs[n]).reshape(KH, P).T)
    a["L0_gnn_ee_b1_cols"] = np.ascontiguousarray(np.asarray(inputs["L0_gnn_ee_b1"]).reshape(KD, P).T)
    a["L1_gnn_b_cols"] = np.ascontiguousarray(np.asarray(inputs["L1_gnn_b"]).reshape(KD, P).T)
    a["L1_gnn_W_t"] = np.ascontiguousarray(np.asarray(inputs["L1_gnn_W"]).T)
    pad = NBP * BE - E
    src = np.concatenate([np.asarray(inputs["src"]), np.zeros(pad, np.int32)])
    dst = np.concatenate([np.asarray(inputs["dst"]), np.full(pad, N, np.int32)])
    a["src_cols"] = np.ascontiguousarray(src.reshape(NCH, P).T)
    a["dst_cols"] = np.ascontiguousarray(np.concatenate([np.full(BE, N, np.int32), dst]).reshape(NCH + CB, P).T)
    a["dst_flat"] = dst
    ea = np.concatenate([np.asarray(inputs["edge_attr_64"]), np.zeros((pad, ED), np.float32)])
    a["edge_t"] = np.ascontiguousarray(ea.reshape(NBP, BE, ED).transpose(0, 2, 1))

    nc = bacc.Bacc("TRN2", target_bir_lowering=False, num_devices=1)
    t = {n: nc.dram_tensor(n, v.shape, mybir.dt.from_np(v.dtype), kind="ExternalInput").ap() for n, v in a.items()}
    out = nc.dram_tensor("out", (N, D), F32, kind="ExternalOutput").ap()
    build(nc, t, out)
    r = run_bass_kernel_spmd(nc, [a], core_ids=[0])
    return r.results[0]["out"]
```

```python
from contextlib import ExitStack

import concourse.bass as bass
from concourse import mybir

F32, F16, I32, I16 = mybir.dt.float32, mybir.dt.float16, mybir.dt.int32, mybir.dt.int16
BF16 = mybir.dt.bfloat16
ALU = mybir.AluOpType
ACT = mybir.ActivationFunctionType
AX = mybir.AxisListType.X
PE, DVE = mybir.EngineType.PE, mybir.EngineType.DVE

P = 128
N, D, E, ED, H = 6250, 256, 100000, 64, 1024
TN = 125
NT = N // TN
CB = 4
BE = CB * P
RING = 4
NB = -(-E // (BE * RING)) * RING
NBP = NB + RING
NCH = NBP * CB
KH, KD = H // P, D // P
HEADS, HD = 8, 32
TW = D + HEADS
AW = D + 2 * HEADS
LN_EPS = 1e-5
SLOPE = 0.2
GUARD = 1e-10
WS = 64.0
PG = 5
XL = 10
FAR = -1.0e30
CAP = 87.0


def build(nc, t, out):
    with ExitStack() as ctx:
        keep = Memory(nc, ctx)
        dram = {
            "h0": nc.dram_tensor("h0_scratch", (N, D), F32, kind="Internal").ap(),
            "tab0": nc.dram_tensor("tab0_scratch", (N, 2 * D), F16, kind="Internal").ap(),
            "tab1": nc.dram_tensor("tab1_scratch", (N, TW), F32, kind="Internal").ap(),
            "x1": nc.dram_tensor("x1_scratch", (N, D), F32, kind="Internal").ap(),
            "sched": nc.dram_tensor("sched_scratch", (2, NBP + 4), I32, kind="Internal").ap(),
        }
        sb = {}
        for name, shape, dt in [
            ("acc", [P, NT, 2 * D], F32),
            ("ident", [P, P], F32), ("iota16", [P, TN], F16),
            ("negbase", [P, NT], F32), ("nodeid", [P, NT], F32),
            ("st", [P, NT, 2 * HEADS], F32),
            ("epscol", [P, 1], F32), ("lneps", [P, 1], F32),
        ]:
            sb[name] = keep.sb(name, shape, dt)
        with ExitStack() as first:
            layer0 = Memory(nc, first)
            for name, shape, dt in [
                ("w1h", [P, KD, H], F16), ("w1l", [P, KD, H], F16),
                ("w2h", [P, KH, H], F16), ("w2l", [P, KH, H], F16),
                ("w3h", [P, KH, D], F16), ("w3l", [P, KH, D], F16),
            ]:
                sb[name] = layer0.sb(name, shape, dt)
            with ExitStack() as edge_mlp:
                for name, shape, dt in [("ewa", [P, D], F16), ("ewb", [ED + 2, D], F16)]:
                    sb[name] = Memory(nc, edge_mlp).sb(name, shape, dt)
                stale = prepare(nc, t, dram, sb)
                edges0(nc, t, dram, sb)
            nodes(nc, t, dram, sb, stale)
        smax, maxima, x1_tail = edges1(nc, t, dram, sb, keep)
        finish(nc, t, dram, sb, smax, maxima, x1_tail, out)


class Memory:

    def __init__(self, nc, ctx):
        self.nc, self.ctx, self.sems = nc, ctx, []

    def sb(self, name, shape, dt):
        return self.ctx.enter_context(self.nc.sbuf_tensor(name, shape, dt))

    def ps(self, name, shape, dt=F32):
        return self.ctx.enter_context(self.nc.psum_tensor(name, shape, dt))

    def sem(self, name):
        self.sems.append(self.ctx.enter_context(self.nc.semaphore(name)))
        return self.sems[-1]


def prepare(nc, t, dram, sb):
    with ExitStack() as ctx:
        m = Memory(nc, ctx)
        acc = sb["acc"]
        flat = acc[:].rearrange("p t c -> p (t c)")
        xall = flat[0:TN, 0:NT * D].rearrange("p (t c) -> p t c", c=D)
        o = NT * D
        w1r = flat[:, o:o + KD * H].rearrange("p (k n) -> p k n", n=H)
        w2r = flat[:, o + KD * H:o + (KD + KH) * H].rearrange("p (k n) -> p k n", n=H)
        o += (KD + KH) * H
        w3r = flat[:, o:o + KH * D].rearrange("p (k n) -> p k n", n=D)

        icol = m.sb("icol", [P, P], I32)
        idiag = m.sb("idiag", [P, P], I32)
        ineg = m.sb("ineg", [P, NT], I32)
        inode = m.sb("inode", [P, NT], I32)
        ithr = m.sb("ithr", [P, NT - 1], I32)
        thr = m.sb("thr", [P, NT - 1], F32)
        b2bc = m.sb("p_b2bc", [TN, D], F32)
        er = m.sb("er", [P, D], F32)
        ebr = m.sb("ebr", [ED + 2, D], F32)
        ebh = m.sb("ebh", [ED + 2, D], F16)
        stat = m.sb("stat", [TN, NT, 6], F32)
        mv = m.sb("mv", [TN, NT, 2], F32)
        rstd = m.sb("rstd", [TN, NT], F32)
        nmr = m.sb("nmr", [TN, NT], F32)
        h0 = m.sb("h0", [TN, 2, PG, D], F32)
        tb = m.sb("tb", [TN, 2, PG, 2 * D], F16)
        wsum = m.sb("wsum", [P, KD + KH], F32)
        wneg = m.sb("wneg", [P, KD + KH], F32)
        half = NBP // 2
        drow = m.sb("drow", [half, 2, BE], I32)
        ext = m.sb("ext", [half, 4], F32)
        cmp_ = m.sb("cmp_", [half, 4, NT - 1], F32)
        tile = m.sb("tile", [half, 4], F32)
        sched_sb = m.sb("sched_sb", [half, 2, 2], I32)

        ld_x = [m.sem(f"ld_x{i}") for i in range(NT // XL)]
        ld_w = m.sem("ld_w")
        ld_small = m.sem("ld_small")
        ld_dst = m.sem("ld_dst")
        iotas = m.sem("iotas")
        eb_split = m.sem("eb_split")
        var_ready = m.sem("var_ready")
        sd_ready = m.sem("sd_ready")
        coef_ready = m.sem("coef_ready")
        h0_ready = m.sem("h0_ready")
        t_ready = m.sem("t_ready")
        hi_ready = m.sem("hi_ready")
        tb_ready = m.sem("tb_ready")
        h0_stored = [m.sem(f"h0_stored{s}") for s in range(2)]
        tb_stored = [m.sem(f"tb_stored{s}") for s in range(2)]
        centred = m.sem("centred")
        norm_ready = m.sem("norm_ready")
        wneg_ready = m.sem("wneg_ready")
        whi_ready = m.sem("whi_ready")
        act_chain = m.sem("p_act_chain")
        dve_chain = m.sem("p_dve_chain")
        sched_ready = m.sem("sched_ready")
        stored = m.sem("p_stored")
        ewb_done = m.sem("ewb_done")
        x_v = t["x"].rearrange("(p t) c -> p t c", t=NT)
        h0_v = dram["h0"].rearrange("(p t) c -> p t c", t=NT)
        tb_v = dram["tab0"].rearrange("(p t) c -> p t c", t=NT)
        splits = ([(w1r[:, k, :], sb["w1h"][:, k, :], sb["w1l"][:, k, :]) for k in range(KD)]
                  + [(w2r[:, k, :], sb["w2h"][:, k, :], sb["w2l"][:, k, :]) for k in range(KH)])
        w3s = (w3r[:, :, :], sb["w3h"][:, :, :], sb["w3l"][:, :, :])

        block = ctx.enter_context(nc.Block())

        @block.sync
        def _(sp):
            for i in range(NT // XL):
                sp.dma_start(xall[:, i * XL:(i + 1) * XL, :], x_v[:, i * XL:(i + 1) * XL, :]).then_inc(ld_x[i], 16)
            sp.dma_start(drow[:], t["dst_flat"].rearrange("(p j e) -> p j e", p=half, j=2)).then_inc(ld_dst, 16)
            sp.dma_start(w1r, t["L0_gnn_w1"].rearrange("(k p) n -> p k n", p=P)).then_inc(ld_w, 16)
            sp.dma_start(w2r, t["L0_gnn_w2"].rearrange("(k p) n -> p k n", p=P)).then_inc(ld_w, 16)
            sp.dma_start(w3r, t["L0_gnn_w3"].rearrange("(k p) n -> p k n", p=P)).then_inc(ld_w, 16)
            with sp.Fori(0, NT // PG // 2) as i:
                for u in range(2):
                    tiles = bass.ds((2 * i + u) * PG, PG)
                    sp.wait_ge(h0_ready, 1)
                    sp.sem_inc(h0_ready, -1)
                    sp.dma_start(h0_v[:, tiles, :], h0[:, u]).then_inc(h0_stored[u], 16)
                    sp.wait_ge(tb_ready, 1)
                    sp.sem_inc(tb_ready, -1)
                    sp.dma_start(tb_v[:, tiles, :], tb[:, u]).then_inc(tb_stored[u], 16)
            sp.wait_ge(sched_ready, 1)
            sp.sem_inc(sched_ready, -1)
            for part in range(2):
                row = dram["sched"][part]
                sp.dma_start(row[1:NBP + 1].rearrange("(p j) -> p j", j=2), sched_sb[:, part, :]).then_inc(stored, 16)
                sp.dma_start(row[0:1].unsqueeze(0), sched_sb[0:1, part, 0:1]).then_inc(stored, 16)
            sp.wait_ge(stored, 64)
            for u in range(2):
                sp.wait_ge(h0_stored[u], 16)
                sp.wait_ge(tb_stored[u], 16)

        @block.gpsimd
        def _(pool):
            pool.iota(icol[:], [[1, P]], base=0, channel_multiplier=0).then_inc(iotas, 1)
            pool.iota(idiag[:], [[1, P]], base=0, channel_multiplier=-1).then_inc(iotas, 1)
            pool.iota(ineg[:], [[-TN, NT]], base=0, channel_multiplier=0).then_inc(iotas, 1)
            pool.iota(inode[:], [[TN, NT]], base=0, channel_multiplier=1).then_inc(iotas, 1)
            pool.iota(ithr[:], [[TN, NT - 1]], base=TN, channel_multiplier=0).then_inc(iotas, 1)
            pool.wait_ge(wneg_ready, 1)
            for k in range(KD + KH // 2, KD + KH):
                raw = splits[k][0]
                pool.tensor_scalar(raw, raw, WS, wneg[:, k:k + 1], ALU.mult, ALU.add).then_inc(centred, 1)
            pool.memset(acc[:, 0:NT // 2, :], 0.0)

        @block.scalar
        def _(act):
            act.dma_start(b2bc[:], t["L0_gnn_ee_b2"].partition_broadcast(TN)).then_inc(ld_small, 16)
            act.dma_start(er[0:ED, :], t["L0_gnn_ee_w1"]).then_inc(ld_small, 16)
            act.dma_start(er[ED:2 * ED, :], t["L0_gnn_ee_w1"]).then_inc(ld_small, 16)
            act.dma_start(ebr[0:ED, :], t["L0_gnn_ee_w1"]).then_inc(ld_small, 16)
            act.dma_start(ebr[ED:ED + 2, :], t["L0_gnn_ee_b1"].partition_broadcast(2)).then_inc(ld_small, 16)
            act.dma_start(sb["epscol"][:], t["L0_gnn_eps"].partition_broadcast(P)).then_inc(ld_small, 16)
            def normalised(i, u):
                act.wait_ge(h0_stored[u], 16)
                act.sem_inc(h0_stored[u], -16)
                for j in range(PG):
                    k = bass.ds(i * PG + j, 1)
                    ins = act.activation(h0[:, u, j, :], xall[:, k, :].rearrange("p a c -> p (a c)"), ACT.Relu,
                                         bias=nmr[:, k], scale=rstd[:, k])
                ins.then_inc(act_chain, 1)
                act.wait_ge(act_chain, 1)
                act.sem_inc(act_chain, -1)
                act.sem_inc(h0_ready, 1)
                act.sem_inc(norm_ready, 1)

            def high(i, u):
                act.wait_ge(t_ready, 1)
                act.sem_inc(t_ready, -1)
                act.wait_ge(tb_stored[u], 16)
                act.sem_inc(tb_stored[u], -16)
                act.activation(tb[:, u, :, 0:D], xall[:, bass.ds(i * PG, PG), :], ACT.Copy).then_inc(hi_ready, 1)

            for u in range(2):
                act.sem_inc(h0_stored[u], 16)
                act.sem_inc(tb_stored[u], 16)
            act.wait_ge(var_ready, 1)
            act.sem_inc(var_ready, -1)
            act.activation(rstd[:], mv[:, :, 1], ACT.Sqrt, bias=sb["lneps"][0:TN, :]).then_inc(sd_ready, 1)
            act.wait_ge(coef_ready, 1)
            act.sem_inc(coef_ready, -1)
            last = NT // PG - 1
            normalised(0, 0)
            with act.Fori(0, (last - 1) // 2) as i:
                for u in range(2):
                    normalised(2 * i + u + 1, 1 - u)
                    high(2 * i + u, u)
            normalised(last, last % 2)
            high(last - 1, (last - 1) % 2)
            high(last, last % 2)
            act.wait_ge(ld_w, 48)
            act.activation(w3s[0], w3s[0], ACT.Copy, scale=WS).then_inc(act_chain, 1)
            act.wait_ge(wneg_ready, 1)
            act.sem_inc(wneg_ready, -1)
            for k, (raw, _, _) in enumerate(splits[:KD + KH // 2]):
                act.activation(raw, raw, ACT.Identity, bias=wneg[:, k:k + 1], scale=WS).then_inc(act_chain, 1)
            act.wait_ge(act_chain, KD + KH // 2 + 1)
            act.sem_inc(act_chain, -(KD + KH // 2 + 1))
            act.activation(w3s[1], w3s[0], ACT.Copy).then_inc(whi_ready, 1)
            for k, (raw, hi, _) in enumerate(splits):
                if k >= KD + KH // 2:
                    act.wait_ge(centred, 1)
                    act.sem_inc(centred, -1)
                act.activation(hi, raw, ACT.Copy).then_inc(whi_ready, 1)
            act.wait_ge(eb_split, 1)
            act.sem_inc(eb_split, -1)
            act.dma_start(sb["ewb"][ED:ED + 1, :], ebh[ED:ED + 1, :]).then_inc(ewb_done, 16)
            act.wait_ge(ewb_done, 16)

        @block.vector
        def _(dve):
            dve.memset(sb["lneps"][:], LN_EPS).then_inc(dve_chain, 1)
            dve.wait_ge(dve_chain, 1)
            dve.sem_inc(dve_chain, -1)
            dve.wait_ge(iotas, 5)
            dve.sem_inc(iotas, -5)
            dve.tensor_copy(sb["iota16"][:], icol[:, 0:TN]).then_inc(dve_chain, 1)
            dve.wait_ge(dve_chain, 1)
            dve.sem_inc(dve_chain, -1)
            dve.tensor_copy(sb["negbase"][:], ineg[:]).then_inc(dve_chain, 1)
            dve.wait_ge(dve_chain, 1)
            dve.sem_inc(dve_chain, -1)
            dve.tensor_copy(sb["nodeid"][:], inode[:]).then_inc(dve_chain, 1)
            dve.wait_ge(dve_chain, 1)
            dve.sem_inc(dve_chain, -1)
            dve.tensor_copy(thr[:], ithr[:]).then_inc(dve_chain, 1)
            dve.wait_ge(dve_chain, 1)
            dve.sem_inc(dve_chain, -1)
            dve.tensor_scalar(sb["ident"][:], idiag[:], 0.0, None, ALU.is_equal).then_inc(dve_chain, 1)
            dve.wait_ge(dve_chain, 1)
            dve.sem_inc(dve_chain, -1)
            for step in range(NT // XL):
                dve.wait_ge(ld_x[step], 16)
                for i in range(step * XL, (step + 1) * XL):
                    dve.bn_stats(stat[:, i, :], xall[:, i, :]).then_inc(dve_chain, 1)
                dve.wait_ge(dve_chain, XL)
                dve.sem_inc(dve_chain, -XL)
                for i in range(step * XL, (step + 1) * XL):
                    ins = dve.bn_aggr(mv[:, i, :], stat[:, i, :])
            ins.then_inc(var_ready, 1)
            dve.wait_ge(sd_ready, 1)
            dve.sem_inc(sd_ready, -1)
            dve.reciprocal(rstd[:], rstd[:]).then_inc(dve_chain, 1)
            dve.wait_ge(dve_chain, 1)
            dve.sem_inc(dve_chain, -1)
            dve.scalar_tensor_tensor(out=nmr[:], in0=mv[:, :, 0], scalar=-1.0, in1=rstd[:],
                                     op0=ALU.mult, op1=ALU.mult).then_inc(coef_ready, 1)
            dve.wait_ge(ld_small, 96)
            dve.tensor_scalar(sb["epscol"][:], sb["epscol"][:], 2.0, None, ALU.add).then_inc(dve_chain, 1)
            dve.wait_ge(dve_chain, 1)
            dve.sem_inc(dve_chain, -1)
            dve.tensor_copy(sb["ewa"][:], er[:]).then_inc(dve_chain, 1)
            dve.wait_ge(dve_chain, 1)
            dve.sem_inc(dve_chain, -1)
            dve.tensor_copy(ebh[:], ebr[:]).then_inc(dve_chain, 1)
            dve.wait_ge(dve_chain, 1)
            dve.sem_inc(dve_chain, -1)
            dve.tensor_tensor(sb["ewb"][:], ebr[:], ebh[:], ALU.subtract).then_inc(dve_chain, 1)
            dve.wait_ge(dve_chain, 1)
            dve.sem_inc(dve_chain, -1)
            dve.sem_inc(eb_split, 1)
            dve.wait_ge(ld_dst, 16)
            dve.sem_inc(ld_dst, -16)
            for j in range(2):
                dve.tensor_reduce(ext[:, j:j + 1], drow[:, j, :], AX, ALU.min).then_inc(dve_chain, 1)
                dve.wait_ge(dve_chain, 1)
                dve.sem_inc(dve_chain, -1)
                dve.tensor_reduce(ext[:, 2 + j:3 + j], drow[:, j, :], AX, ALU.max).then_inc(dve_chain, 1)
                dve.wait_ge(dve_chain, 1)
                dve.sem_inc(dve_chain, -1)
            dve.tensor_tensor(cmp_[:], ext[:].unsqueeze(2).broadcast_to([half, 4, NT - 1]),
                              thr[0:half, :].unsqueeze(1).broadcast_to([half, 4, NT - 1]), ALU.is_ge).then_inc(dve_chain, 1)
            dve.wait_ge(dve_chain, 1)
            dve.sem_inc(dve_chain, -1)
            dve.tensor_reduce(tile[:], cmp_[:], AX, ALU.add).then_inc(dve_chain, 1)
            dve.wait_ge(dve_chain, 1)
            dve.sem_inc(dve_chain, -1)
            dve.tensor_copy(sched_sb[:, 0, :], tile[:, 0:2]).then_inc(dve_chain, 1)
            dve.wait_ge(dve_chain, 1)
            dve.sem_inc(dve_chain, -1)
            dve.tensor_scalar(sched_sb[:, 1, :], tile[:, 2:4], 1.0, None, ALU.add).then_inc(sched_ready, 1)

            def summed(i, u):
                dve.wait_ge(norm_ready, 1)
                dve.sem_inc(norm_ready, -1)
                dve.tensor_tensor(xall[:, bass.ds(i * PG, PG), :], h0[:, u], b2bc[:].unsqueeze(1).broadcast_to([TN, PG, D]),
                                  ALU.add).then_inc(t_ready, 1)

            def low(i, u):
                dve.wait_ge(hi_ready, 1)
                dve.sem_inc(hi_ready, -1)
                dve.tensor_tensor(tb[:, u, :, D:2 * D], xall[:, bass.ds(i * PG, PG), :], tb[:, u, :, 0:D],
                                  ALU.subtract).then_inc(tb_ready, 1)

            last = NT // PG - 1
            w12 = flat[:, NT * D:NT * D + (KD + KH) * H].rearrange("p (k n) -> p k n", n=H)
            pairs, each = (last - 1) // 2, 3
            summed(0, 0)
            for u in range(2):
                summed(u + 1, 1 - u)
                low(u, u)
            dve.wait_ge(ld_w, 48)
            with dve.Fori(1, pairs) as i:
                for u in range(2):
                    summed(2 * i + u + 1, 1 - u)
                    low(2 * i + u, u)
                ks = bass.ds(each * (i - 1), each)
                dve.tensor_reduce(wsum[:, ks], w12[:, ks, :], AX, ALU.add)
            summed(last, last % 2)
            low(last - 1, (last - 1) % 2)
            low(last, last % 2)
            done = each * (pairs - 1)
            dve.tensor_reduce(wsum[:, done:KD + KH], w12[:, done:KD + KH, :], AX, ALU.add).then_inc(dve_chain, 1)
            dve.wait_ge(dve_chain, 1)
            dve.sem_inc(dve_chain, -1)
            dve.tensor_scalar(wneg[:], wsum[:], -WS / H, None, ALU.mult).then_inc(dve_chain, 1)
            dve.wait_ge(dve_chain, 1)
            dve.sem_inc(dve_chain, -1)
            dve.sem_inc(wneg_ready, 2)
            for raw, hi, lo in [w3s] + splits:
                dve.wait_ge(whi_ready, 1)
                dve.sem_inc(whi_ready, -1)
                dve.tensor_tensor(lo, raw, hi, ALU.subtract)
    return range(m.sems[0].num, m.sems[-1].num + 1)


def one_hot16(dve, out, iota16, dsts, negbase, b, tile, passed=None):
    for k in range(CB):
        ins = dve.tensor_scalar(out[:, k, :], iota16[:], dsts[:, bass.ds(CB * (b + 1) + k, 1)],
                                negbase[:, bass.ds(tile, 1)], ALU.subtract, ALU.is_equal)
        if passed is not None and k == 0:
            ins.then_inc(passed, 1)
    return ins


def tiles_of(nc, engine, table, b, n):
    why = "the schedule counts the tile bounds that a dst has passed: 0 to NT - 1, and one more for ends"
    both = []
    for part, least in ((0, 0), (1, 1)):
        _, v = nc.values_load_multi_w_load_instructions(
            table[0:1, part, bass.ds(b + 1, n)], engines=[engine], min_val=least, max_val=NT - 1 + part,
            skip_runtime_bounds_check_because=why)
        both.append(v)
    return list(zip(*both))


def edges0(nc, t, dram, sb):
    with ExitStack() as ctx:
        m = Memory(nc, ctx)
        acc, iota16, negbase, ewa, ewb = sb["acc"], sb["iota16"], sb["negbase"], sb["ewa"], sb["ewb"]
        srcs = m.sb("srcs", [P, NCH], I32)
        dsts = m.sb("dsts", [P, NCH + CB], F32)
        idx = m.sb("idx", [P, RING, CB], I32)
        table = m.sb("table0", [1, 2, NBP + 4], I32)
        rows = m.sb("rows", [P, RING, CB, 2 * D], F16)
        ea = m.sb("ea", [P, 2, BE], F32)
        eab = m.sb("eab", [P, 2, BE], F16)
        eah = m.sb("eah", [ED + 2, 2, BE], F16)
        rh = m.sb("rh", [P, 2, CB, D], F16)
        rl = m.sb("rl", [P, 2, CB, D], F16)
        hot = m.sb("hot", [P, 3, CB, TN], F16)
        mlp_ps = m.ps("mlp_ps", [P, 2, CB, D])
        sum_ps = m.ps("sum_ps", [TN, 3, 2 * D])
        used_ps = m.ps("used_ps", [1, 1])

        ld_idx = m.sem("ld_idx")
        ld_dst = m.sem("e_ld_dst")
        ld_tab = m.sem("ld_tab")
        cleared = m.sem("cleared")
        idx_ready = [m.sem(f"idx_ready{s}") for s in range(RING)]
        rows_ready = [m.sem(f"rows_ready{s}") for s in range(RING)]
        ea_ready = [m.sem(f"ea_ready{s}") for s in range(2)]
        ea_free = m.sem("ea_free")
        ones_ready = m.sem("ones_ready")
        ea_high = m.sem("ea_high")
        ea_split = m.sem("ea_split")
        mlp_done = m.sem("mlp_done")
        r_high = m.sem("r_high")
        r_split = m.sem("r_split")
        r_free = m.sem("r_free")
        rows_free = m.sem("rows_free")
        x_chain = m.sem("x_chain")
        hot_ready = m.sem("hot_ready")
        sum_done = m.sem("sum_done")
        sum_free = m.sem("sum_free")
        xhot_ready = m.sem("xhot_ready")
        xsum_done = m.sem("xsum_done")
        chain_sem = m.sem("e_chain")

        block = ctx.enter_context(nc.Block())

        @block.sync
        def _(sp):
            sp.dma_start(srcs[:], t["src_cols"]).then_inc(ld_idx, 16)
            sp.dma_start(table[:, :, 0:NBP + 1], dram["sched"][:, 0:NBP + 1].unsqueeze(0)).then_inc(ld_tab, 16)

            def load(b, s):
                eb = t["edge_t"][bass.ds(b, 1)].rearrange("a d e -> (a d) e")
                sp.dma_start(ea[0:ED, s, :], eb).then_inc(ea_ready[s], 16)
                sp.dma_start(ea[ED:P, s, :], eb).then_inc(ea_ready[s], 16)

            load(0, 0)
            sp.sem_inc(ea_free, 1)
            with sp.Fori(0, NB // RING) as i:
                for u in range(RING):
                    sp.wait_ge(ea_free, 1)
                    sp.sem_inc(ea_free, -1)
                    load(RING * i + u + 1, (u + 1) % 2)

        @block.gpsimd
        def _(pool):
            pool.dma_start(dsts[:], t["dst_cols"]).then_inc(ld_dst, 16)
            pool.memset(eah[ED:ED + 2, :, :], 1.0).then_inc(ones_ready, 1)
            with pool.Fori(0, NB // RING):
                for s in range(RING):
                    pool.wait_ge(idx_ready[s], 1)
                    pool.sem_inc(idx_ready[s], -1)
                    for k in range(CB):
                        pool.indirect_dma_start(
                            rows[:, s, k, :], None, dram["tab0"],
                            bass.IndirectOffsetOnAxis(ap=idx[:, s, k:k + 1], axis=0),
                        ).then_inc(rows_ready[s], 16)

        @block.scalar
        def _(act):
            def high_parts(s):
                act.wait_ge(ea_ready[s], 32)
                act.sem_inc(ea_ready[s], -32)
                act.activation(eab[:, s, :], ea[:, s, :], ACT.Copy).then_inc(ea_high, 1)
                act.activation(eah[0:ED, s, :], ea[0:ED, s, :], ACT.Copy).then_inc(ea_high, 1)

            act.sem_inc(r_free, 2)
            high_parts(0)
            zero = acc[:, NT * 3 // 4:NT, :].rearrange("p t c -> p (t c)")
            act.activation(zero, iota16[:, 0:1].broadcast_to([P, (NT - NT * 3 // 4) * 2 * D]), ACT.Copy, scale=0.0).then_inc(cleared, 1)
            with act.Fori(0, NB // RING) as i:
                for u in range(RING):
                    b, s = RING * i + u, u % 2
                    high_parts(1 - s)
                    act.wait_ge(mlp_done, 1)
                    act.sem_inc(mlp_done, -1)
                    act.wait_ge(r_free, 1)
                    act.sem_inc(r_free, -1)
                    act.activation(rh[:, s].rearrange("p k d -> p (k d)"), mlp_ps[:, s].rearrange("p k d -> p (k d)"),
                                   ACT.Relu).then_inc(r_high, 1)

        @block.tensor
        def _(pe):
            def edge_mlp(s):
                pe.wait_ge(ea_split, 1)
                pe.sem_inc(ea_split, -1)
                pe.sem_inc(ea_free, 1)
                for k in range(CB):
                    e = slice(k * P, (k + 1) * P)
                    pe.matmul(mlp_ps[:, s, k, :], eab[:, s, e], ewa[:], start=True, stop=False)
                    ins = pe.matmul(mlp_ps[:, s, k, :], eah[:, s, e], ewb[:], start=False, stop=True)
                ins.then_inc(mlp_done, 1)

            def sums(out, h, ring, s):
                for k in range(CB):
                    lhs = hot[:, h, k, :]
                    pe.matmul(out[:, 0:D], lhs, rows[:, ring, k, 0:D], start=(k == 0), stop=False, skip_group_check=True)
                    pe.matmul(out[:, 0:D], lhs, rows[:, ring, k, D:2 * D], start=False, stop=False, skip_group_check=True)
                    pe.matmul(out[:, D:2 * D], lhs, rh[:, s, k, :], start=False, stop=False, skip_group_check=True)
                    ins = pe.matmul(out[:, D:2 * D], lhs, rl[:, s, k, :], start=False, stop=(k == CB - 1), skip_group_check=True)
                return ins

            pe.wait_ge(ld_tab, 16)
            pe.wait_ge(ones_ready, 1)
            pe.sem_inc(ones_ready, -1)
            pe.sem_inc(sum_free, 2)
            edge_mlp(0)
            with pe.Fori(0, NB // RING) as i:
                tiles = tiles_of(nc, PE, table, RING * i, RING)
                for u in range(RING):
                    b, s = RING * i + u, u % 2
                    edge_mlp(1 - s)
                    lo, end = tiles[u]
                    pe.wait_ge(hot_ready, 1)
                    pe.sem_inc(hot_ready, -1)
                    pe.wait_ge(sum_free, 1)
                    pe.sem_inc(sum_free, -1)
                    pe.wait_ge(r_split, 1)
                    pe.sem_inc(r_split, -1)
                    pe.wait_ge(rows_ready[u], 16 * CB * (i + 1))
                    sums(sum_ps[:, s, :], s, u, s).then_inc(sum_done, 1)
                    with pe.If(end > lo + 1):
                        with pe.Fori(lo + 1, end):
                            pe.wait_ge(xhot_ready, 1)
                            pe.sem_inc(xhot_ready, -1)
                            sums(sum_ps[:, 2, :], 2, u, s).then_inc(xsum_done, 1)
                    pe.matmul(used_ps[:], ewa[:, 0:1], ewa[:, 0:1], start=True, stop=True).then_inc(r_free, 1)
                    pe.matmul(used_ps[:], ewa[:, 0:1], ewa[:, 0:1], start=True, stop=True).then_inc(rows_free, 1)

        @block.vector
        def _(dve):
            def low_parts(s):
                dve.wait_ge(ea_high, 2)
                dve.sem_inc(ea_high, -2)
                dve.tensor_tensor(eab[ED:P, s, :], ea[ED:P, s, :], eab[ED:P, s, :], ALU.subtract).then_inc(ea_split, 1)

            def add(s, lo):
                dve.wait_ge(chain_sem, 1)
                dve.sem_inc(chain_sem, -1)
                dve.wait_ge(sum_done, 1)
                dve.sem_inc(sum_done, -1)
                a = acc[0:TN, bass.ds(lo, 1), :].rearrange("p a c -> p (a c)")
                dve.tensor_tensor(a, a, sum_ps[:, s, :], ALU.add).then_inc(sum_free, 1)

            def extra_hot(b, x):
                one_hot16(dve, hot[:, 2], iota16, dsts, negbase, b, x).then_inc(xhot_ready, 1)

            def add_extra(x):
                dve.wait_ge(xsum_done, 1)
                dve.sem_inc(xsum_done, -1)
                ax = acc[0:TN, bass.ds(x, 1), :].rearrange("p a c -> p (a c)")
                dve.tensor_tensor(ax, ax, sum_ps[:, 2, :], ALU.add).then_inc(x_chain, 1)
                dve.wait_ge(x_chain, 1)
                dve.sem_inc(x_chain, -1)

            def indices(b, s):
                dve.tensor_copy(idx[:, s, :], srcs[:, bass.ds(CB * b, CB)]).then_inc(idx_ready[s], 1)

            def main_hot(b, s, lo):
                one_hot16(dve, hot[:, s], iota16, dsts, negbase, b, lo, chain_sem).then_inc(hot_ready, 1)

            def low_activations(s):
                dve.wait_ge(r_high, 1)
                dve.sem_inc(r_high, -1)
                dve.scalar_tensor_tensor(out=rl[:, s].rearrange("p k d -> p (k d)"), in0=mlp_ps[:, s].rearrange("p k d -> p (k d)"),
                                         scalar=0.0, in1=rh[:, s].rearrange("p k d -> p (k d)"),
                                         op0=ALU.max, op1=ALU.subtract).then_inc(r_split, 1)

            def advance(b, s, ring, lo, end, following):
                with dve.If(end > lo + 1):
                    add(1 - s, lo)
                    extra_hot(b - 1, end - 1)
                    low_parts(1 - s)
                    low_activations(s)
                    main_hot(b + 1, 1 - s, following)
                    add_extra(end - 1)
                    with dve.If(end > lo + 2):
                        with dve.Fori(lo + 1, end - 1) as x:
                            extra_hot(b - 1, x)
                            add_extra(x)
                with dve.Else():
                    low_parts(1 - s)
                    low_activations(s)
                    add(1 - s, lo)
                    main_hot(b + 1, 1 - s, following)
                dve.wait_ge(rows_free, 1)
                dve.sem_inc(rows_free, -1)
                indices(b - 1 + RING, ring)

            dve.wait_ge(ld_dst, 16)
            dve.wait_ge(ld_tab, 16)
            dve.wait_ge(ld_idx, 16)
            for b in range(RING):
                indices(b, b)
            main_hot(0, 0, tiles_of(nc, DVE, table, 0, 1)[0][0])
            dve.wait_ge(chain_sem, 1)
            dve.sem_inc(chain_sem, -1)
            low_parts(0)
            dve.memset(acc[:, NT // 2:NT * 3 // 4, :], 0.0).then_inc(chain_sem, 1)
            dve.wait_ge(chain_sem, 1)
            dve.sem_inc(chain_sem, -1)
            dve.wait_ge(cleared, 1)
            dve.sem_inc(cleared, -1)
            with dve.Fori(0, NB // RING) as i:
                tiles = tiles_of(nc, DVE, table, RING * i - 1, RING + 2)
                for u in range(RING):
                    b, s = RING * i + u, u % 2
                    if u:
                        advance(b, s, u - 1, *tiles[u], tiles[u + 2][0])
                    else:
                        with dve.If(i > 0):
                            advance(b, s, RING - 1, *tiles[u], tiles[u + 2][0])
                        with dve.Else():
                            low_parts(1 - s)
                            low_activations(s)
                            main_hot(b + 1, 1 - s, tiles[u + 2][0])
            lo, end = tiles_of(nc, DVE, table, NB - 1, 1)[0]
            add((NB - 1) % 2, lo)
            with dve.If(end > lo + 1):
                with dve.Fori(lo + 1, end) as x:
                    extra_hot(NB - 1, x)
                    add_extra(x)


def nodes(nc, t, dram, sb, stale):
    with ExitStack() as ctx:
        m = Memory(nc, ctx)
        acc, ident, lneps, epscol = sb["acc"], sb["ident"], sb["lneps"], sb["epscol"]
        w2e = m.sb("w2e", [P, KD, D], F32)
        waug = m.sb("waug", [P, KD, AW], F32)
        bcol = m.sb("bcol", [P, KD], F32)
        ones = m.sb("ones", [P, P], F32)
        zero = m.sb("zero", [P, 1], F32)
        ihead = m.sb("ihead", [P, KD, HEADS], I32)
        head = m.sb("head", [P, KD, HEADS], F32)
        acol = m.sb("acol", [P, 2, KD], F32)
        eb1 = m.sb("eb1", [P, KD], F32)
        cols = {n: m.sb("c_" + n, [P, KH], F32) for n in ("b1", "g1", "be1", "b2", "g2", "be2")}
        csum = m.sb("csum", [P, 2], F32)
        bc = {n: m.sb("bc_" + n, [TN, D], F32) for n in ("ee_b2", "b3", "bn_g", "bn_b")}
        baug = m.sb("baug", [TN, AW], F32)
        hf = m.sb("hf", [TN, D], F32)
        u = m.sb("u", [TN, 2, D], F32)
        rr = m.sb("rr", [TN, 2, D], F32)
        rt = m.sb("rt", [P, KD, TN], F32)
        hh = m.sb("hh", [P, KD, TN], F16)
        hl = m.sb("hl", [P, KD, TN], F16)
        z = [m.sb(f"z{j}", [P, KH, TN], F32) for j in (1, 2)]
        a = [m.sb(f"a{j}", [P, KH, TN], F32) for j in (1, 2)]
        room = z[0][:].rearrange("p k n -> p (k n)")
        o1, o2 = KD * D, KD * (D + TN)
        wt = room[:, 0:o1].rearrange("p (k n) -> p k n", n=D)
        bcb = room[:, o1:o2].rearrange("p (k n) -> p k n", n=TN)
        att = room[:, o2:o2 + KD * 2 * HEADS].rearrange("p (k n) -> p k n", n=2 * HEADS)
        ah = [m.sb(f"ah{j}", [P, n, KH, TN], F16) for j, n in ((1, 2), (2, 1))]
        al = [m.sb(f"al{j}", [P, n, KH, TN], F16) for j, n in ((1, 2), (2, 1))]
        ssq = [m.sb(f"ssq{j}", [P, TN], F32) for j in (1, 2)]
        rstd = [m.sb(f"rstd{j}", [P, TN], F32) for j in (1, 2)]
        hx = m.sb("hx", [TN, 2, D], F32)
        o = m.sb("o", [TN, D], F32)
        x1 = m.sb("x1", [TN, D], F32)
        h2 = m.sb("h2", [TN, D], F32)
        h2t = m.sb("h2t", [P, KD, TN], F32)
        prow = m.sb("prow", [TN, AW], F32)
        st3 = m.sb("st3", [TN, 2, 6], F32)
        mv3 = m.sb("mv3", [TN, 2, 2], F32)
        rrow = m.sb("rrow", [TN, 2], F32)

        z_ps = [m.ps(f"z{j}_ps", [P, 2, 512]) for j in (1, 2)]
        tv_ps = m.ps("tv_ps", [P, 3, TN])
        hv_ps = m.ps("hv_ps", [P, 3, TN])
        y_ps = m.ps("y_ps", [P, D])
        gp_ps = m.ps("gp_ps", [P, 512])
        t_ps, h_ps, v_ps = tv_ps[:, 0:KD, :], hv_ps[:, 0:KD, :], [hv_ps[:, KD, :], tv_ps[:, KD, :]]
        g_ps = gp_ps[:, 0:KD * TN].rearrange("p (k n) -> p k n", n=TN)
        p_ps = gp_ps[0:TN, 0:AW]

        def sem(n):
            return m.sem("n_" + n)

        ld, ld_act, setup, setup_ps, setup_done, ready = (
            sem("ld"), sem("ld_act"), sem("setup"), sem("setup_ps"), sem("setup_done"), sem("ready"))
        hf_ready, hf_free = sem("hf_ready"), sem("hf_free")
        hx_ready, hx_free = sem("hx_ready"), sem("hx_free")
        u_ready, acc_free = sem("u_ready"), sem("acc_free")
        rr_ready, rr_free = sem("rr_ready"), sem("rr_free")
        t_done, rt_ready = sem("t_done"), sem("rt_ready")
        h_done, hh_ready, h_split = sem("h_done"), sem("hh_ready"), sem("h_split")
        z_done = [sem(f"z{j}_done") for j in (1, 2)]
        z_ready = [sem(f"z{j}_ready") for j in (1, 2)]
        ssq_ready = [sem(f"ssq{j}_ready") for j in (1, 2)]
        var_done = [sem(f"var{j}_done") for j in (1, 2)]
        sd_ready = [sem(f"sd{j}_ready") for j in (1, 2)]
        zn_ready = [sem(f"zn{j}_ready") for j in (1, 2)]
        ah_ready = [sem(f"ah{j}_ready") for j in (1, 2)]
        a_split = [sem(f"a{j}_split") for j in (1, 2)]
        y_done, y_free, hb_ready = sem("y_done"), sem("y_free"), sem("hb_ready")
        x1_ready, x1_stored = sem("x1_ready"), sem("x1_stored")
        h2_ready, g_done, h2t_ready = sem("h2_ready"), sem("g_done"), sem("h2t_ready")
        p_done, p_free = sem("p_done"), sem("p_free")
        prow_ready, prow_stored = sem("prow_ready"), sem("prow_stored")
        row_var = [sem(f"row_var{j}") for j in (0, 1)]
        row_coef = [sem(f"row_coef{j}") for j in (0, 1)]
        act_chain, st_kept = sem("act_chain"), sem("st_kept")
        chain_sem = sem("chain")

        def tiles_v(ap):
            return ap.rearrange("(t p) c -> t p c", p=TN)

        h0_v, x_v, x1_v, tab_v = tiles_v(dram["h0"]), tiles_v(t["x"]), tiles_v(dram["x1"]), tiles_v(dram["tab1"])

        def one(ap, i):
            return ap[bass.ds(i, 1)].rearrange("a p c -> (a p) c")

        def bodies(eng, body):
            first, last = 4, NT - 2
            for i in range(first):
                body(i, i % 2)
            with eng.Fori(0, (last - first) // 2) as pair:
                for k in range(2):
                    body(2 * pair + (first + k), k)
            for i in range(last, NT + 4):
                body(i, i % 2)

        def has(i, back, ahead=0):
            return not isinstance(i, int) or 0 <= i + ahead - back < NT

        block = ctx.enter_context(nc.Block())

        @block.sync
        def _(sp):
            sp.dma_start(w2e[:], t["L0_gnn_ee_w2"].rearrange("(k p) n -> p k n", p=P)).then_inc(ld, 16)
            sp.dma_start(waug[:, :, 0:D], t["L1_gnn_W"].rearrange("(k p) n -> p k n", p=P)).then_inc(ld, 16)
            sp.dma_start(wt, t["L1_gnn_W_t"].rearrange("(k p) n -> p k n", p=P)).then_inc(ld, 16)
            sp.dma_start(bcol[:], t["L1_gnn_b_cols"]).then_inc(ld, 16)
            sp.dma_start(eb1[:], t["L0_gnn_ee_b1_cols"]).then_inc(ld, 16)
            sp.dma_start(baug[:, 0:D], t["L1_gnn_b"].partition_broadcast(TN)).then_inc(ld, 16)

            def load_front(i):
                sp.dma_start(hf[:], one(h0_v, i)).then_inc(hf_ready, 16)

            load_front(0)
            sp.sem_inc(hx_free, 1)

            def body(i, p):
                if has(i, 0, 1):
                    sp.wait_ge(hf_free, 1)
                    sp.sem_inc(hf_free, -1)
                    load_front(i + 1)
                if has(i, 2):
                    sp.wait_ge(hx_free, 1)
                    sp.sem_inc(hx_free, -1)
                    sp.dma_start(hx[:, 0, :], one(h0_v, i - 2)).then_inc(hx_ready, 16)
                    sp.dma_start(hx[:, 1, :], one(x_v, i - 2)).then_inc(hx_ready, 16)
                if has(i, 3):
                    sp.wait_ge(x1_ready, 1)
                    sp.sem_inc(x1_ready, -1)
                    sp.dma_start(one(x1_v, i - 3), x1[:]).then_inc(x1_stored, 16)
                if has(i, 4):
                    sp.wait_ge(prow_ready, 1)
                    sp.sem_inc(prow_ready, -1)
                    sp.dma_start(one(tab_v, i - 4), prow[:, 0:TW]).then_inc(prow_stored, 16)

            bodies(sp, body)
            sp.wait_ge(x1_stored, 16)
            sp.wait_ge(prow_stored, 16)

        @block.gpsimd
        def _(pool):
            pool.memset(zero[:], 0.0).then_inc(setup, 1)
            pool.iota(ihead[:], [[P, KD], [-HD, HEADS]], base=0, channel_multiplier=1).then_inc(setup, 1)
            pool.wait_ge(setup, 2)
            def turnable(i, p):
                pool.tensor_copy(rr[:, p, :], acc[0:TN, bass.ds(i, 1), D:2 * D].rearrange("p a c -> p (a c)")).then_inc(rr_ready, 1)

            turnable(0, 0)
            turnable(1, 1)

            def body(i, p):
                if has(i, 0):
                    pool.wait_ge(rr_free, 1)
                    pool.sem_inc(rr_free, -1)
                if has(i, 0, 2):
                    turnable(i + 2, p)
                if has(i, 2):
                    pool.wait_ge(hx_ready, 32)
                    pool.sem_inc(hx_ready, -32)
                    pool.tensor_tensor(hx[:, 0, :], hx[:, 0, :], bc["b3"][:], ALU.add).then_inc(hb_ready, 1)
                if has(i, 1):
                    pool.wait_ge(acc_free, 1)
                    pool.sem_inc(acc_free, -1)
                    pool.tensor_copy(acc[0:TN, bass.ds(i - 1, 1), 0:TW].rearrange("p a c -> p (a c)"), zero[0:TN, :].broadcast_to([TN, TW]))

            pool.wait_ge(ready, 1)
            bodies(pool, body)
            pool.sem_clear(stale)

        @block.tensor
        def _(pe):
            pe.wait_ge(ld, 16 * 6)
            pe.wait_ge(ld_act, 16 * (2 + len(cols) + len(bc)))
            pe.wait_ge(setup_done, 1)
            pe.sem_inc(setup_done, -1)
            for j in range(KD):
                for k in range(KD):
                    pe.matmul(t_ps[:, 0, 2 * HEADS * j:2 * HEADS * (j + 1)], wt[:, k, j * P:(j + 1) * P], att[:, k, :],
                              start=(k == 0), stop=(k == KD - 1))
            for k in range(KD):
                pe.matmul(p_ps[:, 0:2 * HEADS], bcb[:, k, :], att[:, k, :], start=(k == 0), stop=(k == KD - 1))
            pe.matmul(y_ps[:, 0:KH], ones[:], cols["b1"][:], start=True, stop=True)
            pe.matmul(y_ps[:, KH:2 * KH], ones[:], cols["b2"][:], start=True, stop=True).then_inc(setup_ps, 1)

            def turn(i, p):
                pe.wait_ge(rr_ready, 1)
                pe.sem_inc(rr_ready, -1)
                for k in range(KD):
                    ins = pe.transpose(t_ps[:, k, :], rr[:, p, k * P:(k + 1) * P], ident[0:TN, 0:TN])
                ins.then_inc(t_done, 1)

            def products(out, hi, lo, whi, wlo, n, ks=None, rows=False):
                for k in ks or range(n):
                    for q, (x_, w_) in enumerate(((hi, whi), (lo, whi), (hi, wlo))):
                        lhs, rhs = (x_(k), w_(k)) if rows else (w_(k), x_(k))
                        ins = pe.matmul(out, lhs, rhs, start=(k == 0 and q == 0), stop=(k == n - 1 and q == 2))
                return ins

            def hidden(j, half, outputs, n, hi, lo, whi, wlo):
                for b in outputs:
                    f = slice((4 * half + b) * P, (4 * half + b + 1) * P)
                    out = z_ps[j][:, half, b * TN:(b + 1) * TN]
                    ins = products(out, hi, lo, lambda k: whi[:, k, f], lambda k: wlo[:, k, f], n)
                if b == 3:
                    ins.then_inc(z_done[j], 1)

            def layer2(half, outputs, p):
                hidden(1, half, outputs, KH, lambda k: ah[0][:, p, k, :], lambda k: al[0][:, p, k, :], sb["w2h"], sb["w2l"])

            def output(ks):
                return products(y_ps[0:TN, 0:D], lambda k: ah[1][:, 0, k, :], lambda k: al[1][:, 0, k, :],
                                lambda k: sb["w3h"][:, k, :], lambda k: sb["w3l"][:, k, :], KH, ks, rows=True)

            def variance(j):
                pe.wait_ge(ssq_ready[j], 1)
                pe.sem_inc(ssq_ready[j], -1)
                pe.matmul(v_ps[j], ones[:], ssq[j][:], start=True, stop=True).then_inc(var_done[j], 1)

            pe.wait_ge(ready, 1)
            pe.sem_inc(y_free, 1)
            pe.sem_inc(p_free, 1)

            def make_h(i, p):
                pe.wait_ge(u_ready, 1)
                pe.sem_inc(u_ready, -1)
                for j in range(KD):
                    f = slice(j * P, (j + 1) * P)
                    for k in range(KD):
                        pe.matmul(h_ps[:, j, :], w2e[:, k, f], rt[:, k, :], start=(k == 0), stop=False)
                    ins = pe.matmul(h_ps[:, j, :], u[:, p, f], ident[0:TN, 0:TN], start=False, stop=True)
                ins.then_inc(h_done, 1)

            turn(0, 0)
            pe.wait_ge(rt_ready, 1)
            pe.sem_inc(rt_ready, -1)
            pe.sem_inc(rr_free, 1)
            make_h(0, 0)
            turn(1, 1)

            def body(i, p):
                if has(i, 0):
                    pe.wait_ge(h_split, 1)
                    pe.sem_inc(h_split, -1)
                    for half in range(2):
                        hidden(0, half, range(4), KD, lambda k: hh[:, k, :], lambda k: hl[:, k, :], sb["w1h"], sb["w1l"])
                if has(i, 0, 1):
                    pe.wait_ge(rt_ready, 1)
                    pe.sem_inc(rt_ready, -1)
                    pe.sem_inc(rr_free, 1)
                if has(i, 2):
                    variance(1)
                if has(i, 4):
                    pe.wait_ge(h2_ready, 1)
                    pe.sem_inc(h2_ready, -1)
                    pe.wait_ge(p_free, 1)
                    pe.sem_inc(p_free, -1)
                    for k in range(KD):
                        ins = pe.transpose(g_ps[:, k, :], h2[:, k * P:(k + 1) * P], ident[0:TN, 0:TN])
                    ins.then_inc(g_done, 1)
                if has(i, 1):
                    pe.wait_ge(a_split[0], 1)
                    pe.sem_inc(a_split[0], -1)
                    layer2(0, range(4), 1 - p)
                if has(i, 0):
                    variance(0)
                if has(i, 1):
                    layer2(1, range(4), 1 - p)
                if has(i, 4):
                    pe.wait_ge(h2t_ready, 1)
                    pe.sem_inc(h2t_ready, -1)
                    for k in range(KD):
                        ins = pe.matmul(p_ps, h2t[:, k, :], waug[:, k, :], start=(k == 0), stop=(k == KD - 1))
                    ins.then_inc(p_done, 1)
                if has(i, 2):
                    pe.wait_ge(a_split[1], 1)
                    pe.sem_inc(a_split[1], -1)
                    pe.wait_ge(y_free, 1)
                    pe.sem_inc(y_free, -1)
                    output(range(KH // 2))
                if has(i, 0, 1):
                    make_h(i + 1, 1 - p)
                if has(i, 0, 2):
                    turn(i + 2, p)
                if has(i, 2):
                    output(range(KH // 2, KH)).then_inc(y_done, 1)

            bodies(pe, body)

        @block.scalar
        def _(act):
            for c, n in enumerate(("L1_gnn_a_src", "L1_gnn_a_trg")):
                act.dma_start(acol[:, c, :], t[n + "_cols"]).then_inc(ld_act, 16)
            for n, c in cols.items():
                act.dma_start(c[:], t[f"L0_gnn_{n}_cols"]).then_inc(ld_act, 16)
            for n, c in bc.items():
                act.dma_start(c[:], t[f"L0_gnn_{n}"].partition_broadcast(TN)).then_inc(ld_act, 16)
            act.wait_ge(ready, 1)

            def turned(i):
                act.wait_ge(t_done, 1)
                act.sem_inc(t_done, -1)
                for k in range(KD):
                    ins = act.activation(rt[:, k, :], t_ps[:, k, :], ACT.Identity, bias=eb1[:, k:k + 1])
                ins.then_inc(rt_ready, 1)

            def biased(j, b, half):
                act.wait_ge(z_done[j], 1)
                act.sem_inc(z_done[j], -1)
                for k in range(4 * half, 4 * half + 4):
                    ins = act.activation(z[j][:, k, :], z_ps[j][:, half, (k % 4) * TN:(k % 4 + 1) * TN], ACT.Identity,
                                         bias=cols[b][:, k:k + 1], scale=(1.0, 1.0 / WS)[j])
                if half:
                    ins.then_inc(z_ready[j], 1)

            def deviation(j):
                act.wait_ge(var_done[j], 1)
                act.sem_inc(var_done[j], -1)
                act.activation(rstd[j][:], v_ps[j], ACT.Sqrt, bias=lneps[:]).then_inc(sd_ready[j], 1)

            def row_deviation(j):
                act.wait_ge(row_var[j], 1)
                act.sem_inc(row_var[j], -1)
                act.activation(rrow[:, j:j + 1], mv3[:, j, 1:2], ACT.Sqrt, bias=lneps[0:TN, :]).then_inc(row_coef[j], 1)

            def activated(j, slot, g, be):
                act.wait_ge(zn_ready[j], 1)
                act.sem_inc(zn_ready[j], -1)
                for k in range(KH):
                    ins = act.activation(a[j][:, k, :], z[j][:, k, :], ACT.Relu, bias=cols[be][:, k:k + 1], scale=cols[g][:, k:k + 1])
                ins.then_inc(act_chain, 1)
                act.wait_ge(act_chain, 1)
                act.sem_inc(act_chain, -1)
                act.activation(ah[j][:, slot], a[j][:], ACT.Copy).then_inc(ah_ready[j], 1)

            turned(0)

            def body(i, p):
                if has(i, 0):
                    act.wait_ge(h_done, 1)
                    act.sem_inc(h_done, -1)
                    act.activation(hh[:], h_ps, ACT.Copy, scale=1.0 / WS).then_inc(hh_ready, 1)
                if has(i, 0, 1):
                    turned(i + 1)
                if has(i, 0):
                    biased(0, "b1", 0)
                    biased(0, "b1", 1)
                if has(i, 2):
                    deviation(1)
                    activated(1, 0, "g2", "be2")
                if has(i, 4):
                    act.wait_ge(g_done, 1)
                    act.sem_inc(g_done, -1)
                    act.activation(h2t[:], g_ps, ACT.Relu).then_inc(h2t_ready, 1)
                if has(i, 0):
                    deviation(0)
                if has(i, 1):
                    biased(1, "b2", 0)
                if has(i, 3):
                    row_deviation(0)
                if has(i, 0):
                    activated(0, p, "g1", "be1")
                if has(i, 1):
                    biased(1, "b2", 1)
                if has(i, 3):
                    row_deviation(1)

            bodies(act, body)

        @block.vector
        def _(dve):
            dve.memset(ones[:], 1.0 / H).then_inc(chain_sem, 1)
            dve.wait_ge(chain_sem, 1)
            dve.sem_inc(chain_sem, -1)
            dve.wait_ge(setup, 2)
            dve.tensor_scalar(head[:], ihead[:], 0.0, None, ALU.is_ge).then_inc(chain_sem, 1)
            dve.wait_ge(chain_sem, 1)
            dve.sem_inc(chain_sem, -1)
            dve.scalar_tensor_tensor(out=head[:], in0=ihead[:], scalar=float(HD - 1), in1=head[:], op0=ALU.is_le, op1=ALU.mult).then_inc(chain_sem, 1)
            dve.wait_ge(chain_sem, 1)
            dve.sem_inc(chain_sem, -1)
            dve.wait_ge(ld, 16 * 6)
            dve.wait_ge(ld_act, 16 * (2 + len(cols) + len(bc)))
            for c in range(2):
                dve.tensor_tensor(att[:, :, c * HEADS:(c + 1) * HEADS], head[:],
                                  acol[:, c, :].unsqueeze(2).broadcast_to([P, KD, HEADS]), ALU.mult).then_inc(chain_sem, 1)
                dve.wait_ge(chain_sem, 1)
                dve.sem_inc(chain_sem, -1)
            dve.tensor_scalar(eb1[:], eb1[:], 0.0, None, ALU.max).then_inc(chain_sem, 1)
            dve.wait_ge(chain_sem, 1)
            dve.sem_inc(chain_sem, -1)
            dve.tensor_copy(bcb, bcol[:].unsqueeze(2).broadcast_to([P, KD, TN])).then_inc(chain_sem, 1)
            dve.wait_ge(chain_sem, 1)
            dve.sem_inc(chain_sem, -1)
            dve.sem_inc(setup_done, 1)
            dve.wait_ge(setup_ps, 1)
            dve.sem_inc(setup_ps, -1)
            for j in range(KD):
                dve.tensor_copy(waug[:, j, D:AW], t_ps[:, 0, 2 * HEADS * j:2 * HEADS * (j + 1)]).then_inc(chain_sem, 1)
                dve.wait_ge(chain_sem, 1)
                dve.sem_inc(chain_sem, -1)
            dve.tensor_copy(baug[:, D:AW], p_ps[:, 0:2 * HEADS]).then_inc(chain_sem, 1)
            dve.wait_ge(chain_sem, 1)
            dve.sem_inc(chain_sem, -1)
            for j, n in ((0, "b1"), (1, "b2")):
                dve.tensor_reduce(csum[:, j:j + 1], y_ps[:, KH * j:KH * (j + 1)], AX, ALU.add).then_inc(chain_sem, 1)
                dve.wait_ge(chain_sem, 1)
                dve.sem_inc(chain_sem, -1)
                dve.tensor_scalar(cols[n][:], cols[n][:], csum[:, j:j + 1], None, ALU.subtract).then_inc(chain_sem, 1)
                dve.wait_ge(chain_sem, 1)
                dve.sem_inc(chain_sem, -1)
            dve.sem_inc(ready, 1)
            dve.sem_inc(x1_stored, 16)
            dve.sem_inc(prow_stored, 16)
            dve.sem_inc(st_kept, 1)

            def front(i, p):
                dve.wait_ge(hf_ready, 16)
                dve.sem_inc(hf_ready, -16)
                dve.scalar_tensor_tensor(out=u[:, p, :], in0=hf[:], scalar=epscol[0:TN, :], in1=bc["ee_b2"][:],
                                         op0=ALU.mult, op1=ALU.add).then_inc(chain_sem, 1)
                dve.wait_ge(chain_sem, 1)
                dve.sem_inc(chain_sem, -1)
                dve.sem_inc(hf_free, 1)
                dve.tensor_tensor(u[:, p, :], u[:, p, :], acc[0:TN, bass.ds(i, 1), 0:D].rearrange("p a c -> p (a c)"), ALU.add).then_inc(chain_sem, 1)
                dve.wait_ge(chain_sem, 1)
                dve.sem_inc(chain_sem, -1)
                dve.sem_inc(acc_free, 1)

            def squares(j):
                dve.wait_ge(z_ready[j], 1)
                dve.sem_inc(z_ready[j], -1)
                dve.tensor_tensor(a[j][:], z[j][:], z[j][:], ALU.mult).then_inc(chain_sem, 1)
                dve.wait_ge(chain_sem, 1)
                dve.sem_inc(chain_sem, -1)
                dve.tensor_reduce(ssq[j][:], a[j][:].rearrange("p k n -> p n k"), AX, ALU.add).then_inc(chain_sem, 1)
                dve.wait_ge(chain_sem, 1)
                dve.sem_inc(chain_sem, -1)
                dve.sem_inc(ssq_ready[j], 1)

            def scaled(j, read=None):
                dve.wait_ge(sd_ready[j], 1)
                dve.sem_inc(sd_ready[j], -1)
                if read is not None:
                    dve.sem_inc(read, 1)
                dve.reciprocal(rstd[j][:], rstd[j][:]).then_inc(chain_sem, 1)
                dve.wait_ge(chain_sem, 1)
                dve.sem_inc(chain_sem, -1)
                dve.tensor_tensor(z[j][:], z[j][:], rstd[j][:].unsqueeze(1).broadcast_to([P, KH, TN]), ALU.mult).then_inc(zn_ready[j], 1)

            def low(j, slot):
                dve.wait_ge(ah_ready[j], 1)
                dve.sem_inc(ah_ready[j], -1)
                dve.tensor_tensor(al[j][:, slot], a[j][:], ah[j][:, slot], ALU.subtract).then_inc(chain_sem, 1)
                dve.wait_ge(chain_sem, 1)
                dve.sem_inc(chain_sem, -1)
                dve.sem_inc(a_split[j], 1)

            def row_stats(j, src):
                dve.bn_stats(st3[:, j, :], src).then_inc(chain_sem, 1)
                dve.wait_ge(chain_sem, 1)
                dve.sem_inc(chain_sem, -1)
                dve.bn_aggr(mv3[:, j, :], st3[:, j, :]).then_inc(chain_sem, 1)
                dve.wait_ge(chain_sem, 1)
                dve.sem_inc(chain_sem, -1)
                dve.sem_inc(row_var[j], 1)

            def row_norm(j, dst, src):
                dve.wait_ge(row_coef[j], 1)
                dve.sem_inc(row_coef[j], -1)
                dve.reciprocal(rrow[:, j:j + 1], rrow[:, j:j + 1]).then_inc(chain_sem, 1)
                dve.wait_ge(chain_sem, 1)
                dve.sem_inc(chain_sem, -1)
                return dve.tensor_scalar(dst, src, mv3[:, j, 0:1], rrow[:, j:j + 1], ALU.subtract, ALU.mult)

            front(0, 0)
            dve.sem_inc(u_ready, 1)

            def body(i, p):
                if has(i, 0):
                    dve.wait_ge(hh_ready, 1)
                    dve.sem_inc(hh_ready, -1)
                    dve.scalar_tensor_tensor(out=hl[:], in0=h_ps, scalar=1.0 / WS, in1=hh[:],
                                             op0=ALU.mult, op1=ALU.subtract).then_inc(h_split, 1)
                if has(i, 1):
                    low(0, 1 - p)
                if has(i, 2):
                    squares(1)
                if has(i, 4):
                    row_norm(1, h2[:], x1[:]).then_inc(chain_sem, 1)
                    dve.wait_ge(chain_sem, 1)
                    dve.sem_inc(chain_sem, -1)
                    dve.sem_inc(h2_ready, 1)
                if has(i, 2):
                    scaled(1)
                if has(i, 0):
                    squares(0)
                if has(i, 0, 1):
                    front(i + 1, 1 - p)
                if has(i, 3):
                    dve.wait_ge(y_done, 1)
                    dve.sem_inc(y_done, -1)
                    dve.wait_ge(hb_ready, 1)
                    dve.sem_inc(hb_ready, -1)
                    dve.scalar_tensor_tensor(out=o[:], in0=y_ps[0:TN, 0:D], scalar=1.0 / WS, in1=hx[:, 0, :],
                                             op0=ALU.mult, op1=ALU.add).then_inc(chain_sem, 1)
                    dve.wait_ge(chain_sem, 1)
                    dve.sem_inc(chain_sem, -1)
                    dve.sem_inc(y_free, 1)
                    row_stats(0, o[:])
                if has(i, 0):
                    scaled(0, u_ready if has(i, 0, 1) else None)
                if has(i, 2):
                    low(1, 0)
                if has(i, 3):
                    row_norm(0, o[:], o[:]).then_inc(chain_sem, 1)
                    dve.wait_ge(chain_sem, 1)
                    dve.sem_inc(chain_sem, -1)
                    dve.tensor_tensor(o[:], o[:], bc["bn_g"][:], ALU.mult).then_inc(chain_sem, 1)
                    dve.wait_ge(chain_sem, 1)
                    dve.sem_inc(chain_sem, -1)
                if has(i, 4):
                    dve.wait_ge(p_done, 1)
                    dve.sem_inc(p_done, -1)
                    dve.wait_ge(prow_stored, 16)
                    dve.sem_inc(prow_stored, -16)
                    dve.wait_ge(st_kept, 1)
                    dve.sem_inc(st_kept, -1)
                    dve.tensor_tensor(prow[:], p_ps, baug[:], ALU.add).then_inc(chain_sem, 1)
                    dve.wait_ge(chain_sem, 1)
                    dve.sem_inc(chain_sem, -1)
                    dve.sem_inc(p_free, 1)
                    dve.sem_inc(prow_ready, 1)
                    dve.tensor_copy(sb["st"][0:TN, bass.ds(i - 4, 1), :].rearrange("p a c -> p (a c)"), prow[:, D:AW]).then_inc(st_kept, 1)
                if has(i, 3):
                    dve.tensor_tensor(o[:], o[:], bc["bn_b"][:], ALU.add).then_inc(chain_sem, 1)
                    dve.wait_ge(chain_sem, 1)
                    dve.sem_inc(chain_sem, -1)
                    dve.wait_ge(x1_stored, 16)
                    dve.sem_inc(x1_stored, -16)
                    dve.scalar_tensor_tensor(out=x1[:], in0=o[:], scalar=0.0, in1=hx[:, 1, :],
                                             op0=ALU.max, op1=ALU.add).then_inc(chain_sem, 1)
                    dve.wait_ge(chain_sem, 1)
                    dve.sem_inc(chain_sem, -1)
                    dve.sem_inc(x1_ready, 1)
                    dve.sem_inc(hx_free, 1)
                    row_stats(1, x1[:])

            bodies(dve, body)


def one_hot(dve, out, iota16, dsts, negbase, b, tile):
    return dve.scalar_tensor_tensor(
        out=out, in0=iota16[:].unsqueeze(1).broadcast_to([P, CB, TN]), scalar=negbase[:, bass.ds(tile, 1)],
        in1=dsts[:, bass.ds(CB * (b + 1), CB)].unsqueeze(2).broadcast_to([P, CB, TN]),
        op0=ALU.subtract, op1=ALU.is_equal)


def split3(dve, chain_sem, x, parts, rest):
    dve.tensor_copy(parts[0], x).then_inc(chain_sem, 1)
    dve.wait_ge(chain_sem, 1)
    dve.sem_inc(chain_sem, -1)
    dve.tensor_tensor(rest, x, parts[0], ALU.subtract).then_inc(chain_sem, 1)
    dve.wait_ge(chain_sem, 1)
    dve.sem_inc(chain_sem, -1)
    dve.tensor_copy(parts[1], rest).then_inc(chain_sem, 1)
    dve.wait_ge(chain_sem, 1)
    dve.sem_inc(chain_sem, -1)
    dve.tensor_tensor(parts[2], rest, parts[1], ALU.subtract).then_inc(chain_sem, 1)
    dve.wait_ge(chain_sem, 1)
    dve.sem_inc(chain_sem, -1)


def leaky(dve, out, x):
    return dve.scalar_tensor_tensor(out=out, in0=x, scalar=SLOPE, in1=x, op0=ALU.mult, op1=ALU.max)


def edges1(nc, t, dram, sb, keep):
    smax = keep.sb("smax", [P, HEADS], F32)
    maxima = keep.sb("maxima", [P, CB, HEADS], F32)
    x1_tail = keep.sb("x1_tail", [TN, NT, D - (2 * D - TW)], F32)
    with ExitStack() as ctx:
        m = Memory(nc, ctx)
        acc, iota16, negbase, nodeid, ident, st = (
            sb["acc"], sb["iota16"], sb["negbase"], sb["nodeid"], sb["ident"], sb["st"])
        srcs = m.sb("a_srcs", [P, NCH], I32)
        dsts = m.sb("a_dsts", [P, NCH + CB], F32)
        far = m.sb("far", [P, NCH + CB], F32)
        idx = m.sb("a_idx", [P, RING, CB], I32)
        table = m.sb("table1", [1, 2, NBP + 4], I32)
        dstb = m.sb("dstb", [P, RING, BE], I32)
        trg = m.sb("trg", [TN, 3, NT, HEADS], BF16)
        rest = m.sb("rest", [TN, NT, HEADS], F32)
        rows = m.sb("a_rows", [P, RING, CB, TW], F32)
        hot_t = m.sb("hot_t", [TN, 3, BE], BF16)
        hot = m.sb("a_hot", [P, 3, CB, TN], F32)
        ht = m.sb("ht", [P, 2, CB, HEADS], F32)
        ec = m.sb("ec", [P, 2, CB, HEADS], F32)
        d = m.sb("d", [P, 2, CB, HEADS], F32)
        feat = m.sb("feat", [P, 2, CB, TW], F32)
        part = m.sb("part", [TN, HEADS], F32)
        smax_col = m.sb("smax_col", [HEADS, 1], F32)
        diag = m.sb("diag", [HEADS, HEADS], F32)
        ones = m.sb("a_ones", [HEADS, P], F32)
        ht_ps = [m.ps(f"ht{s}_ps", [P, CB, HEADS]) for s in range(3)]
        sum_ps = [m.ps(f"sum{s}_ps", [TN, TW]) for s in range(3)]

        ld_idx, ld_dst, ld_tab = m.sem("a_ld_idx"), m.sem("a_ld_dst"), m.sem("a_ld_tab")
        ld_x1 = m.sem("ld_x1")
        smax_in, smax_turned = m.sem("smax_in"), m.sem("smax_turned")
        diag_ready, smax_done = m.sem("diag_ready"), m.sem("smax_done")
        idx_ready = [m.sem(f"a_idx_ready{s}") for s in range(RING)]
        rows_ready = [m.sem(f"a_rows_ready{s}") for s in range(RING)]
        dstb_ready = [m.sem(f"dstb_ready{s}") for s in range(RING)]
        dstb_free = m.sem("dstb_free")
        hot_t_ready = m.sem("hot_t_ready")
        ht_done = m.sem("ht_done")
        xhot_t_ready = m.sem("xhot_t_ready")
        xht_done = m.sem("xht_done")
        hot_cleared = m.sem("hot_cleared")
        d_ready = m.sem("d_ready")
        p_ready = m.sem("p_ready")
        feat_ready = m.sem("feat_ready")
        sum_done = m.sem("a_sum_done")
        xhot_ready = m.sem("a_xhot_ready")
        xsum_done = m.sem("a_xsum_done")
        chain_sem = m.sem("a_chain")

        block = ctx.enter_context(nc.Block())

        @block.sync
        def _(sp):
            sp.dma_start(srcs[:], t["src_cols"]).then_inc(ld_idx, 16)
            sp.dma_start(table[:, :, 0:NBP + 1], dram["sched"][:, 0:NBP + 1].unsqueeze(0)).then_inc(ld_tab, 16)
            dst_rows = t["dst_flat"].rearrange("(b e) -> b e", e=BE)

            def load(b, s):
                sp.dma_start(dstb[:, s, :], dst_rows[bass.ds(b, 1)].broadcast_to([P, BE])).then_inc(dstb_ready[s], 16)

            for s in range(RING):
                load(s, s)
            x1_v, fits = dram["x1"].rearrange("(t p) c -> p t c", p=TN), 2 * D - TW

            def load_x1(tiles):
                sp.dma_start(acc[0:TN, tiles, TW:2 * D], x1_v[:, tiles, 0:fits]).then_inc(ld_x1, 16)
                sp.dma_start(x1_tail[:, tiles, :], x1_v[:, tiles, fits:D]).then_inc(ld_x1, 16)

            rounds = NB // RING
            load_x1(slice(rounds, NT))
            with sp.Fori(0, NB // RING) as i:
                for u in range(RING):
                    sp.wait_ge(dstb_free, 1)
                    sp.sem_inc(dstb_free, -1)
                    load(RING * (i + 1) + u, u)
                load_x1(bass.ds(i, 1))
            sp.wait_ge(ld_x1, 32 * (rounds + 1))

        @block.gpsimd
        def _(pool):
            pool.dma_start(dsts[:], t["dst_cols"]).then_inc(ld_dst, 16)
            with pool.Fori(0, NB // RING):
                for s in range(RING):
                    pool.wait_ge(idx_ready[s], 1)
                    pool.sem_inc(idx_ready[s], -1)
                    for k in range(CB):
                        pool.indirect_dma_start(
                            rows[:, s, k, :], None, dram["tab1"],
                            bass.IndirectOffsetOnAxis(ap=idx[:, s, k:k + 1], axis=0),
                        ).then_inc(rows_ready[s], 16)

        @block.scalar
        def _(act):
            with act.Fori(0, NB // RING):
                for u in range(RING):
                    s = u % 2
                    act.wait_ge(d_ready, 1)
                    act.sem_inc(d_ready, -1)
                    act.activation(feat[:, s, :, D:TW], d[:, s], ACT.Exp).then_inc(p_ready, 1)

        @block.tensor
        def _(pe):
            def targets(out, h, tile):
                for k in range(CB):
                    lhs = hot_t[:, h, k * P:(k + 1) * P]
                    for q in range(3):
                        ins = pe.matmul(out[:, k, :], lhs, trg[:, q, bass.ds(tile, 1), :].rearrange("p a c -> p (a c)"),
                                        start=(q == 0), stop=(q == 2))
                return ins

            def other_targets(lo, end):
                with pe.If(end > lo + 1):
                    pe.wait_ge(xhot_t_ready, 1)
                    pe.sem_inc(xhot_t_ready, -1)
                    targets(ht_ps[2], 2, end - 1).then_inc(xht_done, 1)
                    with pe.If(end > lo + 2):
                        with pe.Fori(lo + 1, end - 1) as x:
                            pe.wait_ge(xhot_t_ready, 1)
                            pe.sem_inc(xhot_t_ready, -1)
                            targets(ht_ps[2], 2, x).then_inc(xht_done, 1)

            def sums(out, h, s):
                for k in range(CB):
                    ins = pe.matmul(out[:], hot[:, h, k, :], feat[:, s, k, :], start=(k == 0), stop=(k == CB - 1))
                return ins

            def other_sums(s, lo, end):
                with pe.If(end > lo + 1):
                    with pe.Fori(lo + 1, end):
                        pe.wait_ge(xhot_ready, 1)
                        pe.sem_inc(xhot_ready, -1)
                        sums(sum_ps[2], 2, s).then_inc(xsum_done, 1)

            pe.wait_ge(smax_in, 1)
            pe.sem_inc(smax_in, -1)
            pe.transpose(sum_ps[0][0:HEADS, 0:TN], part[:], ident[0:TN, 0:TN]).then_inc(smax_turned, 1)
            pe.wait_ge(diag_ready, 1)
            pe.sem_inc(diag_ready, -1)
            pe.matmul(ht_ps[0][:, 0, :], ones[:], diag[:], start=True, stop=True).then_inc(smax_done, 1)
            pe.wait_ge(ld_tab, 16)
            lo, end = tiles_of(nc, PE, table, 0, 1)[0]
            pe.wait_ge(hot_t_ready, 1)
            pe.sem_inc(hot_t_ready, -1)
            targets(ht_ps[0], 0, lo).then_inc(ht_done, 1)
            other_targets(lo, end)
            pe.wait_ge(hot_t_ready, 1)
            pe.sem_inc(hot_t_ready, -1)
            targets(ht_ps[1], 1, tiles_of(nc, PE, table, 1, 1)[0][0]).then_inc(ht_done, 1)
            pe.wait_ge(hot_cleared, 1)
            pe.sem_inc(hot_cleared, -1)
            sums(sum_ps[1], 1, 1).then_inc(sum_done, 1)
            with pe.Fori(0, NB // RING) as i:
                tiles = tiles_of(nc, PE, table, RING * i - 1, RING + 3)
                for u in range(RING):
                    s = u % 2
                    pe.wait_ge(hot_t_ready, 1)
                    pe.sem_inc(hot_t_ready, -1)
                    targets(ht_ps[s], s, tiles[u + 3][0]).then_inc(ht_done, 1)
                    other_sums(1 - s, *tiles[u])
                    other_targets(*tiles[u + 2])
                    pe.wait_ge(feat_ready, 1)
                    pe.sem_inc(feat_ready, -1)
                    sums(sum_ps[s], s, s).then_inc(sum_done, 1)
            other_sums((NB - 1) % 2, *tiles_of(nc, PE, table, NB - 1, 1)[0])

        @block.vector
        def _(dve):
            def node_hot(slot, row, tile):
                return dve.tensor_scalar(hot_t[:, slot, :], dstb[0:TN, row, :], nodeid[0:TN, bass.ds(tile, 1)], None, ALU.is_equal)

            def first_targets(b, s):
                dve.wait_ge(ht_done, 1)
                dve.sem_inc(ht_done, -1)
                fars = far[:, bass.ds(CB * (b + 1), CB)].unsqueeze(2).broadcast_to([P, CB, HEADS])
                dve.tensor_tensor(ht[:, s], ht_ps[s][:], fars, ALU.add).then_inc(chain_sem, 1)
                dve.wait_ge(chain_sem, 1)
                dve.sem_inc(chain_sem, -1)

            def target_hot(row, x):
                node_hot(2, row, x).then_inc(xhot_t_ready, 1)

            def more_targets(s):
                dve.wait_ge(xht_done, 1)
                dve.sem_inc(xht_done, -1)
                dve.tensor_tensor(ht[:, s], ht[:, s], ht_ps[2][:], ALU.add).then_inc(chain_sem, 1)
                dve.wait_ge(chain_sem, 1)
                dve.sem_inc(chain_sem, -1)

            def logits(i, u, s):
                dve.wait_ge(rows_ready[u], 16 * CB * (i + 1))
                e, c = ec[:, 0], ec[:, 1]
                dve.tensor_tensor(e, rows[:, u, :, D:TW], ht[:, s], ALU.add)
                dve.tensor_tensor(c, ht[:, s], smax[:].unsqueeze(1).broadcast_to([P, CB, HEADS]), ALU.add).then_inc(chain_sem, 1)
                dve.wait_ge(chain_sem, 1)
                dve.sem_inc(chain_sem, -1)
                leaky(dve, ec[:], ec[:]).then_inc(chain_sem, 1)
                dve.wait_ge(chain_sem, 1)
                dve.sem_inc(chain_sem, -1)
                dve.tensor_tensor(d[:, s], e, c, ALU.subtract).then_inc(d_ready, 1)
                dve.tensor_tensor(maxima[:], maxima[:], e, ALU.max).then_inc(chain_sem, 1)

            def weighted(u, s):
                dve.wait_ge(p_ready, 1)
                dve.sem_inc(p_ready, -1)
                p = feat[:, s, :, D:TW].unsqueeze(3).broadcast_to([P, CB, HEADS, HD])
                dve.tensor_tensor(feat[:, s, :, 0:D].rearrange("p k (h f) -> p k h f", h=HEADS),
                                  rows[:, u, :, 0:D].rearrange("p k (h f) -> p k h f", h=HEADS), p, ALU.mult).then_inc(feat_ready, 1)

            def add(slot, tile):
                a = acc[0:TN, bass.ds(tile, 1), 0:TW].rearrange("p a c -> p (a c)")
                dve.tensor_tensor(a, a, sum_ps[slot][:], ALU.add).then_inc(chain_sem, 1)
                dve.wait_ge(chain_sem, 1)
                dve.sem_inc(chain_sem, -1)

            def extra_hot(b, x):
                one_hot(dve, hot[:, 2], iota16, dsts, negbase, b, x).then_inc(xhot_ready, 1)

            def add_extra(x):
                dve.wait_ge(xsum_done, 1)
                dve.sem_inc(xsum_done, -1)
                add(2, x)

            def middle(b, u, s, lo, end):
                with dve.If(end > lo + 1):
                    extra_hot(b - 1, end - 1)
                    first_targets(b + 1, 1 - s)
                    weighted(u, s)
                    add_extra(end - 1)
                    with dve.If(end > lo + 2):
                        with dve.Fori(lo + 1, end - 1) as x:
                            extra_hot(b - 1, x)
                            add_extra(x)
                with dve.Else():
                    first_targets(b + 1, 1 - s)
                    weighted(u, s)

            def last_part(b, s, row, before, lo, end):
                with dve.If(end > lo + 1):
                    target_hot(row, end - 1)
                    dve.wait_ge(sum_done, 1)
                    dve.sem_inc(sum_done, -1)
                    add(1 - s, before)
                    more_targets(1 - s)
                    with dve.If(end > lo + 2):
                        with dve.Fori(lo + 1, end - 1) as x:
                            target_hot(row, x)
                            more_targets(1 - s)
                with dve.Else():
                    dve.wait_ge(sum_done, 1)
                    dve.sem_inc(sum_done, -1)
                    add(1 - s, before)
                dve.sem_inc(dstb_free, 1)

            def indices(b, s):
                dve.tensor_copy(idx[:, s, :], srcs[:, bass.ds(CB * b, CB)]).then_inc(idx_ready[s], 1)

            dve.wait_ge(ld_idx, 16)
            for b in range(RING):
                indices(b, b)
            dve.tensor_reduce(part[:], st[0:TN, :, 0:HEADS].rearrange("p t h -> p h t"), AX, ALU.max).then_inc(chain_sem, 1)
            dve.wait_ge(chain_sem, 1)
            dve.sem_inc(chain_sem, -1)
            dve.sem_inc(smax_in, 1)
            dve.memset(ones[:], 1.0).then_inc(chain_sem, 1)
            dve.wait_ge(chain_sem, 1)
            dve.sem_inc(chain_sem, -1)
            dve.memset(maxima[:], FAR).then_inc(chain_sem, 1)
            dve.wait_ge(chain_sem, 1)
            dve.sem_inc(chain_sem, -1)
            dve.memset(hot[:, 1:2], 0.0)
            dve.memset(feat[:, 1], 0.0).then_inc(chain_sem, 1)
            dve.wait_ge(chain_sem, 1)
            dve.sem_inc(chain_sem, -1)
            dve.sem_inc(hot_cleared, 1)
            dve.wait_ge(smax_turned, 1)
            dve.sem_inc(smax_turned, -1)
            dve.tensor_reduce(smax_col[:], sum_ps[0][0:HEADS, 0:TN], AX, ALU.max).then_inc(chain_sem, 1)
            dve.wait_ge(chain_sem, 1)
            dve.sem_inc(chain_sem, -1)
            dve.tensor_scalar(diag[:], ident[0:HEADS, 0:HEADS], smax_col[:], None, ALU.mult).then_inc(chain_sem, 1)
            dve.wait_ge(chain_sem, 1)
            dve.sem_inc(chain_sem, -1)
            dve.sem_inc(diag_ready, 1)
            split3(dve, chain_sem, st[0:TN, :, HEADS:2 * HEADS], [trg[:, q] for q in range(3)], rest[:])
            dve.wait_ge(smax_done, 1)
            dve.sem_inc(smax_done, -1)
            dve.tensor_copy(smax[:], ht_ps[0][:, 0, :]).then_inc(chain_sem, 1)
            dve.wait_ge(chain_sem, 1)
            dve.sem_inc(chain_sem, -1)
            dve.wait_ge(ld_dst, 16)
            dve.wait_ge(ld_tab, 16)
            dve.tensor_scalar(far[:], dsts[:], float(N), FAR, ALU.is_ge, ALU.mult).then_inc(chain_sem, 1)
            dve.wait_ge(chain_sem, 1)
            dve.sem_inc(chain_sem, -1)
            lo, end = tiles_of(nc, DVE, table, 0, 1)[0]
            dve.wait_ge(dstb_ready[0], 16)
            dve.sem_inc(dstb_ready[0], -16)
            node_hot(0, 0, lo).then_inc(hot_t_ready, 1)
            dve.wait_ge(dstb_ready[1], 16)
            dve.sem_inc(dstb_ready[1], -16)
            node_hot(1, 1, tiles_of(nc, DVE, table, 1, 1)[0][0]).then_inc(hot_t_ready, 1)
            first_targets(0, 0)
            with dve.If(end > lo + 1):
                target_hot(0, end - 1)
                more_targets(0)
                with dve.If(end > lo + 2):
                    with dve.Fori(lo + 1, end - 1) as x:
                        target_hot(0, x)
                        more_targets(0)
            dve.sem_inc(dstb_free, 1)
            with dve.Fori(0, NB // RING) as i:
                tiles = tiles_of(nc, DVE, table, RING * i - 1, RING + 3)
                for u in range(RING):
                    b, s = RING * i + u, u % 2
                    logits(i, u, s)
                    dve.wait_ge(dstb_ready[(u + 2) % RING], 16)
                    dve.sem_inc(dstb_ready[(u + 2) % RING], -16)
                    node_hot(s, (u + 2) % RING, tiles[u + 3][0]).then_inc(hot_t_ready, 1)
                    one_hot(dve, hot[:, s], iota16, dsts, negbase, b, tiles[u + 1][0])
                    dve.wait_ge(chain_sem, 1)
                    dve.sem_inc(chain_sem, -1)
                    middle(b, u, s, *tiles[u])
                    indices(b + RING, u)
                    last_part(b, s, (u + 1) % RING, tiles[u][0], *tiles[u + 2])
            b, s = NB - 1, (NB - 1) % 2
            lo, end = tiles_of(nc, DVE, table, b, 1)[0]
            dve.wait_ge(sum_done, 1)
            dve.sem_inc(sum_done, -1)
            add(s, lo)
            with dve.If(end > lo + 1):
                with dve.Fori(lo + 1, end) as x:
                    extra_hot(b, x)
                    add_extra(x)
            dve.wait_ge(dstb_ready[(NB + 2) % RING], 16)
            dve.sem_inc(dstb_ready[(NB + 2) % RING], -16)
            dve.wait_ge(dstb_ready[(NB + 3) % RING], 16)
            dve.sem_inc(dstb_ready[(NB + 3) % RING], -16)
    return smax, maxima, x1_tail


def finish(nc, t, dram, sb, smax, maxima, x1_tail, out):
    with ExitStack() as ctx:
        m = Memory(nc, ctx)
        acc, ident, st = sb["acc"], sb["ident"], sb["st"]
        e = m.sb("f_e", [TN, NT, HEADS], F32)
        c = m.sb("f_c", [TN, NT, HEADS], F32)
        p = m.sb("f_p", [TN, NT, HEADS], F32)
        g = m.sb("f_g", [TN, NT, HEADS], F32)
        mx = m.sb("mx", [P, 2], F32)
        mrow = m.sb("mrow", [1, 1], F32)
        ones = m.sb("f_ones", [1, P], F32)
        top = m.sb("top", [P, 1], F32)
        FB = 5
        steps = NT // FB
        hp = m.sb("hp", [TN, NT, D], F32)
        turn_ps = m.ps("turn_ps", [1, P])
        top_ps = m.ps("top_ps", [P, 1])

        loaded = [m.sem(f"f_loaded{i}") for i in range(steps)]
        out_ready = m.sem("out_ready")
        out_stored = m.sem("out_stored")
        mx_ready, turned, mrow_ready, top_done = m.sem("mx_ready"), m.sem("turned"), m.sem("mrow_ready"), m.sem("top_done")
        exp_in, exp_ready = m.sem("exp_in"), m.sem("exp_ready")
        coef_ready, self_ready = m.sem("f_coef_ready"), m.sem("self_ready")
        chain_sem = m.sem("f_chain")

        block = ctx.enter_context(nc.Block())

        @block.sync
        def _(sp):
            hp_v = dram["tab1"].rearrange("(t p) c -> p t c", p=TN)
            out_v = out.rearrange("(t p) c -> p t c", p=TN)
            for i in range(steps):
                tiles = slice(i * FB, (i + 1) * FB)
                sp.dma_start(hp[:, tiles, :], hp_v[:, tiles, 0:D]).then_inc(loaded[i], 16)
            with sp.Fori(0, steps) as i:
                sp.wait_ge(out_ready, 1)
                sp.sem_inc(out_ready, -1)
                tiles = bass.ds(i * FB, FB)
                sp.dma_start(out_v[:, tiles, :], acc[0:TN, tiles, 0:D]).then_inc(out_stored, 16)
            sp.wait_ge(out_stored, 16 * steps)

        @block.scalar
        def _(act):
            act.wait_ge(exp_in, 1)
            act.sem_inc(exp_in, -1)
            act.activation(p[:], e[:], ACT.Exp).then_inc(exp_ready, 1)
            act.wait_ge(exp_in, 1)
            act.sem_inc(exp_in, -1)
            act.activation(g[:], c[:], ACT.Exp).then_inc(exp_ready, 1)

        @block.tensor
        def _(pe):
            pe.wait_ge(mx_ready, 1)
            pe.sem_inc(mx_ready, -1)
            pe.transpose(turn_ps[:], mx[:, 0:1], ident[:]).then_inc(turned, 1)
            pe.wait_ge(mrow_ready, 1)
            pe.sem_inc(mrow_ready, -1)
            pe.matmul(top_ps[:], ones[:], mrow[:], start=True, stop=True).then_inc(top_done, 1)

        @block.gpsimd
        def _(pool):
            pool.wait_ge(coef_ready, 1)
            for i in range(steps):
                pool.wait_ge(loaded[i], 16)
                pool.sem_inc(loaded[i], -16)
                tiles = slice(i * FB, (i + 1) * FB)
                h = hp[:, tiles, :].rearrange("p t (h f) -> p t h f", h=HEADS)
                pool.tensor_tensor(h, h, p[:, tiles, :].unsqueeze(3).broadcast_to([TN, FB, HEADS, HD]),
                                   ALU.mult).then_inc(self_ready, 1)

        @block.vector
        def _(dve):
            dve.memset(ones[:], 1.0).then_inc(chain_sem, 1)
            dve.wait_ge(chain_sem, 1)
            dve.sem_inc(chain_sem, -1)
            dve.tensor_tensor(e[:], st[0:TN, :, 0:HEADS], st[0:TN, :, HEADS:2 * HEADS], ALU.add).then_inc(chain_sem, 1)
            dve.wait_ge(chain_sem, 1)
            dve.sem_inc(chain_sem, -1)
            leaky(dve, e[:], e[:]).then_inc(chain_sem, 1)
            dve.wait_ge(chain_sem, 1)
            dve.sem_inc(chain_sem, -1)
            dve.tensor_tensor(c[:], st[0:TN, :, HEADS:2 * HEADS], smax[0:TN, :].unsqueeze(1).broadcast_to([TN, NT, HEADS]), ALU.add).then_inc(chain_sem, 1)
            dve.wait_ge(chain_sem, 1)
            dve.sem_inc(chain_sem, -1)
            leaky(dve, c[:], c[:]).then_inc(chain_sem, 1)
            dve.wait_ge(chain_sem, 1)
            dve.sem_inc(chain_sem, -1)
            dve.tensor_reduce(mx[:, 0:1], maxima[:].rearrange("p k h -> p (k h)"), AX, ALU.max).then_inc(chain_sem, 1)
            dve.wait_ge(chain_sem, 1)
            dve.sem_inc(chain_sem, -1)
            dve.tensor_reduce(mx[0:TN, 1:2], e[:].rearrange("p t h -> p (t h)"), AX, ALU.max).then_inc(chain_sem, 1)
            dve.wait_ge(chain_sem, 1)
            dve.sem_inc(chain_sem, -1)
            dve.tensor_tensor(mx[0:TN, 0:1], mx[0:TN, 0:1], mx[0:TN, 1:2], ALU.max).then_inc(chain_sem, 1)
            dve.wait_ge(chain_sem, 1)
            dve.sem_inc(chain_sem, -1)
            dve.sem_inc(mx_ready, 1)
            dve.tensor_tensor(e[:], e[:], c[:], ALU.subtract).then_inc(chain_sem, 1)
            dve.wait_ge(chain_sem, 1)
            dve.sem_inc(chain_sem, -1)
            dve.sem_inc(exp_in, 1)
            dve.wait_ge(turned, 1)
            dve.sem_inc(turned, -1)
            dve.tensor_reduce(mrow[:], turn_ps[:], AX, ALU.max).then_inc(mrow_ready, 1)
            dve.wait_ge(top_done, 1)
            dve.sem_inc(top_done, -1)
            dve.tensor_copy(top[:], top_ps[:]).then_inc(chain_sem, 1)
            dve.wait_ge(chain_sem, 1)
            dve.sem_inc(chain_sem, -1)
            dve.tensor_scalar(c[:], c[:], top[0:TN, :], -1.0, ALU.subtract, ALU.mult).then_inc(chain_sem, 1)
            dve.wait_ge(chain_sem, 1)
            dve.sem_inc(chain_sem, -1)
            dve.tensor_scalar(c[:], c[:], CAP, None, ALU.min).then_inc(chain_sem, 1)
            dve.wait_ge(chain_sem, 1)
            dve.sem_inc(chain_sem, -1)
            dve.sem_inc(exp_in, 1)
            dve.wait_ge(exp_ready, 2)
            dve.sem_inc(exp_ready, -2)
            dve.scalar_tensor_tensor(out=g[:], in0=g[:], scalar=GUARD, in1=p[:], op0=ALU.mult, op1=ALU.add).then_inc(chain_sem, 1)
            dve.wait_ge(chain_sem, 1)
            dve.sem_inc(chain_sem, -1)
            dve.tensor_tensor(g[:], g[:], acc[0:TN, :, D:TW], ALU.add).then_inc(chain_sem, 1)
            dve.wait_ge(chain_sem, 1)
            dve.sem_inc(chain_sem, -1)
            dve.reciprocal(g[:], g[:]).then_inc(chain_sem, 1)
            dve.wait_ge(chain_sem, 1)
            dve.sem_inc(chain_sem, -1)
            dve.tensor_tensor(p[:], p[:], g[:], ALU.mult).then_inc(chain_sem, 1)
            dve.wait_ge(chain_sem, 1)
            dve.sem_inc(chain_sem, -1)
            dve.sem_inc(coef_ready, 1)
            fits = 2 * D - TW
            with dve.Fori(0, steps) as i:
                tiles = bass.ds(i * FB, FB)
                a = acc[0:TN, tiles, 0:D]
                a4 = a.rearrange("p t (h f) -> p t h f", h=HEADS)
                dve.tensor_tensor(a4, a4, g[:, tiles, :].unsqueeze(3).broadcast_to([TN, FB, HEADS, HD]), ALU.mult).then_inc(chain_sem, 1)
                dve.wait_ge(chain_sem, 1)
                dve.sem_inc(chain_sem, -1)
                dve.tensor_tensor(a[:, :, 0:fits], a[:, :, 0:fits], acc[0:TN, tiles, TW:2 * D], ALU.add)
                dve.tensor_tensor(a[:, :, fits:D], a[:, :, fits:D], x1_tail[:, tiles, :], ALU.add).then_inc(chain_sem, 1)
                dve.wait_ge(chain_sem, 1)
                dve.sem_inc(chain_sem, -1)
                dve.wait_ge(self_ready, 1)
                dve.sem_inc(self_ready, -1)
                dve.tensor_tensor(a, a, hp[:, tiles, :], ALU.add).then_inc(out_ready, 1)


_PLAIN = ["x", "L0_gnn_eps", "L0_gnn_ee_w1", "L0_gnn_ee_b1", "L0_gnn_ee_w2", "L0_gnn_ee_b2", "L0_gnn_w1",
          "L0_gnn_w2", "L0_gnn_w3", "L0_gnn_b3", "L0_gnn_bn_g", "L0_gnn_bn_b", "L1_gnn_W", "L1_gnn_b"]
_COLS = ["L0_gnn_b1", "L0_gnn_g1", "L0_gnn_be1", "L0_gnn_b2", "L0_gnn_g2", "L0_gnn_be2"]


def kernel(**inputs):
    import concourse.bacc as bacc
    import numpy as np
    from concourse.bass_utils import run_bass_kernel_spmd

    a = {n: np.ascontiguousarray(inputs[n]) for n in _PLAIN}
    for n in ("L1_gnn_a_src", "L1_gnn_a_trg"):
        a[n + "_cols"] = np.ascontiguousarray(np.asarray(inputs[n]).reshape(KD, P).T)
    a["L0_gnn_eps"] = a["L0_gnn_eps"].reshape(1)
    for n in _COLS:
        a[n + "_cols"] = np.ascontiguousarray(np.asarray(inputs[n]).reshape(KH, P).T)
    a["L0_gnn_ee_b1_cols"] = np.ascontiguousarray(np.asarray(inputs["L0_gnn_ee_b1"]).reshape(KD, P).T)
    a["L1_gnn_b_cols"] = np.ascontiguousarray(np.asarray(inputs["L1_gnn_b"]).reshape(KD, P).T)
    a["L1_gnn_W_t"] = np.ascontiguousarray(np.asarray(inputs["L1_gnn_W"]).T)
    pad = NBP * BE - E
    src = np.concatenate([np.asarray(inputs["src"]), np.zeros(pad, np.int32)])
    dst = np.concatenate([np.asarray(inputs["dst"]), np.full(pad, N, np.int32)])
    a["src_cols"] = np.ascontiguousarray(src.reshape(NCH, P).T)
    a["dst_cols"] = np.ascontiguousarray(np.concatenate([np.full(BE, N, np.int32), dst]).reshape(NCH + CB, P).T)
    a["dst_flat"] = dst
    ea = np.concatenate([np.asarray(inputs["edge_attr_64"]), np.zeros((pad, ED), np.float32)])
    a["edge_t"] = np.ascontiguousarray(ea.reshape(NBP, BE, ED).transpose(0, 2, 1))

    nc = bacc.Bacc("TRN2", target_bir_lowering=False, num_devices=1)
    t = {n: nc.dram_tensor(n, v.shape, mybir.dt.from_np(v.dtype), kind="ExternalInput").ap() for n, v in a.items()}
    out = nc.dram_tensor("out", (N, D), F32, kind="ExternalOutput").ap()
    build(nc, t, out)
    r = run_bass_kernel_spmd(nc, [a], core_ids=[0])
    return r.results[0]["out"]
```
